# Optimizing a Trainium2 kernel written in Bass

```python
import numpy as np
import jax
import jax.numpy as jnp

def _softmax(x, axis=-1):
    return jax.nn.softmax(x, axis=axis)

def _gelu(x):
    return jax.nn.gelu(x, approximate=True)

def _silu(x):
    return jax.nn.silu(x)

def _sigmoid(x):
    return jax.nn.sigmoid(x)

def _layernorm(x, axis=-1, eps=1e-05):
    m = jnp.mean(x, axis=axis, keepdims=True)
    v = jnp.var(x, axis=axis, keepdims=True)
    return (x - m) / jnp.sqrt(v + eps)

def _scatter_add(tgt, idx, src, axis=0):
    return tgt.at[idx].add(src)

def _segment_sum(src, seg, n):
    return jax.ops.segment_sum(src, seg, n)
kernel_name = 'mk_conv_attn_hybrid_d2_conv_nchw512_r2_a7524b'

def setup_inputs(seed: int=0):
    np.random.seed(seed)
    _w = jnp.asarray

    def _rec_inputs():
        import jax
        import jax.numpy as jnp
        _gk = jax.random.key(seed)
        x = -0.0002928 + 1 * jax.random.normal(jax.random.fold_in(_gk, 1), (2, 256, 32, 32), jnp.float32)
        return x
    x = _rec_inputs()

    def _L0_conv_setup():
        import jax, jax.numpy as jnp
        import numpy as np
        NUM_GROUPS = 32
        EPS = 1e-06

        def _group_norm(x, w, b):
            B, C, H, W = x.shape
            g = x.reshape(B, NUM_GROUPS, C // NUM_GROUPS, H, W)
            mu = jnp.mean(g, axis=(2, 3, 4), keepdims=True)
            var = jnp.mean(jnp.square(g - mu), axis=(2, 3, 4), keepdims=True)
            g = (g - mu) * jax.lax.rsqrt(var + EPS)
            x = g.reshape(B, C, H, W)
            return x * w[None, :, None, None] + b[None, :, None, None]

        def _conv1x1(x, w, b):
            return jnp.einsum('bchw,oc->bohw', x, w) + b[None, :, None, None]
        key = jax.random.key(seed)
        ks = jax.random.split(key, 8)
        B, C, H, W = (2, 256, 32, 32)
        s = 1.0 / np.sqrt(C)
        return {'x': jax.random.normal(ks[0], (B, C, H, W), dtype=jnp.float32), 'norm_w': jnp.ones((C,), jnp.float32), 'norm_b': jnp.zeros((C,), jnp.float32), 'wq': jax.random.normal(ks[1], (C, C), dtype=jnp.float32) * s, 'bq': jnp.zeros((C,), jnp.float32), 'wk': jax.random.normal(ks[2], (C, C), dtype=jnp.float32) * s, 'bk': jnp.zeros((C,), jnp.float32), 'wv': jax.random.normal(ks[3], (C, C), dtype=jnp.float32) * s, 'bv': jnp.zeros((C,), jnp.float32), 'wp': jax.random.normal(ks[4], (C, C), dtype=jnp.float32) * s, 'bp': jnp.zeros((C,), jnp.float32)}
    _L0_conv_all = _L0_conv_setup()
    _L0_conv_in = {k: v for k, v in _L0_conv_all.items() if k in ('norm_w', 'norm_b', 'wq', 'bq', 'wk', 'bk', 'wv', 'bv', 'wp', 'bp')}
    del _L0_conv_all

    def _L1_attn_setup():
        import math
        import jax, jax.numpy as jnp
        import numpy as np
        NUM_HEADS = 8
        FACTOR = 2
        key = jax.random.key(seed)
        ks = jax.random.split(key, 9)
        B, L, DM = (4, 2048, 256)
        s = 1.0 / math.sqrt(DM)
        return {'x': jax.random.normal(ks[0], (B, L, DM), jnp.float32), 'Wq': jax.random.normal(ks[1], (DM, DM), jnp.float32) * s, 'bq': jax.random.normal(ks[2], (DM,), jnp.float32) * s, 'Wk': jax.random.normal(ks[3], (DM, DM), jnp.float32) * s, 'bk': jax.random.normal(ks[4], (DM,), jnp.float32) * s, 'Wv': jax.random.normal(ks[5], (DM, DM), jnp.float32) * s, 'bv': jax.random.normal(ks[6], (DM,), jnp.float32) * s, 'Wo': jax.random.normal(ks[7], (DM, DM), jnp.float32) * s, 'bo': jax.random.normal(ks[8], (DM,), jnp.float32) * s}
    _L1_attn_all = _L1_attn_setup()
    _L1_attn_in = {k: v for k, v in _L1_attn_all.items() if k in ('Wq', 'bq', 'Wk', 'bk', 'Wv', 'bv', 'Wo', 'bo')}
    del _L1_attn_all

    def _L1_ffn_setup():
        import jax, jax.numpy as jnp
        import numpy as np
        NUM_EXPERTS = 8
        TOP_K = 2
        key = jax.random.key(seed)
        ks = jax.random.split(key, 5)
        B, N, E, H, X = (8, 1024, 256, 384, NUM_EXPERTS)
        s_in = 0.02
        return {'x': jax.random.normal(ks[0], (B, N, E), dtype=jnp.float32), 'Wg': jax.random.normal(ks[1], (E, X), dtype=jnp.float32) * s_in, 'bg': jnp.zeros((X,), dtype=jnp.float32), 'W1': jax.random.normal(ks[2], (X, E, H), dtype=jnp.float32) * (1.0 / np.sqrt(E)), 'b1': jnp.zeros((X, H), dtype=jnp.float32), 'W2': jax.random.normal(ks[3], (X, H, E), dtype=jnp.float32) * (1.0 / np.sqrt(H)), 'b2': jnp.zeros((X, E), dtype=jnp.float32)}
    _L1_ffn_all = _L1_ffn_setup()
    _L1_ffn_in = {k: v for k, v in _L1_ffn_all.items() if k in ('Wg', 'bg', 'W1', 'b1', 'W2', 'b2')}
    del _L1_ffn_all
    return {'x': x, 'L0_conv_norm_w': _L0_conv_in['norm_w'], 'L0_conv_norm_b': _L0_conv_in['norm_b'], 'L0_conv_wq': _L0_conv_in['wq'], 'L0_conv_bq': _L0_conv_in['bq'], 'L0_conv_wk': _L0_conv_in['wk'], 'L0_conv_bk': _L0_conv_in['bk'], 'L0_conv_wv': _L0_conv_in['wv'], 'L0_conv_bv': _L0_conv_in['bv'], 'L0_conv_wp': _L0_conv_in['wp'], 'L0_conv_bp': _L0_conv_in['bp'], 'L1_attn_Wq': _L1_attn_in['Wq'], 'L1_attn_bq': _L1_attn_in['bq'], 'L1_attn_Wk': _L1_attn_in['Wk'], 'L1_attn_bk': _L1_attn_in['bk'], 'L1_attn_Wv': _L1_attn_in['Wv'], 'L1_attn_bv': _L1_attn_in['bv'], 'L1_attn_Wo': _L1_attn_in['Wo'], 'L1_attn_bo': _L1_attn_in['bo'], 'L1_ffn_Wg': _L1_ffn_in['Wg'], 'L1_ffn_bg': _L1_ffn_in['bg'], 'L1_ffn_W1': _L1_ffn_in['W1'], 'L1_ffn_b1': _L1_ffn_in['b1'], 'L1_ffn_W2': _L1_ffn_in['W2'], 'L1_ffn_b2': _L1_ffn_in['b2']}

def reference(x, L0_conv_norm_w, L0_conv_norm_b, L0_conv_wq, L0_conv_bq, L0_conv_wk, L0_conv_bk, L0_conv_wv, L0_conv_bv, L0_conv_wp, L0_conv_bp, L1_attn_Wq, L1_attn_bq, L1_attn_Wk, L1_attn_bk, L1_attn_Wv, L1_attn_bv, L1_attn_Wo, L1_attn_bo, L1_ffn_Wg, L1_ffn_bg, L1_ffn_W1, L1_ffn_b1, L1_ffn_W2, L1_ffn_b2):
    import jax
    import jax.numpy as jnp

    def _L0_conv_ref(x, norm_w, norm_b, wq, bq, wk, bk, wv, bv, wp, bp):
        import jax, jax.numpy as jnp
        import numpy as np
        NUM_GROUPS = 32
        EPS = 1e-06

        def _group_norm(x, w, b):
            B, C, H, W = x.shape
            g = x.reshape(B, NUM_GROUPS, C // NUM_GROUPS, H, W)
            mu = jnp.mean(g, axis=(2, 3, 4), keepdims=True)
            var = jnp.mean(jnp.square(g - mu), axis=(2, 3, 4), keepdims=True)
            g = (g - mu) * jax.lax.rsqrt(var + EPS)
            x = g.reshape(B, C, H, W)
            return x * w[None, :, None, None] + b[None, :, None, None]

        def _conv1x1(x, w, b):
            return jnp.einsum('bchw,oc->bohw', x, w) + b[None, :, None, None]
        B, C, H, W = x.shape
        h_ = _group_norm(x, norm_w, norm_b)
        q = _conv1x1(h_, wq, bq)
        k = _conv1x1(h_, wk, bk)
        v = _conv1x1(h_, wv, bv)
        N = H * W
        q = q.reshape(B, C, N).transpose(0, 2, 1)
        k = k.reshape(B, C, N)
        v = v.reshape(B, C, N)
        scale = jnp.asarray(int(C) ** (-0.5), x.dtype)
        w_ = jnp.einsum('bic,bcj->bij', q, k) * scale
        w_ = jax.nn.softmax(w_, axis=-1)
        h_ = jnp.einsum('bci,bij->bcj', v, w_)
        h_ = h_.reshape(B, C, H, W)
        h_ = _conv1x1(h_, wp, bp)
        return x + h_

    def _L1_attn_ref(x, Wq, bq, Wk, bk, Wv, bv, Wo, bo):
        import math
        import jax, jax.numpy as jnp
        import numpy as np
        NUM_HEADS = 8
        FACTOR = 2
        B, L, DM = x.shape
        H = NUM_HEADS
        Dk = DM // H

        def proj(W, b):
            return (x @ W.T + b).reshape(B, L, H, Dk).transpose(0, 2, 1, 3)
        Q = proj(Wq, bq)
        K = proj(Wk, bk)
        V = proj(Wv, bv)
        qf = jnp.fft.rfft(Q.astype(jnp.float32), axis=2)
        kf = jnp.fft.rfft(K.astype(jnp.float32), axis=2)
        corr = jnp.fft.irfft(qf * jnp.conj(kf), n=L, axis=2)
        corr_mean = corr.mean(axis=-1)
        k = min(int(FACTOR * math.log(L)), L)
        w, delays = jax.lax.top_k(corr_mean, k)
        w = jax.nn.softmax(w, axis=-1)
        t = jnp.arange(L)
        idx = (t[None, None, :, None] - delays[:, :, None, :]) % L
        gathered = jnp.take_along_axis(V[:, :, :, None, :], idx[:, :, :, :, None], axis=2)
        ctx = jnp.einsum('bhlkd,bhk->bhld', gathered, w.astype(gathered.dtype))
        ctx = ctx.transpose(0, 2, 1, 3).reshape(B, L, DM)
        return ctx @ Wo.T + bo

    def _L1_ffn_ref(x, Wg, bg, W1, b1, W2, b2):
        import jax, jax.numpy as jnp
        import numpy as np
        NUM_EXPERTS = 8
        TOP_K = 2
        scores = jnp.einsum('bne,ex->bnx', x, Wg) + bg
        topk_vals, topk_idx = jax.lax.top_k(scores, TOP_K)
        gates = jax.nn.softmax(topk_vals, axis=-1)
        h = jnp.einsum('bne,xeh->bnxh', x, W1) + b1
        h = jax.nn.gelu(h, approximate=False)
        expert_out = jnp.einsum('bnxh,xhe->bnxe', h, W2) + b2
        onehot = jax.nn.one_hot(topk_idx, NUM_EXPERTS, dtype=x.dtype)
        combine = jnp.einsum('bnk,bnkx->bnx', gates, onehot)
        out = jnp.einsum('bnx,bnxe->bne', combine, expert_out)
        return out

    def _gn(v, G=32, eps=1e-05):
        B_, C_, H_, W_ = v.shape
        g = v.reshape(B_, G, C_ // G, H_, W_)
        m = jnp.mean(g, axis=(2, 3, 4), keepdims=True)
        s = jnp.var(g, axis=(2, 3, 4), keepdims=True)
        return ((g - m) / jnp.sqrt(s + eps)).reshape(v.shape)

    def _ln_c(v, eps=1e-06):
        m = jnp.mean(v, axis=1, keepdims=True)
        s = jnp.var(v, axis=1, keepdims=True)
        return (v - m) / jnp.sqrt(s + eps)

    def _ln_t(v, eps=1e-05):
        m = jnp.mean(v, axis=-1, keepdims=True)
        s = jnp.var(v, axis=-1, keepdims=True)
        return (v - m) / jnp.sqrt(s + eps)

    def _to_tokens(v):
        B_, C_, H_, W_ = v.shape
        return v.reshape(B_, C_, H_ * W_).transpose(0, 2, 1)

    def _from_tokens(t, like):
        B_, C_, H_, W_ = like.shape
        return t.transpose(0, 2, 1).reshape(B_, C_, H_, W_)
    x = _L0_conv_ref(x, L0_conv_norm_w, L0_conv_norm_b, L0_conv_wq, L0_conv_bq, L0_conv_wk, L0_conv_bk, L0_conv_wv, L0_conv_bv, L0_conv_wp, L0_conv_bp)
    t = _to_tokens(x)
    t = t + _L1_attn_ref(_ln_t(t), L1_attn_Wq, L1_attn_bq, L1_attn_Wk, L1_attn_bk, L1_attn_Wv, L1_attn_bv, L1_attn_Wo, L1_attn_bo)
    t = t + _L1_ffn_ref(_ln_t(t), L1_ffn_Wg, L1_ffn_bg, L1_ffn_W1, L1_ffn_b1, L1_ffn_W2, L1_ffn_b2)
    x = _from_tokens(t, x)
    return x

_drawn_inputs = setup_inputs


def setup_inputs(seed=0):
    import zlib

    import numpy as np

    out = dict(_drawn_inputs(seed))
    spreads = {'L0_conv_norm_w': (1.0, 0.2),
     'L0_conv_norm_b': (0.0, 0.1),
     'L0_conv_bq': (0.0, 0.1),
     'L0_conv_bk': (0.0, 0.1),
     'L0_conv_bv': (0.0, 0.1),
     'L0_conv_bp': (0.0, 0.1),
     'L1_ffn_bg': (0.0, 0.1),
     'L1_ffn_b1': (0.0, 0.1),
     'L1_ffn_b2': (0.0, 0.1)}
    factors = {}
    for name, (base, spread) in spreads.items():
        noise = np.random.default_rng([zlib.crc32(name.encode()), seed]).standard_normal(out[name].shape)
        drawn = base * np.exp(spread * noise) if base else spread * noise
        out[name] = jnp.asarray(drawn.astype(out[name].dtype))
    for name, factor in factors.items():
        out[name] = (out[name] * factor).astype(out[name].dtype)
    return out
```

```python
from contextlib import ExitStack

import numpy as np

import concourse.bass as bass
from concourse import mybir

ALU = mybir.AluOpType
ACT = mybir.ActivationFunctionType
AX_X = mybir.AxisListType.X
F32 = mybir.dt.float32
F16 = mybir.dt.float16
U32 = mybir.dt.uint32

P = 128
B = 2
C = 256
CC = C // P
N = 1024
NT = N // P
HALF = N // 2
QUARTER = N // 4
HEADS = 8
DK = C // HEADS
TOPK = int(2 * np.log(N))
GROUP = C // 32
E = 8
H = 384
HC = H // P
T = B * N
TT = T // P
EPS_CONV = 1e-6
EPS_TOK = 1e-5
ATT_SCALE = 1.0 / 16
SPEC_SCALE = 1.0 / 32
ODD, EVEN = 4 * HALF, 2 * QUARTER
TAB = ODD + 2 * EVEN


def split16(a):
    hi = a.astype(np.float16)
    return hi, (a - hi.astype(np.float64)).astype(np.float16)


def dft_constants():
    k = np.arange(P)

    def rows(freq, length, last):
        t = np.arange(length)
        ang = 2 * np.pi * np.outer(freq, t) / N
        re, im = np.cos(ang), -np.sin(ang)
        weight = np.full(len(freq), 2.0)
        wim = weight.copy()
        if last:
            im[0] = np.cos(np.pi * t)
            weight[0] = wim[0] = 1.0
        return [re, im], [re * weight[:, None], im * wim[:, None]]

    o0, io0 = rows(1 + 2 * k, HALF, False)
    o1, io1 = rows(1 + 2 * (k + P), HALF, False)
    e, ie = rows(2 + 4 * k, QUARTER, False)
    z, iz = rows(4 * k, QUARTER, True)

    def forward(parts, length):
        m = np.concatenate(parts, 0).T
        return m.reshape(length // P, P, -1).transpose(1, 0, 2).reshape(P, -1)

    def inverse(parts):
        return np.stack(parts, 1).reshape(P, -1)

    fwd = np.concatenate([forward(o0 + o1, HALF), forward(e, QUARTER), forward(z, QUARTER)], 1)
    inv = np.concatenate([inverse(io0 + io1), inverse(ie), inverse(iz)], 1)
    pair_mask = np.ones((P, 4 * HEADS), np.float32)
    pair_mask[0, 3 * HEADS:] = 0.0
    p = np.arange(P)
    consts = np.concatenate([
        np.eye(P), (p[:, None] // GROUP == p[None, :] // GROUP) / float(GROUP),
        pair_mask, np.tile(np.arange(E), (P, 1)),
    ], 1).astype(np.float32)
    return {
        "const_f32": consts, "inv_f32": inv.astype(np.float32),
        "fwd_hi": split16(fwd)[0], "fwd_lo": split16(fwd)[1],
        "inv_hi": split16(inv)[0], "inv_lo": split16(inv)[1],
    }


def conv_attn_moe_kernel(nc, g, out, debug=None):
    with ExitStack() as ctx:
        def sb(name, shape, dt=F32):
            return ctx.enter_context(nc.sbuf_tensor(name, shape, dt))

        def sem(name):
            return ctx.enter_context(nc.semaphore(name))

        def view(region, at_kb, dims, dt):
            size = int(np.prod(dims)) * (2 if dt == F32 else 1)
            flat = region[:, at_kb * 512:at_kb * 512 + size]
            if dt == F32:
                flat = flat.bitcast(F32)
            names = "abc"[:len(dims)]
            return flat.rearrange(f"p ({' '.join(names)}) -> p {' '.join(names)}", **dict(zip(names[1:], dims[1:]))) \
                if len(dims) > 1 else flat

        psS = ctx.enter_context(nc.psum_tensor("psS", [P, 2, N], F32))
        psD = ctx.enter_context(nc.psum_tensor("psD", [P, 2, 512], F32))
        psA = ctx.enter_context(nc.psum_tensor("psA", [P, 2, 512], F32))

        const = sb("const", [P, 2 * P + 4 * HEADS + E])
        ident, blockdiag = const[:, 0:P], const[:, P:2 * P]
        pair_mask = const[:, 2 * P:2 * P + 4 * HEADS]
        iota8 = const[:, 2 * P + 4 * HEADS:]
        fwd = [sb("fwd_hi_sb", [P, TAB], F16), sb("fwd_lo_sb", [P, TAB], F16)]
        ones = sb("ones", [1, P])
        dc_row = sb("dc_row", [1, P])
        half_neg = sb("half_neg", [P, NT])

        def odd(tab, k):
            return tab[:, 512 * k:512 * (k + 1)]

        def even(tab, which, k):
            o = ODD + which * EVEN + QUARTER * k
            return tab[:, o:o + QUARTER]

        raw_region = sb("raw_region", [P, 8 * 1024], F16)
        wraw = view(raw_region, 0, [8, CC * C], F32)
        inv32 = view(raw_region, 0, [TAB], F32)

        def raw(which, chunk):
            return wraw[:, which, chunk * C:(chunk + 1) * C]

        WQ, WK, WV, WP = range(4)
        wpT = sb("wpT", [P, CC, C])
        A = [sb(f"A_{i}", [P, CC, C], F16) for i in "hl"]
        UW = [sb(f"UW_{i}", [P, CC, C + 1], F16) for i in "hl"]
        gq = sb("gq", [P, CC])
        ub = sb("ub", [1, C + 1])
        qkvW = [sb(f"qkvW_{i}", [P, CC, 3 * C], F16) for i in "hl"]
        woW = [sb(f"woW_{i}", [P, CC, C], F16) for i in "hl"]
        cols = sb("cols", [P, 5, CC])
        NW, NB, BQ, BK, BV = range(5)
        bp_all = sb("bp_all", [P, C])
        bo_all = sb("bo_all", [P, C])
        qkv_row = sb("qkv_row", [1, 3 * C])
        bg_all = sb("bg_all", [P, E])

        x_region = sb("x_region", [P, 8 * 1024], F16)
        x_sb = view(x_region, 0, [B * CC, N], F32)
        bn = sb("bn", [P, B * CC, 2, 6])
        mv = sb("mv", [P, B * CC, 2])
        gn = sb("gn", [P, 8, B * CC])
        h = [sb(f"h_{i}", [P, B * CC * N], F16) for i in "hl"]
        inv = [h[0], h[1]]
        z_region = sb("z_region", [P, 4 * 1024], F16)
        z = [view(z_region, 4 * i, [CC, N], F16) for i in range(2)]
        uT_region = sb("uT_region", [P, 2 * NT * (C + 1)], F16)
        uT = view(uT_region, 0, [NT, C + 1], F32)
        u_region = [sb(f"u_region{b}", [P, 4 * 1024], F16) for b in range(B)]
        u = [[view(u_region[b], 4 * i, [NT, C], F16) for i in range(2)] for b in range(B)]
        prob_region = sb("prob_region", [P, 4 * 1024], F16)
        prob = view(prob_region, 0, [2, N], F32)
        sm = sb("sm", [P, 5, B * NT])
        arena = [sb(f"arena{b}", [P, 16 * 1024], F16) for b in range(B)]
        Pm = [[view(arena[b], 16 * i, [NT, N], F16) for i in range(2)] for b in range(B)]

        t1 = sb("t1", [P, B, NT, C])
        tst = sb("tst", [P, NT, 6])
        tmv = sb("tmv", [P, NT, 2])
        trs = sb("trs", [P, 2, NT])
        xhat = [[view(arena[b], 4 * i, [CC, N], F16) for i in range(2)] for b in range(B)]
        xf32 = [view(arena[b], 8, [NT, C], F32) for b in range(B)]
        xf = [[view(arena[b], 16 + 4 * i, [NT, C], F16) for i in range(2)] for b in range(B)]
        xn = [view(arena[b], 24, [NT, C], F32) for b in range(B)]
        fold = view(z_region, 0, [4, C], F32)
        qkv = [view(arena[b], 8, [NT, 3 * C], F32) for b in range(B)]
        prod = [view(z_region, 4 * i, [4, C], F32) for i in range(2)]
        cs = sb("cs", [P, 8, 4 * HEADS])
        spec = sb("spec", [P, 2, 4 * HEADS])
        ctx4 = [view(prob_region, 0, [N], F32), view(prob_region, 4, [N], F32),
                view(uT_region, 0, [N], F32), view(uT_region, 4, [N], F32)]
        corr, left, weight, wfold = ctx4
        even32 = [view(arena[b], 0, [4, QUARTER], F32) for b in range(B)]
        e_zero = [view(arena[b], 28, [QUARTER], F32) for b in range(B)]
        top = sb("top", [HEADS, 24])
        wT = [sb(f"wT_{i}", [P, NT * HEADS], F16) for i in "hl"]
        wh = sb("wh", [P, 5, 4 * HEADS])
        wh_raw = sb("wh_raw", [P, NT * HEADS])
        Y32 = [view(arena[b], 0, [NT, C], F32) for b in range(B)]
        Y = [[view(u_region[b], 4 * i, [NT, C], F16) for i in range(2)] for b in range(B)]
        cx = [[view(arena[b], 8 + 4 * i, [CC, N], F16) for i in range(2)] for b in range(B)]
        cx32 = [view(arena[b], 16, [CC, N], F32) for b in range(B)]
        ehalf = [view(arena[b], 24, [CC, HALF], F32) for b in range(B)]
        yn = [view(arena[b], 24, [NT, C], F32) for b in range(B)]

        D, D_ACT, DF, A_AT, AF = {}, {}, 0, {}, 0

        def fills(name, n, act):
            nonlocal DF
            D[name] = (DF, DF + n)
            for k in range(n):
                D_ACT[DF + k] = act
            DF += n

        def afills(name, n):
            nonlocal AF
            A_AT[name] = (AF, AF + n)
            AF += n

        for name, n, act in [("wpT", 1, 0), ("A", 1, 1), ("UW", 1, 1), ("small", 1, 0), ("gn", 2, 0),
                             ("G0", 4, 1), ("attnW", 4, 1), ("G1", 4, 1), ("PV0", 8, 0), ("PV1", 8, 0),
                             ("D0", 4, 1), ("D1", 4, 1),
                             ("C0", 2, 0), ("T0", 1, 1), ("W0", 1, 0), ("I0", 4, 0), ("O0", 8, 0),
                             ("C1", 2, 0), ("T1", 1, 1), ("W1", 1, 0), ("I1", 4, 0), ("O1", 8, 0),
                             ("YT", 8, 0), ("gate", 1, 0), ("combT", 4, 0), ("bias2", 8, 0),
                             ("ffn", E * 4 * 4, 0), ("outT", 8, 0)]:
            fills(name, n, act)
        for name, n in [("U0", 8), ("U1", 8), ("Q0", 16), ("Q1", 16), ("hid", E * 4 * HC)]:
            afills(name, n)

        def hi_count(n):
            return sum(D_ACT[k] for k in range(n + 1))

        d_full, d_taken, d_high = sem("d_full"), sem("d_taken"), sem("d_high")
        a_full, a_taken = sem("a_full"), sem("a_taken")
        s_full, s_exp = sem("s_full"), sem("s_exp")
        x_in = [sem(f"x_in{q}") for q in range(B * CC)]
        w_in, aw_in, small_in, const_in, fwd_in = sem("w_in"), sem("aw_in"), sem("small_in"), sem("const_in"), sem("fwd_in")
        inv32_in, inv_in = sem("inv32_in"), sem("inv_in")
        rows_ready, mean_ready, spread_ready, affine_ready = sem("rows_ready"), sem("mean_ready"), sem("spread_ready"), sem("affine_ready")
        h32_ready, h_high, h_low = sem("h32_ready"), sem("h_high"), sem("h_low")
        bias_ready, p_high, p_low, u_ready = sem("bias_ready"), sem("p_high"), sem("p_low"), sem("u_ready")
        var_ready, rstd_ready, xf32_ready, xf_high, xf_ready = (sem(n) for n in ("var_ready", "rstd_ready", "xf32_ready", "xf_high", "xf_ready"))
        spec_ready, peak_ready, exp_ready, wfold_ready = (sem(n) for n in ("spec_ready", "peak_ready", "exp_ready", "wfold_ready"))
        y_ready, y_high, y_low = sem("y_ready"), sem("y_high"), sem("y_low")
        cx32_ready, cx_high, cx_low = sem("cx32_ready"), sem("cx_high"), sem("cx_low")
        yn_ready, t_bo = sem("yn_ready"), sem("t_bo")
        v_step = sem("v_step")
        root_ready = sem("root_ready")
        out_sem = sem("out_sem")
        consts_made = sem("consts_made")
        ACTV = nc.scalar.activation
        V, PL, PE = nc.vector, nc.gpsimd, nc.tensor


        w1_in = [sem(f"w1_in{s}") for s in range(2)]
        w2_in = [sem(f"w2_in{s}") for s in range(2)]
        gate_ready, gexp_ready, comb_ready, gelu_done = sem("gate_ready"), sem("gexp_ready"), sem("comb_ready"), sem("gelu_done")
        ffn_small = sem("ffn_small")
        ynT = view(x_region, 0, [CC, T], F32)
        w1 = [view(raw_region, 6 * s, [CC, H], F32) for s in range(2)]
        w2 = [view(raw_region, 6 * s + 3, [HC, C], F32) for s in range(2)]
        hT = [view(arena[0], 6 * s, [HC, 512], F32) for s in range(2)]
        outT = view(arena[1], 0, [B * CC, N], F32)
        combT = view(prob_region, 0, [T], F32)
        wg_sb = sb("wg_sb", [P, CC, E])
        b1_sb = sb("b1_sb", [P, E, HC])
        b2_sb = sb("b2_sb", [E, C])
        gs = view(u_region[0], 0, [4, TT * E], F32)
        gidx = sb("gidx", [P, TT, E], U32)
        comb = view(u_region[0], 2, [TT * E], F32)
        gt = view(u_region[0], 3, [8, TT], F32)
        tt = t1[:, :, :, :].rearrange("p b j c -> p (b j) c")

        block = ctx.enter_context(nc.Block())

        @block.sync
        def _(sp):
            sp.dma_start(const[:, :], g["const_f32"]).then_inc(const_in, 16)
            for q in range(B * CC):
                sp.dma_start(x_sb[:, q, :], g["x"][q // CC].rearrange("(k p) a b -> k p (a b)", p=P)[q % CC]).then_inc(x_in[q], 16)
            for n, name in enumerate(["wq", "wk", "wv", "wp"]):
                sp.dma_start(wraw[:, n, :].rearrange("p (k c) -> p k c", k=CC),
                             g[f"L0_conv_{name}"].rearrange("(k p) c -> p k c", p=P)).then_inc(w_in, 16)
            for n, name in enumerate(["Wq", "Wk", "Wv", "Wo"]):
                sp.dma_start(wraw[:, 4 + n, :].rearrange("p (k c) -> p k c", k=CC),
                             g[f"L1_attn_{name}"].rearrange("(k p) c -> p k c", p=P)).then_inc(aw_in, 16)
            for i, name in enumerate(["fwd_hi", "fwd_lo"]):
                sp.dma_start(fwd[i][:, :], g[name]).then_inc(fwd_in, 16)
            sp.wait_ge(d_taken, D["attnW"][1])
            sp.dma_start(inv32, g["inv_f32"]).then_inc(inv32_in, 16)
            sp.wait_ge(s_full, B * NT)
            for i, name in enumerate(["inv_hi", "inv_lo"]):
                sp.dma_start(inv[i][:, 0:TAB], g[name]).then_inc(inv_in, 16)

            sp.wait_ge(d_taken, D["C1"][1])
            for e in range(E):
                if e >= 2:
                    sp.wait_ge(d_full, D["ffn"][0] + 16 * (e - 1))
                sp.dma_start(w1[e % 2], g["L1_ffn_W1"][e].rearrange("(k p) h -> p k h", p=P)).then_inc(w1_in[e % 2], 16)
                sp.dma_start(w2[e % 2], g["L1_ffn_W2"][e].rearrange("(k p) h -> p k h", p=P)).then_inc(w2_in[e % 2], 16)
            for b in range(B):
                sp.wait_ge(d_taken, D["outT"][0] + 4 * (b + 1))
                sp.dma_start(out[b].rearrange("(k p) a b -> p k (a b)", p=P), outT[:, b * CC:(b + 1) * CC, :]).then_inc(out_sem, 16)
            sp.wait_ge(out_sem, 16 * B)

        SMALL = 5 + 2 + 3 + 1

        @block.gpsimd
        def _(pool):
            for n, name in enumerate(["L0_conv_norm_w", "L0_conv_norm_b", "L0_conv_bq", "L0_conv_bk", "L0_conv_bv"]):
                pool.dma_start(cols[:, n, :], g[name].rearrange("(k p) -> p k", p=P), allow_slow_non_contiguous=True).then_inc(small_in, 16)
            pool.dma_start(bp_all[:, :], g["L0_conv_bp"].partition_broadcast(P)).then_inc(small_in, 16)
            pool.dma_start(bo_all[:, :], g["L1_attn_bo"].partition_broadcast(P)).then_inc(small_in, 16)
            pool.dma_start(bg_all[:, :], g["L1_ffn_bg"].partition_broadcast(P)).then_inc(small_in, 16)
            for n, name in enumerate(["bq", "bk", "bv"]):
                pool.dma_start(qkv_row[:, n * C:(n + 1) * C], g[f"L1_attn_{name}"].rearrange("(a n) -> a n", a=1)).then_inc(small_in, 16)
            pool.dma_start(wg_sb[:, :, :], g["L1_ffn_Wg"].rearrange("(k p) e -> p k e", p=P)).then_inc(ffn_small, 16)
            pool.dma_start(b1_sb[:, :, :], g["L1_ffn_b1"].rearrange("e (k p) -> p e k", p=P), allow_slow_non_contiguous=True).then_inc(ffn_small, 16)
            pool.dma_start(b2_sb[:, :], g["L1_ffn_b2"]).then_inc(ffn_small, 16)
            PL.memset(half_neg[:, :], -0.5).then_inc(consts_made, 1)
            pool.wait_ge(consts_made, 1)
            pool.wait_ge(d_taken, D["gn"][1])
            PL.tensor_tensor(gn[:, 3, :], gn[:, 5, :], half_neg[:, 0:B * CC], ALU.pow).then_inc(root_ready, 1)
            for q in range(B * CC):
                pool.wait_ge(h_high, q + 1)
                PL.tensor_tensor(h[1][:, q * N:(q + 1) * N], prob[:, q % 2, :], h[0][:, q * N:(q + 1) * N],
                                 ALU.subtract).then_inc(h_low, 1)

            def low_probs(b):
                for i in range(NT):
                    n = b * NT + i
                    pool.wait_ge(p_high, n + 1)
                    PL.tensor_tensor(Pm[b][1][:, i, :], prob[:, n % 2, :], Pm[b][0][:, i, :], ALU.subtract).then_inc(p_low, 1)

            def rstd(n):
                pool.wait_ge(var_ready, n + 1)
                PL.tensor_tensor(trs[:, 1, :], trs[:, 0, :], half_neg[:, :], ALU.pow).then_inc(rstd_ready, 1)

            for b in range(B):
                low_probs(b)
            for b in range(B):
                rstd(b)
            for b in range(B):
                rstd(B + b)

        @block.scalar
        def _(act):
            high = [0]

            def take_high(fill, out_ap, in_cols, **kw):
                act.wait_ge(d_full, fill + 1)
                ACTV(out_ap, psD[:, fill % 2, in_cols] if isinstance(in_cols, slice) else in_cols, ACT.Identity, **kw).then_inc(d_high, 1)
                high[0] += 1
                assert high[0] == hi_count(fill)

            def weights():
                f = D["A"][0]
                take_high(f, A[0][:, :, :].rearrange("p k c -> p (k c)"), slice(0, 512), scale=ATT_SCALE)
                f = D["UW"][0]
                act.wait_ge(d_full, f + 1)
                ACTV(UW[0][:, :, 0:C], psD[:, f % 2, :].rearrange("p (k c) -> p k c", k=CC), ACT.Identity).then_inc(d_high, 1)
                high[0] += 1

            def attn_weights():
                for w in range(4):
                    f = D["attnW"][0] + w
                    dst = woW[0][:, :, :] if w == 3 else qkvW[0][:, :, w * C:(w + 1) * C]
                    act.wait_ge(d_full, f + 1)
                    ACTV(dst, psD[:, f % 2, :].rearrange("p (k c) -> p k c", k=CC), ACT.Identity).then_inc(d_high, 1)
                    high[0] += 1

            def normalise():
                act.wait_ge(affine_ready, B)
                for q in range(B * CC):
                    act.wait_ge(x_in[q], 16)
                    if q >= 2:
                        act.wait_ge(h_low, q - 1)
                    ACTV(prob[:, q % 2, :], x_sb[:, q, :], ACT.Identity, bias=gn[:, 7, q:q + 1],
                         scale=gn[:, 6, q:q + 1]).then_inc(h32_ready, 1)

            def zs(b):
                for k in range(4):
                    f = D[f"G{b}"][0] + k
                    m, half = k // 2, k % 2
                    take_high(f, z[0][:, m, half * 512:(half + 1) * 512], slice(0, 512), bias=gq[:, m:m + 1])

            def us(b):
                for i in range(NT):
                    f = A_AT[f"U{b}"][0] + i
                    act.wait_ge(a_full, f + 1)
                    if b == 1 and i == 0:
                        act.wait_ge(u_ready, NT)
                    ACTV(uT[:, i, :], psA[:, f % 2, 0:C + 1], ACT.Identity).then_inc(a_taken, 1)

            def exps(b):
                for i in range(NT):
                    n = b * NT + i
                    act.wait_ge(bias_ready, n + 1)
                    if n >= 2:
                        act.wait_ge(p_low, n - 1)
                    else:
                        act.wait_ge(h_low, B * CC)
                    ACTV(prob[:, n % 2, :], psS[:, n % 2, :], ACT.Exp, bias=sm[:, 2, n:n + 1],
                         accum_out=sm[:, 3, n:n + 1]).then_inc(s_exp, 1)

            def xf_hi(b):
                act.wait_ge(xf32_ready, b + 1)
                ACTV(xf[b][0].rearrange("p a c -> p (a c)"), xf32[b].rearrange("p a c -> p (a c)"), ACT.Identity).then_inc(xf_high, 1)

            def spectra(b):
                for k in range(4):
                    take_high(D[f"D{b}"][0] + k, xhat[b][0][:, k // 2, (k % 2) * 512:(k % 2 + 1) * 512], slice(0, 512))

            def take_qkv(b):
                for k in range(2 * NT):
                    f = A_AT[f"Q{b}"][0] + k
                    act.wait_ge(a_full, f + 1)
                    if k == 0:
                        act.wait_ge(d_taken, D[f"D{b}"][1])
                    w = 512 if k % 2 == 0 else 256
                    ACTV(qkv[b][:, k // 2, (k % 2) * 512:(k % 2) * 512 + w], psA[:, f % 2, 0:w], ACT.Identity).then_inc(a_taken, 1)

            def delays(b):
                act.wait_ge(peak_ready, b + 1)
                ACTV(weight[0:HEADS, :], corr[0:HEADS, :], ACT.Exp, bias=top[:, 16:17], scale=1.0 / (N * DK)).then_inc(exp_ready, 1)
                take_high(D[f"T{b}"][0], wT[0][:, :], slice(0, NT * HEADS))

            def y_hi(b):
                act.wait_ge(y_ready, b + 1)
                ACTV(Y[b][0].rearrange("p a c -> p (a c)"), Y32[b].rearrange("p a c -> p (a c)"), ACT.Identity).then_inc(y_high, 1)

            def cx_hi(b):
                for m in range(CC):
                    act.wait_ge(d_taken, D[f"I{b}"][0] + 2 * m + 2)
                    ACTV(cx[b][0][:, m, :], cx32[b][:, m, :], ACT.Identity).then_inc(cx_high, 1)

            weights()
            normalise()
            zs(0)
            us(0)
            exps(0)
            attn_weights()
            zs(1)
            us(1)
            exps(1)
            for b in range(B):
                xf_hi(b)
                spectra(b)
            for b in range(B):
                take_qkv(b)
            for b in range(B):
                delays(b)
                y_hi(b)
                cx_hi(b)

            act.wait_ge(gate_ready, 1)
            ACTV(gt[:, 1, :], gt[:, 0, :], ACT.Exp).then_inc(gexp_ready, 1)
            act.wait_ge(ffn_small, 48)
            for n in range(E * 4):
                if n >= 2:
                    act.wait_ge(d_full, D["ffn"][0] + 4 * (n - 1))
                for k in range(HC):
                    f = A_AT["hid"][0] + n * HC + k
                    act.wait_ge(a_full, f + 1)
                    ACTV(hT[n % 2][:, k, :], psA[:, f % 2, :], ACT.Gelu, bias=b1_sb[:, n // 4, k:k + 1]).then_inc(a_taken, 1)

        @block.vector
        def _(dve):
            steps = [0]

            def step(ins):
                steps[0] += 1
                ins.then_inc(v_step, 1)
                dve.wait_ge(v_step, steps[0])

            def full(f):
                dve.wait_ge(d_full, f + 1)

            def low(fill, dst, bank, hi, **kw):
                full(fill)
                dve.wait_ge(d_high, hi_count(fill))
                V.scalar_tensor_tensor(out=dst, in0=bank, scalar=kw.get("scalar", 1.0), in1=hi,
                                       op0=kw.get("op0", ALU.mult), op1=ALU.subtract).then_inc(d_taken, 1)

            V.memset(ones[:, :], 1.0).then_inc(rows_ready, 1)
            step(V.memset(dc_row[:, :], 0.0))
            V.memset(dc_row[:, 0:1], float(N)).then_inc(rows_ready, 1)

            for q in range(B * CC):
                dve.wait_ge(x_in[q], 16)
                for s in range(2):
                    last = V.bn_stats(bn[:, q, s, :], x_sb[:, q, s * 512:(s + 1) * 512])
                step(last)
                last = V.bn_aggr(mv[:, q, :], bn[:, q, :, :].rearrange("p a b -> p (a b)"))
            last.then_inc(mean_ready, 1)

            f = D["wpT"][0]
            full(f)
            V.tensor_copy(wpT[:, :, :].rearrange("p k c -> p (k c)"), psD[:, f % 2, :]).then_inc(d_taken, 1)
            f = D["A"][0]
            low(f, A[1][:, :, :].rearrange("p k c -> p (k c)"), psD[:, f % 2, :], A[0][:, :, :].rearrange("p k c -> p (k c)"), scalar=ATT_SCALE)
            f = D["UW"][0]
            low(f, UW[1][:, :, 0:C], psD[:, f % 2, :].rearrange("p (k c) -> p k c", k=CC), UW[0][:, :, 0:C])
            f = D["small"][0]
            full(f)
            step(V.tensor_scalar(gq[:, :], psD[:, f % 2, 0:2], ATT_SCALE, None, ALU.mult))
            step(V.tensor_scalar(gn[:, 0, 0:2], psD[:, f % 2, 2:4], ATT_SCALE, None, ALU.mult))
            step(V.tensor_copy(UW[0][:, :, C], gn[:, 0, 0:2]))
            step(V.tensor_tensor(UW[1][:, :, C], gn[:, 0, 0:2], UW[0][:, :, C], ALU.subtract))
            step(V.tensor_copy(ub[:, 0:C], psD[0:1, f % 2, 8:8 + C]))
            V.tensor_scalar(ub[:, C:C + 1], psD[0:1, f % 2, 4:5], ATT_SCALE, None, ALU.mult).then_inc(d_taken, 1)

            f = D["gn"][0]
            full(f)
            V.tensor_copy(gn[:, 1, :], psD[:, f % 2, 0:4]).then_inc(d_taken, 1)
            dve.wait_ge(d_taken, f + 1)
            step(V.tensor_tensor(gn[:, 2, :], mv[:, :, 0], gn[:, 1, :], ALU.subtract))
            step(V.tensor_tensor(gn[:, 3, :], gn[:, 2, :], gn[:, 2, :], ALU.mult))
            V.tensor_tensor(gn[:, 4, :], gn[:, 3, :], mv[:, :, 1], ALU.add).then_inc(spread_ready, 1)
            f += 1
            full(f)
            V.tensor_scalar(gn[:, 5, :], psD[:, f % 2, 0:4], EPS_CONV, None, ALU.add).then_inc(d_taken, 1)
            dve.wait_ge(root_ready, 1)
            for b in range(B):
                q = slice(b * CC, (b + 1) * CC)
                step(V.tensor_tensor(gn[:, 6, q], gn[:, 3, q], cols[:, NW, :], ALU.mult))
                step(V.tensor_tensor(gn[:, 2, q], gn[:, 1, q], gn[:, 6, q], ALU.mult))
                V.tensor_tensor(gn[:, 7, q], cols[:, NB, :], gn[:, 2, q], ALU.subtract).then_inc(affine_ready, 1)
            for q in range(B * CC):
                dve.wait_ge(h32_ready, q + 1)
                V.tensor_copy(h[0][:, q * N:(q + 1) * N], prob[:, q % 2, :]).then_inc(h_high, 1)

            def zs(b):
                for k in range(4):
                    f = D[f"G{b}"][0] + k
                    m, s = k // 2, slice((k % 2) * 512, (k % 2 + 1) * 512)
                    low(f, z[1][:, m, s], psD[:, f % 2, :], z[0][:, m, s], scalar=gq[:, m:m + 1], op0=ALU.add)

            def score_max(b, i):
                n = b * NT + i
                dve.wait_ge(a_taken, A_AT[f"U{b}"][0] + i + 1)
                dve.wait_ge(s_full, n + 1)
                step(V.reduce_max(sm[:, 0, n:n + 1], psS[:, n % 2, :], AX_X))
                step(V.tensor_tensor(sm[:, 1, n:n + 1], sm[:, 0, n:n + 1], uT[:, i, C:C + 1], ALU.add))
                V.tensor_tensor(sm[:, 2, n:n + 1], uT[:, i, C:C + 1], sm[:, 1, n:n + 1], ALU.subtract).then_inc(bias_ready, 1)

            def after_exp(b, i):
                n = b * NT + i
                dve.wait_ge(s_exp, n + 1)
                V.tensor_copy(Pm[b][0][:, i, :], prob[:, n % 2, :]).then_inc(p_high, 1)
                step(V.reciprocal(sm[:, 4, n:n + 1], sm[:, 3, n:n + 1]))
                step(V.tensor_scalar(u[b][0][:, i, :], uT[:, i, 0:C], sm[:, 4, n:n + 1], None, ALU.mult))
                V.scalar_tensor_tensor(out=u[b][1][:, i, :], in0=uT[:, i, 0:C], scalar=sm[:, 4, n:n + 1],
                                       in1=u[b][0][:, i, :], op0=ALU.mult, op1=ALU.subtract).then_inc(u_ready, 1)

            def take_token(b, j):
                f = D[f"PV{b}"][0] + j
                full(f)
                V.tensor_tensor(t1[:, b, j, :], psD[:, f % 2, 0:C], bp_all[:, :], ALU.add).then_inc(d_taken, 1)
                dve.wait_ge(d_taken, f + 1)

            def token_norm(b, dst, n, mark):
                for j in range(NT):
                    last = V.bn_stats(tst[:, j, :], t1[:, b, j, :])
                step(last)
                for j in range(NT):
                    last = V.bn_aggr(tmv[:, j, :], tst[:, j, :])
                step(last)
                V.tensor_scalar(trs[:, 0, :], tmv[:, :, 1], EPS_TOK, None, ALU.add).then_inc(var_ready, 1)
                dve.wait_ge(rstd_ready, n + 1)
                for j in range(NT):
                    last = V.tensor_scalar(dst[:, j, :], t1[:, b, j, :], tmv[:, j, 0:1], trs[:, 1, j:j + 1],
                                           ALU.subtract, ALU.mult)
                if mark is None:
                    step(last)
                else:
                    last.then_inc(mark, 1)

            def fold_tokens(b):
                x = xn[b]
                V.tensor_tensor(xf32[b][:, 0:4, :], x[:, 0:4, :], x[:, 4:8, :], ALU.subtract)
                step(V.tensor_tensor(fold, x[:, 0:4, :], x[:, 4:8, :], ALU.add))
                V.tensor_tensor(xf32[b][:, 4:6, :], fold[:, 0:2, :], fold[:, 2:4, :], ALU.subtract)
                V.tensor_tensor(xf32[b][:, 6:8, :], fold[:, 0:2, :], fold[:, 2:4, :], ALU.add).then_inc(xf32_ready, 1)
                dve.wait_ge(xf_high, b + 1)
                V.tensor_tensor(xf[b][1], xf32[b], xf[b][0], ALU.subtract).then_inc(xf_ready, 1)
                for j in range(NT):
                    last = V.tensor_tensor(t1[:, b, j, :], t1[:, b, j, :], bo_all[:, :], ALU.add)
                step(last)

            def spectra(b):
                for k in range(4):
                    f = D[f"D{b}"][0] + k
                    s = slice((k % 2) * 512, (k % 2 + 1) * 512)
                    low(f, xhat[b][1][:, k // 2, s], psD[:, f % 2, :], xhat[b][0][:, k // 2, s])

            def part(b, which, im):
                return qkv[b][:, im::2, which * C:(which + 1) * C]

            def cross_spectrum(b):
                dve.wait_ge(a_taken, A_AT[f"Q{b}"][1])
                for n, (qi, ki) in enumerate([(0, 0), (1, 1), (1, 0), (0, 1)]):
                    step(V.tensor_tensor(prod[n % 2], part(b, 0, qi), part(b, 1, ki), ALU.mult))
                    last = V.tensor_reduce(cs[:, n, :], prod[n % 2].rearrange("p a (h d) -> p (a h) d", d=DK), AX_X, ALU.add)
                step(last)
                rr, ii, ir, ri = (cs[:, n, :] for n in range(4))
                step(V.tensor_tensor(cs[:, 4, :], pair_mask, ii, ALU.mult))
                V.tensor_tensor(spec[:, 0, :], rr, cs[:, 4, :], ALU.add)
                V.tensor_tensor(cs[:, 5, :], ii, cs[:, 4, :], ALU.subtract)
                step(V.tensor_tensor(cs[:, 6, :], ir, ri, ALU.subtract))
                step(V.tensor_tensor(cs[:, 7, :], pair_mask, cs[:, 6, :], ALU.mult))
                V.tensor_tensor(spec[:, 1, :], cs[:, 7, :], cs[:, 5, :], ALU.add).then_inc(spec_ready, 1)

            def delays(b):
                hs = slice(0, HEADS)
                fe, fo = D[f"C{b}"][0], D[f"C{b}"][0] + 1
                ev, ep = even32[b][hs, 0:2, :], even32[b][hs, 2:4, :]
                full(fe)
                step(V.tensor_copy(ev[:, 0, :], psD[hs, fe % 2, QUARTER:512]))
                V.tensor_tensor(ep[:, 0, :], ev[:, 0, :], psD[hs, fe % 2, 0:QUARTER], ALU.add)
                V.tensor_tensor(ep[:, 1, :], ev[:, 0, :], psD[hs, fe % 2, 0:QUARTER], ALU.subtract).then_inc(d_taken, 1)
                dve.wait_ge(d_taken, fe + 1)
                ecat = ep.rearrange("p a b -> p (a b)")
                full(fo)
                V.tensor_tensor(corr[hs, 0:HALF], ecat, psD[hs, fo % 2, :], ALU.add)
                V.tensor_tensor(corr[hs, HALF:N], ecat, psD[hs, fo % 2, :], ALU.subtract).then_inc(d_taken, 1)
                dve.wait_ge(d_taken, fo + 1)
                step(V.max(top[:, 0:8], corr[hs, :]))
                V.tensor_scalar(top[:, 16:17], top[:, 0:1], -1.0 / (N * DK), None, ALU.mult).then_inc(peak_ready, 1)
                step(V.match_replace(left[hs, :], top[:, 0:8], corr[hs, :], -3.0e38))
                step(V.max(top[:, 8:16], left[hs, :]))
                dve.wait_ge(exp_ready, b + 1)
                step(V.scalar_tensor_tensor(out=left[hs, :], in0=corr[hs, :], scalar=top[:, TOPK - 1:TOPK],
                                            in1=weight[hs, :], op0=ALU.is_ge, op1=ALU.mult))
                step(V.reduce_sum(top[:, 17:18], left[hs, :], AX_X))
                step(V.reciprocal(top[:, 18:19], top[:, 17:18]))
                step(V.tensor_scalar(weight[hs, :], left[hs, :], top[:, 18:19], None, ALU.mult))
                w, s = weight[hs, :], left[hs, 0:HALF]
                V.tensor_tensor(wfold[hs, 0:HALF], w[:, 0:HALF], w[:, HALF:N], ALU.subtract)
                step(V.tensor_tensor(s, w[:, 0:HALF], w[:, HALF:N], ALU.add))
                V.tensor_tensor(wfold[hs, HALF:HALF + QUARTER], s[:, 0:QUARTER], s[:, QUARTER:HALF], ALU.subtract)
                V.tensor_tensor(wfold[hs, HALF + QUARTER:N], s[:, 0:QUARTER], s[:, QUARTER:HALF], ALU.add).then_inc(wfold_ready, 1)
                f = D[f"T{b}"][0]
                low(f, wT[1][:, :], psD[:, f % 2, 0:NT * HEADS], wT[0][:, :])

            def apply_delays(b):
                f = D[f"W{b}"][0]
                full(f)
                V.tensor_scalar(wh_raw[:, :], psD[:, f % 2, 0:NT * HEADS], SPEC_SCALE, None, ALU.mult).then_inc(d_taken, 1)
                dve.wait_ge(d_taken, f + 1)
                pairs = wh_raw[:, :].rearrange("p (a i h) -> p a i h", i=2, h=HEADS)
                m = pair_mask.rearrange("p (a h) -> p a h", h=HEADS)
                wq = [wh[:, n, :].rearrange("p (a h) -> p a h", h=HEADS) for n in range(5)]
                step(V.tensor_tensor(wq[0], m, pairs[:, :, 1, :], ALU.mult))
                V.tensor_tensor(wq[1], pairs[:, :, 1, :], wq[0], ALU.subtract)
                step(V.tensor_tensor(wq[2], m, pairs[:, :, 0, :], ALU.mult))
                step(V.tensor_tensor(wq[3], wq[2], wq[1], ALU.add))
                step(V.tensor_copy(wq[4], pairs[:, :, 0, :]))

                def spread(n):
                    return wh[:, n, :].unsqueeze(2).to_broadcast([P, 4 * HEADS, DK])

                def heads(ap):
                    return ap.rearrange("p a (h d) -> p a h d", d=DK)

                vr, vi = heads(part(b, 2, 0)), heads(part(b, 2, 1))
                yr, yi = heads(Y32[b][:, 0::2, :]), heads(Y32[b][:, 1::2, :])
                pr = [heads(p) for p in prod]

                def w4(n):
                    return wh[:, n, :].rearrange("p (a h) -> p a h", h=HEADS).unsqueeze(3).to_broadcast([P, 4, HEADS, DK])

                V.tensor_tensor(pr[0], vr, w4(4), ALU.mult)
                step(V.tensor_tensor(pr[1], vi, w4(0), ALU.mult))
                step(V.tensor_tensor(yr, pr[0], pr[1], ALU.subtract))
                V.tensor_tensor(pr[0], vr, w4(0), ALU.mult)
                step(V.tensor_tensor(pr[1], vi, w4(3), ALU.mult))
                V.tensor_tensor(yi, pr[0], pr[1], ALU.add).then_inc(y_ready, 1)
                dve.wait_ge(y_high, b + 1)
                V.tensor_tensor(Y[b][1], Y32[b], Y[b][0], ALU.subtract).then_inc(y_low, 1)

            def inverse(b):
                for m in range(CC):
                    fe = D[f"I{b}"][0] + 2 * m
                    fo = fe + 1
                    full(fe)
                    e0 = e_zero[b]
                    e2 = ehalf[b][:, m, :]
                    step(V.tensor_copy(e0, psD[:, fe % 2, QUARTER:512]))
                    V.tensor_tensor(e2[:, 0:QUARTER], e0, psD[:, fe % 2, 0:QUARTER], ALU.add)
                    V.tensor_tensor(e2[:, QUARTER:HALF], e0, psD[:, fe % 2, 0:QUARTER], ALU.subtract).then_inc(d_taken, 1)
                    dve.wait_ge(d_taken, fe + 1)
                    full(fo)
                    V.tensor_tensor(cx32[b][:, m, 0:HALF], e2, psD[:, fo % 2, :], ALU.add)
                    V.tensor_tensor(cx32[b][:, m, HALF:N], e2, psD[:, fo % 2, :], ALU.subtract).then_inc(d_taken, 1)
                for m in range(CC):
                    dve.wait_ge(cx_high, b * CC + m + 1)
                    V.tensor_tensor(cx[b][1][:, m, :], cx32[b][:, m, :], cx[b][0][:, m, :], ALU.subtract).then_inc(cx_low, 1)

            def add_attention(b):
                for j in range(NT):
                    f = D[f"O{b}"][0] + j
                    full(f)
                    last = V.scalar_tensor_tensor(out=t1[:, b, j, :], in0=psD[:, f % 2, 0:C], scalar=1.0 / (N * SPEC_SCALE),
                                                  in1=t1[:, b, j, :], op0=ALU.mult, op1=ALU.add)
                    last.then_inc(d_taken, 1)
                dve.wait_ge(d_taken, f + 1)

            zs(0)
            for i in range(NT + 1):
                if i < NT:
                    score_max(0, i)
                if i >= 1:
                    after_exp(0, i - 1)
            for w in range(4):
                f = D["attnW"][0] + w
                sel = (lambda i: woW[i][:, :, :]) if w == 3 else (lambda i: qkvW[i][:, :, w * C:(w + 1) * C])
                low(f, sel(1), psD[:, f % 2, :].rearrange("p (k c) -> p k c", k=CC), sel(0))
            zs(1)
            for i in range(NT + 1):
                if i < NT:
                    score_max(1, i)
                if i >= 1:
                    after_exp(1, i - 1)
                    take_token(0, i - 1)
            token_norm(0, xn[0], 0, None)
            fold_tokens(0)
            for j in range(NT):
                take_token(1, j)
            token_norm(1, xn[1], 1, None)
            spectra(0)
            fold_tokens(1)
            spectra(1)
            for b in range(B):
                cross_spectrum(b)
                delays(b)
                apply_delays(b)
                inverse(b)
                add_attention(b)
                token_norm(b, yn[b], B + b, yn_ready)

            for k in range(8):
                f = D["YT"][0] + k
                full(f)
                V.tensor_copy(ynT[:, :, k * 256:(k + 1) * 256], psD[:, f % 2, :].rearrange("p (k t) -> p k t", k=CC)).then_inc(d_taken, 1)
            f = D["gate"][0]
            full(f)
            dve.wait_ge(small_in, 16 * SMALL)
            sc3 = gs[:, 0, :].rearrange("p (t e) -> p t e", e=E)
            mx3 = gs[:, 1, :].rearrange("p (t e) -> p t e", e=E)
            i3 = gs[:, 2, :].rearrange("p (t e) -> p t e", e=E)
            oh3 = gs[:, 3, :].rearrange("p (t e) -> p t e", e=E)
            V.tensor_tensor(sc3, psD[:, f % 2, 0:TT * E].rearrange("p (t e) -> p t e", e=E),
                            bg_all[:, :].unsqueeze(1).to_broadcast([P, TT, E]), ALU.add).then_inc(d_taken, 1)
            dve.wait_ge(d_taken, f + 1)
            for j in range(TT):
                last = V.max(mx3[:, j, :], sc3[:, j, :])
            step(last)
            for j in range(TT):
                last = V.max_index(gidx[:, j, :], mx3[:, j, :], sc3[:, j, :])
            step(last)
            step(V.tensor_copy(i3, gidx[:, :, :]))
            V.tensor_tensor(gt[:, 0, :], mx3[:, :, 1], mx3[:, :, 0], ALU.subtract).then_inc(gate_ready, 1)
            dve.wait_ge(gexp_ready, 1)
            step(V.tensor_scalar(gt[:, 2, :], gt[:, 1, :], 1.0, None, ALU.add))
            step(V.reciprocal(gt[:, 3, :], gt[:, 2, :]))
            step(V.tensor_tensor(gt[:, 4, :], gt[:, 1, :], gt[:, 3, :], ALU.mult))
            c3 = comb.rearrange("p (t e) -> p t e", e=E)
            io = iota8.unsqueeze(1).to_broadcast([P, TT, E])
            step(V.tensor_tensor(oh3, io, i3[:, :, 0].unsqueeze(2).to_broadcast([P, TT, E]), ALU.is_equal))
            step(V.tensor_tensor(c3, oh3, gt[:, 3, :].unsqueeze(2).to_broadcast([P, TT, E]), ALU.mult))
            step(V.tensor_tensor(oh3, io, i3[:, :, 1].unsqueeze(2).to_broadcast([P, TT, E]), ALU.is_equal))
            step(V.tensor_tensor(oh3, oh3, gt[:, 4, :].unsqueeze(2).to_broadcast([P, TT, E]), ALU.mult))
            V.tensor_tensor(c3, c3, oh3, ALU.add).then_inc(comb_ready, 1)
            for k in range(4):
                f = D["combT"][0] + k
                full(f)
                V.tensor_copy(combT[0:E, k * 512:(k + 1) * 512], psD[0:E, f % 2, :]).then_inc(d_taken, 1)
            for k in range(8):
                f = D["bias2"][0] + k
                full(f)
                V.tensor_tensor(tt[:, 2 * k:2 * k + 2, :], tt[:, 2 * k:2 * k + 2, :], psD[:, f % 2, :].rearrange("p (a c) -> p a c", a=2), ALU.add).then_inc(d_taken, 1)
            for n in range(E * 4):
                for j in range(4):
                    f = D["ffn"][0] + n * 4 + j
                    tile = (n % 4) * 4 + j
                    full(f)
                    if j == 0:
                        dve.wait_ge(d_taken, f - 3)
                    V.scalar_tensor_tensor(out=tt[:, tile, :], in0=psD[:, f % 2, 0:C], scalar=c3[:, tile, n // 4:n // 4 + 1],
                                           in1=tt[:, tile, :], op0=ALU.mult, op1=ALU.add).then_inc(d_taken, 1)
            for k in range(8):
                f = D["outT"][0] + k
                full(f)
                V.tensor_copy(outT[:, (k // 4) * CC:(k // 4 + 1) * CC, (k % 4) * 256:(k % 4 + 1) * 256],
                              psD[:, f % 2, :].rearrange("p (k t) -> p k t", k=CC)).then_inc(d_taken, 1)

        @block.tensor
        def _(pe):
            nd, na = [0], [0]

            def dbank(name):
                f = nd[0]
                assert D[name][0] <= f < D[name][1], (name, f)
                if f >= 2:
                    pe.wait_ge(d_taken, f - 1)
                nd[0] += 1
                return psD[:, f % 2, :]

            def abank(name):
                f = na[0]
                assert A_AT[name][0] <= f < A_AT[name][1], (name, f)
                if f >= 2:
                    pe.wait_ge(a_taken, f - 1)
                na[0] += 1
                return psA[:, f % 2, :]

            def product(dst, parts, more=()):
                seq = []
                for (lh, ll), (rh, rl) in parts:
                    seq += [(lh, rh), (lh, rl), (ll, rh)]
                seq += list(more)
                for n, (lhs, rhs) in enumerate(seq):
                    last = PE.matmul(dst, lhs, rhs, start=(n == 0), stop=(n == len(seq) - 1))
                return last

            def hl(pair, *ix):
                return tuple(t[ix] for t in pair)

            S = slice(None)
            pe.wait_ge(const_in, 16)
            pe.wait_ge(w_in, 64)
            bank = dbank("wpT")
            for m in range(CC):
                for o in range(CC):
                    last = PE.transpose(bank[:, m * C + o * P:m * C + (o + 1) * P], raw(WP, o)[:, m * P:(m + 1) * P], ident)
            last.then_inc(d_full, 1)
            bank = dbank("A")
            for m in range(CC):
                for o in range(CC):
                    last = PE.matmul(bank[:, m * C:(m + 1) * C], raw(WQ, o)[:, m * P:(m + 1) * P], raw(WK, o), start=(o == 0), stop=(o == CC - 1))
            last.then_inc(d_full, 1)
            pe.wait_ge(d_taken, 1)
            bank = dbank("UW")
            for m in range(CC):
                for o in range(CC):
                    last = PE.matmul(bank[:, m * C:(m + 1) * C], raw(WV, o)[:, m * P:(m + 1) * P], wpT[:, o, :], start=(o == 0), stop=(o == CC - 1))
            last.then_inc(d_full, 1)
            pe.wait_ge(small_in, 16 * SMALL)
            bank = dbank("small")
            for at, w, c in ((0, WK, BQ), (2, WQ, BK)):
                for m in range(CC):
                    for o in range(CC):
                        PE.matmul(bank[:, at + m:at + m + 1], raw(w, o)[:, m * P:(m + 1) * P], cols[:, c, o:o + 1], start=(o == 0), stop=(o == CC - 1))
            for o in range(CC):
                PE.matmul(bank[0:1, 4:5], cols[:, BQ, o:o + 1], cols[:, BK, o:o + 1], start=(o == 0), stop=(o == CC - 1))
            for o in range(CC):
                last = PE.matmul(bank[0:1, 8:8 + C], cols[:, BV, o:o + 1], wpT[:, o, :], start=(o == 0), stop=(o == CC - 1))
            last.then_inc(d_full, 1)

            pe.wait_ge(mean_ready, 1)
            bank = dbank("gn")
            PE.matmul(bank[:, 0:4], blockdiag, mv[:, :, 0], start=True, stop=True).then_inc(d_full, 1)
            pe.wait_ge(spread_ready, 1)
            bank = dbank("gn")
            PE.matmul(bank[:, 0:4], blockdiag, gn[:, 4, :], start=True, stop=True).then_inc(d_full, 1)

            def hcols(i, b, k, lo, n):
                o = (b * CC + k) * N + lo
                return h[i][:, o:o + n]

            def hp(b, k, lo, n):
                return tuple(hcols(i, b, k, lo, n) for i in range(2))

            def G(b):
                pe.wait_ge(h_low, CC * (b + 1))
                if b:
                    pe.wait_ge(s_full, NT * b)
                for m in range(CC):
                    for half in range(2):
                        bank = dbank(f"G{b}")
                        product(bank, [(hl(A, S, k, slice(m * P, (m + 1) * P)), hp(b, k, half * 512, 512)) for k in range(CC)]).then_inc(d_full, 1)

            def U(b):
                pe.wait_ge(rows_ready, 1)
                for i in range(NT):
                    bank = abank(f"U{b}")
                    product(bank[:, 0:C + 1], [(hp(b, k, i * P, P), hl(UW, S, k, S)) for k in range(CC)],
                            [(ones[:, :], ub[:, :])]).then_inc(a_full, 1)

            def scores(b, i):
                n = b * NT + i
                if n >= 2:
                    pe.wait_ge(s_exp, n - 1)
                if i == 0:
                    pe.wait_ge(d_taken, D[f"G{b}"][1])
                for half in range(2):
                    last = product(psS[:, n % 2, half * 512:(half + 1) * 512],
                                   [(hl(z, S, k, slice(i * P, (i + 1) * P)), hp(b, k, half * 512, 512)) for k in range(CC)])
                last.then_inc(s_full, 1)

            def values(b, j):
                if j == 0:
                    pe.wait_ge(p_low, NT * (b + 1))
                    pe.wait_ge(u_ready, NT * (b + 1))
                bank = dbank(f"PV{b}")
                js = slice(j * P, (j + 1) * P)
                for k in range(NT):
                    for n, (l, r) in enumerate(((0, 0), (0, 1), (1, 0))):
                        PE.matmul(bank[:, 0:C], Pm[b][l][:, k, js], u[b][r][:, k, :], start=(k == 0 and n == 0), stop=False)
                for k in range(CC):
                    last = PE.matmul(bank[:, k * P:(k + 1) * P], x_sb[:, b * CC + k, js], ident, start=False, stop=(k == CC - 1))
                last.then_inc(d_full, 1)

            def spectra(b):
                pe.wait_ge(fwd_in, 32)
                pe.wait_ge(xf_ready, b + 1)
                for m in range(CC):
                    cs_ = slice(m * P, (m + 1) * P)
                    bank = dbank(f"D{b}")
                    product(bank, [(hl(xf[b], S, k, cs_), tuple(odd(t, k) for t in fwd)) for k in range(4)]).then_inc(d_full, 1)
                    bank = dbank(f"D{b}")
                    for which in range(2):
                        last = product(bank[:, which * QUARTER:(which + 1) * QUARTER],
                                       [(hl(xf[b], S, 4 + 2 * which + k, cs_), tuple(even(t, which, k) for t in fwd)) for k in range(2)])
                    last.then_inc(d_full, 1)

            def project(b):
                pe.wait_ge(d_taken, D[f"D{b}"][1])
                for j in range(NT):
                    for lo, n in ((0, 512), (512, 256)):
                        bank = abank(f"Q{b}")
                        more = [(dc_row[:, :], qkv_row[:, lo:lo + n])] if j == 6 else []
                        product(bank[:, 0:n], [(hl(xhat[b], S, k, slice(j * P, (j + 1) * P)), hl(qkvW, S, k, slice(lo, lo + n))) for k in range(CC)],
                                more).then_inc(a_full, 1)

            def correlate(b):
                pe.wait_ge(inv32_in, 16)
                pe.wait_ge(spec_ready, b + 1)

                def sp_(chunk):
                    return spec[:, chunk % 2, (chunk // 2) * HEADS:(chunk // 2 + 1) * HEADS]

                bank = dbank(f"C{b}")
                for which in range(2):
                    for k in range(2):
                        last = PE.matmul(bank[0:HEADS, which * QUARTER:(which + 1) * QUARTER], sp_(4 + 2 * which + k),
                                         even(inv32, which, k), start=(k == 0), stop=(k == 1))
                last.then_inc(d_full, 1)
                bank = dbank(f"C{b}")
                for k in range(4):
                    last = PE.matmul(bank[0:HEADS, :], sp_(k), odd(inv32, k), start=(k == 0), stop=(k == 3))
                last.then_inc(d_full, 1)

            def weight_spectrum(b):
                pe.wait_ge(wfold_ready, b + 1)
                bank = dbank(f"T{b}")
                for j in range(NT):
                    last = PE.transpose(bank[:, j * HEADS:(j + 1) * HEADS], wfold[0:HEADS, j * P:(j + 1) * P], ident[0:HEADS, 0:HEADS])
                last.then_inc(d_full, 1)
                pe.wait_ge(d_taken, D[f"T{b}"][1])
                bank = dbank(f"W{b}")
                for j in range(NT):
                    if j < 4:
                        ks = [(k, tuple(odd(t, k)[:, j * P:(j + 1) * P] for t in fwd)) for k in range(4)]
                    else:
                        which = (j - 4) // 2
                        ks = [(4 + 2 * which + k, tuple(even(t, which, k)[:, (j % 2) * P:(j % 2 + 1) * P] for t in fwd)) for k in range(2)]
                    last = product(bank[:, j * HEADS:(j + 1) * HEADS],
                                   [(tab, hl(wT, S, slice(k * HEADS, (k + 1) * HEADS))) for k, tab in ks])
                last.then_inc(d_full, 1)

            def inverse(b):
                pe.wait_ge(inv_in, 32)
                pe.wait_ge(y_low, b + 1)
                for m in range(CC):
                    cs_ = slice(m * P, (m + 1) * P)
                    bank = dbank(f"I{b}")
                    for which in range(2):
                        last = product(bank[:, which * QUARTER:(which + 1) * QUARTER],
                                       [(hl(Y[b], S, 4 + 2 * which + k, cs_), tuple(even(t, which, k) for t in inv)) for k in range(2)])
                    last.then_inc(d_full, 1)
                    bank = dbank(f"I{b}")
                    product(bank, [(hl(Y[b], S, k, cs_), tuple(odd(t, k) for t in inv)) for k in range(4)]).then_inc(d_full, 1)

            def out_project(b):
                pe.wait_ge(cx_low, CC * (b + 1))
                for j in range(NT):
                    bank = dbank(f"O{b}")
                    product(bank[:, 0:C], [(hl(cx[b], S, k, slice(j * P, (j + 1) * P)), hl(woW, S, k, S)) for k in range(CC)]).then_inc(d_full, 1)

            G(0)
            U(0)
            for i in range(NT):
                scores(0, i)
            pe.wait_ge(aw_in, 64)
            for w in range(4):
                bank = dbank("attnW")
                for m in range(CC):
                    for o in range(CC):
                        last = PE.transpose(bank[:, m * C + o * P:m * C + (o + 1) * P], raw(4 + w, o)[:, m * P:(m + 1) * P], ident)
                last.then_inc(d_full, 1)
            G(1)
            U(1)
            for i in range(NT):
                scores(1, i)
                values(0, i)
            for j in range(NT):
                values(1, j)
            for b in range(B):
                spectra(b)
            for b in range(B):
                project(b)
            for b in range(B):
                correlate(b)
                weight_spectrum(b)
                inverse(b)
                out_project(b)

            for k in range(8):
                pe.wait_ge(yn_ready, k // 4 + 1)
                bank = dbank("YT")
                for a in range(2):
                    for m in range(CC):
                        last = PE.transpose(bank[:, m * 256 + a * P:m * 256 + (a + 1) * P],
                                            yn[k // 4][:, (2 * k + a) % NT, m * P:(m + 1) * P], ident)
                last.then_inc(d_full, 1)
            pe.wait_ge(ffn_small, 48)
            pe.wait_ge(d_taken, D["YT"][1])
            bank = dbank("gate")
            for j in range(TT):
                for k in range(CC):
                    last = PE.matmul(bank[:, j * E:(j + 1) * E], ynT[:, k, j * P:(j + 1) * P], wg_sb[:, k, :], start=(k == 0), stop=(k == CC - 1))
            last.then_inc(d_full, 1)
            pe.wait_ge(comb_ready, 1)
            for k in range(4):
                bank = dbank("combT")
                for j in range(4):
                    last = PE.transpose(bank[0:E, j * P:(j + 1) * P], comb[:, (4 * k + j) * E:(4 * k + j + 1) * E], ident)
                last.then_inc(d_full, 1)
            pe.wait_ge(d_taken, D["combT"][1])
            for k in range(8):
                bank = dbank("bias2")
                for a in range(2):
                    last = PE.matmul(bank[:, a * C:(a + 1) * C], combT[0:E, (2 * k + a) * P:(2 * k + a + 1) * P], b2_sb[:, :], start=True, stop=True)
                last.then_inc(d_full, 1)
            for n in range(E * 4):
                e, tb = n // 4, n % 4
                pe.wait_ge(w1_in[e % 2], 16 * (e // 2 + 1))
                pe.wait_ge(w2_in[e % 2], 16 * (e // 2 + 1))
                for m in range(HC):
                    bank = abank("hid")
                    for k in range(CC):
                        last = PE.matmul(bank, w1[e % 2][:, k, m * P:(m + 1) * P], ynT[:, k, tb * 512:(tb + 1) * 512], start=(k == 0), stop=(k == CC - 1))
                    last.then_inc(a_full, 1)
                pe.wait_ge(a_taken, A_AT["hid"][0] + (n + 1) * HC)
                for j in range(4):
                    bank = dbank("ffn")
                    for m in range(HC):
                        last = PE.matmul(bank[:, 0:C], hT[n % 2][:, m, j * P:(j + 1) * P], w2[e % 2][:, m, :], start=(m == 0), stop=(m == HC - 1))
                    last.then_inc(d_full, 1)
            pe.wait_ge(d_taken, D["ffn"][1])
            for k in range(8):
                bank = dbank("outT")
                for a in range(2):
                    for m in range(CC):
                        last = PE.transpose(bank[:, m * 256 + a * P:m * 256 + (a + 1) * P], tt[:, 2 * k + a, m * P:(m + 1) * P], ident)
                last.then_inc(d_full, 1)


_INS = ['x', 'L0_conv_norm_w', 'L0_conv_norm_b', 'L0_conv_wq', 'L0_conv_bq', 'L0_conv_wk', 'L0_conv_bk',
        'L0_conv_wv', 'L0_conv_bv', 'L0_conv_wp', 'L0_conv_bp', 'L1_attn_Wq', 'L1_attn_bq', 'L1_attn_Wk',
        'L1_attn_bk', 'L1_attn_Wv', 'L1_attn_bv', 'L1_attn_Wo', 'L1_attn_bo', 'L1_ffn_Wg', 'L1_ffn_bg',
        'L1_ffn_W1', 'L1_ffn_b1', 'L1_ffn_W2', 'L1_ffn_b2']


def kernel(**inputs):
    import numpy as _np
    import concourse.bacc as _bacc
    from concourse import mybir as _mybir
    from concourse.bass_utils import run_bass_kernel_spmd as _run

    nc = _bacc.Bacc("TRN2", target_bir_lowering=False, num_devices=1)
    arrays, tensors = {}, {}
    given = {name: _np.ascontiguousarray(inputs[name]) for name in _INS}
    for name, a in {**given, **dft_constants()}.items():
        arrays[f"in_{name}_dram"] = a
        tensors[name] = nc.dram_tensor(f"in_{name}_dram", a.shape, _mybir.dt.from_np(a.dtype), kind="ExternalInput").ap()
    out = nc.dram_tensor("out_0_dram", (B, C, 32, 32), _mybir.dt.float32, kind="ExternalOutput").ap()
    conv_attn_moe_kernel(nc, tensors, out)
    r = _run(nc, [arrays], core_ids=[0])
    return r.results[0]["out_0_dram"]
```

```python
from contextlib import ExitStack

import numpy as np

import concourse.bass as bass
from concourse import mybir

ALU = mybir.AluOpType
ACT = mybir.ActivationFunctionType
AX_X = mybir.AxisListType.X
F32 = mybir.dt.float32
F16 = mybir.dt.float16
U32 = mybir.dt.uint32

P = 128
B = 2
C = 256
CC = C // P
N = 1024
NT = N // P
HALF = N // 2
QUARTER = N // 4
HEADS = 8
DK = C // HEADS
TOPK = int(2 * np.log(N))
GROUP = C // 32
E = 8
H = 384
HC = H // P
T = B * N
TT = T // P
TILES = 2 * TT + E - 1
EARLY = 12
EPS_CONV = 1e-6
EPS_TOK = 1e-5
ATT_SCALE = 1.0 / 16
SPEC_SCALE = 1.0 / 32
ODD, EVEN = 4 * HALF, 2 * QUARTER
TAB = ODD + 2 * EVEN


def split16(a):
    hi = a.astype(np.float16)
    return hi, (a - hi.astype(np.float64)).astype(np.float16)


def dft_constants():
    k = np.arange(P)

    def rows(freq, length, last):
        t = np.arange(length)
        ang = 2 * np.pi * np.outer(freq, t) / N
        re, im = np.cos(ang), -np.sin(ang)
        weight = np.full(len(freq), 2.0)
        wim = weight.copy()
        if last:
            im[0] = np.cos(np.pi * t)
            weight[0] = wim[0] = 1.0
        return [re, im], [re * weight[:, None], im * wim[:, None]]

    o0, io0 = rows(1 + 2 * k, HALF, False)
    o1, io1 = rows(1 + 2 * (k + P), HALF, False)
    e, ie = rows(2 + 4 * k, QUARTER, False)
    z, iz = rows(4 * k, QUARTER, True)

    def forward(parts, length):
        m = np.concatenate(parts, 0).T
        return m.reshape(length // P, P, -1).transpose(1, 0, 2).reshape(P, -1)

    def inverse(parts):
        return np.stack(parts, 1).reshape(P, -1)

    fwd = np.concatenate([forward(o0 + o1, HALF), forward(e, QUARTER), forward(z, QUARTER)], 1)
    inv = np.concatenate([inverse(io0 + io1), inverse(ie), inverse(iz)], 1)
    pair_mask = np.ones((P, 4 * HEADS), np.float32)
    pair_mask[0, 3 * HEADS:] = 0.0
    p = np.arange(P)
    consts = np.concatenate([
        np.eye(P), (p[:, None] // GROUP == p[None, :] // GROUP) / float(GROUP),
        pair_mask, np.tile(np.arange(E), (P, 1)),
    ], 1).astype(np.float32)
    tile = np.arange(TILES)
    route = np.zeros((P, 2 * TILES + TT + E * TT), np.float32)
    route[:, 0:TILES] = tile
    route[:, TILES:2 * TILES] = 3 * T + P * tile[None, :] + p[:, None]
    route[:, 2 * TILES:2 * TILES + TT] = P * np.arange(TT)
    route[:, 2 * TILES + TT:] = np.tile(np.arange(TT) > 0, E)
    token = P * np.arange(TT)[None, :] + p[:, None]
    const16 = np.concatenate([np.eye(P), p[:, None] < p[None, :], np.ones((P, P)), np.tile(p, (P, 1)), token, token], 1)
    return {
        "const_f16": const16.astype(np.float16), "route_f32": route,
        "const_f32": consts, "inv_f32": inv.astype(np.float32),
        "fwd_hi": split16(fwd)[0], "fwd_lo": split16(fwd)[1],
        "inv_hi": split16(inv)[0], "inv_lo": split16(inv)[1],
    }


def conv_attn_moe_kernel(nc, g, out, debug=None):
    with ExitStack() as ctx:
        def sb(name, shape, dt=F32):
            return ctx.enter_context(nc.sbuf_tensor(name, shape, dt))

        def sem(name):
            return ctx.enter_context(nc.semaphore(name))

        def view(region, at_kb, dims, dt):
            size = int(np.prod(dims)) * (2 if dt == F32 else 1)
            flat = region[:, int(at_kb * 512):int(at_kb * 512) + size]
            if dt == F32:
                flat = flat.bitcast(F32)
            names = "abc"[:len(dims)]
            return flat.rearrange(f"p ({' '.join(names)}) -> p {' '.join(names)}", **dict(zip(names[1:], dims[1:]))) \
                if len(dims) > 1 else flat

        ps = ctx.enter_context(nc.psum_tensor("ps", [P, 8, 512], F32))
        psS = ps[:, 0:2, :].rearrange("p a n -> p (a n)")
        psV = ps[:, 2:6, :].rearrange("p a n -> p (a n)").rearrange("p (j c) -> p j c", c=C)
        RING1, RING2 = [6, 7], [6, 7, 0, 1, 2, 3, 4, 5]

        const = sb("const", [P, 2 * P + 4 * HEADS + E])
        ident, blockdiag = const[:, 0:P], const[:, P:2 * P]
        pair_mask = const[:, 2 * P:2 * P + 4 * HEADS]
        iota8 = const[:, 2 * P + 4 * HEADS:]
        fwd = [sb("fwd_hi_sb", [P, TAB], F16), sb("fwd_lo_sb", [P, TAB], F16)]
        ones = sb("ones", [1, P], F16)
        dc_row = sb("dc_row", [1, P])
        half_neg = sb("half_neg", [P, NT])

        def odd(tab, k):
            return tab[:, 512 * k:512 * (k + 1)]

        def even(tab, which, k):
            o = ODD + which * EVEN + QUARTER * k
            return tab[:, o:o + QUARTER]

        late = sb("late", [P, 12 * 1024], F16)
        wraw = view(late, 0, [8, CC * C], F32)

        def raw(which, chunk):
            return wraw[:, which, chunk * C:(chunk + 1) * C]

        WQ, WK, WV, WP = range(4)
        prep = sb("prep", [P, 3 * 1024 + 256], F16)
        wpT = view(prep, 0, [CC, C], F32)
        A = [view(prep, 2 + i, [CC, C], F16) for i in range(2)]
        UW = [view(prep, 4 + 1.25 * i, [CC, C + 1], F16) for i in range(2)]
        gq = sb("gq", [P, CC])
        ub = [sb(f"ub_{i}", [1, C + 1], F16) for i in "hl"]
        qkvW = [sb(f"qkvW_{i}", [P, CC, 3 * C], F16) for i in "hl"]
        woW = [sb(f"woW_{i}", [P, CC, C], F16) for i in "hl"]
        cols = sb("cols", [P, 5, CC])
        NW, NB, BQ, BK, BV = range(5)
        bp_all = sb("bp_all", [P, C])
        bo_all = sb("bo_all", [P, C])
        qkv_row = sb("qkv_row", [1, 3 * C])
        bg_all = sb("bg_all", [P, E])

        l0 = sb("l0", [P, 24 * 1024], F16)
        x_sb = [view(l0, 24 * b, [CC, N], F32) for b in range(B)]
        h = [[view(l0, 24 * b + 8 + 4 * i, [CC, N], F16) for i in range(2)] for b in range(B)]
        z = [[view(l0, 24 * b + 16 + 4 * i, [CC, N], F16) for i in range(2)] for b in range(B)]
        bn = sb("bn", [P, B * CC, 2, 6])
        mv = sb("mv", [P, B * CC, 2])
        gn = sb("gn", [P, 8, B * CC])
        inv32 = view(l0, 24, [TAB], F32)
        inv = [sb("inv_hi_sb", [P, TAB], F16), sb("inv_lo_sb", [P, TAB], F16)]
        tiles = sb("tiles", [P, 8 * 1024], F16)
        prob = view(tiles, 0, [2, N], F32)
        Pt = [view(tiles, 8 + 4 * i, [2, N], F16) for i in range(2)]
        uT = sb("uT", [P, 2, C + 1])
        u = [sb(f"u_{i}", [P, 2, C], F16) for i in "hl"]
        sm = sb("sm", [P, 5, B * NT])
        t1 = sb("t1", [P, B, NT, C])
        tst = sb("tst", [P, NT, 6])
        tmv = sb("tmv", [P, NT, 2])
        trs = sb("trs", [P, 2, NT])
        work = sb("work", [P, 8 * 1024], F16)
        h32 = view(work, 0, [2, N], F32)
        xn = view(work, 0, [NT, C], F32)
        xf32 = view(work, 8, [NT, C], F32)
        ub32 = view(work, 8, [C + 1], F32)[0:1, :]
        xf = [view(work, 4 * i, [NT, C], F16) for i in range(2)]
        xhat = [view(work, 8 + 4 * i, [CC, N], F16) for i in range(2)]
        fold = [view(l0, 16, [4, C], F32), view(tiles, 0, [4, C], F32)]
        prod = [[view(l0, 16 + 4 * i, [4, C], F32) for i in range(2)], [view(work, 4 * i, [4, C], F32) for i in range(2)]]
        qk = sb("qk", [P, NT, 2 * C])
        val = [sb(f"val{b}", [P, NT, C]) for b in range(B)]
        cs = sb("cs", [P, 8, 4 * HEADS])
        spec = sb("spec", [P, 2, 4 * HEADS])
        dspace = [[view(l0, 4 * i, [N], F32) for i in range(4)], [view(tiles, 4 * i, [N], F32) for i in range(4)]]
        even32 = [view(l0, 16, [4, QUARTER], F32), view(work, 0, [4, QUARTER], F32)]
        top = sb("top", [HEADS, 24])
        wT = [sb(f"wT_{i}", [P, NT * HEADS], F16) for i in "hl"]
        wh = sb("wh", [P, 5, 4 * HEADS])
        wh_raw = sb("wh_raw", [P, NT * HEADS])
        Y32 = view(late, 0, [NT, C], F32)
        Y = [view(late, 8 + 4 * i, [NT, C], F16) for i in range(2)]
        cx32 = view(late, 0, [CC, N], F32)
        cx = [view(late, 16 + 4 * i, [CC, N], F16) for i in range(2)]
        yn = qk[:, :, 0:C]
        ehalf = [view(l0, 16, [CC, 3 * QUARTER], F32), view(work, 0, [CC, 3 * QUARTER], F32)]
        RING, FIRST = [], {}

        def ring(name, n, taker, high=0):
            FIRST.setdefault(name, len(RING))
            RING.extend([(taker, high, name)] * n)

        def step_fills(n):
            ring(f"U{n}", 1, "A")
            if n == 0:
                ring("gn1", 2, "V")
            if 1 <= n <= 4:
                ring(f"attnW{n - 1}", 1, "V", 1)
            if n in (5, 6):
                ring(f"G1_{n - 5}", 2, "V", 1)
            if n in (14, 15):
                ring(f"D0_{n - 14}", 2, "V", 1)

        for args in [("gn0", 2, "V"), ("wpT", 1, "V"), ("A", 1, "V", 1), ("UW", 1, "V", 1), ("small", 1, "V"),
                     ("G0_0", 2, "V", 1), ("G0_1", 2, "V", 1)]:
            ring(*args)
        for n in range(B * NT):
            step_fills(n)
        PHASE2 = len(RING)
        for args in [("Q0", 16, "A"), ("D1_0", 2, "V", 1), ("D1_1", 2, "V", 1), ("C0", 2, "V"), ("Q1", 16, "A"), ("T0", 1, "V", 1), ("W0", 1, "V"),
                     ("I0", 4, "V"), ("C1", 2, "V"), ("O0", 8, "V"), ("T1", 1, "V", 1), ("W1", 1, "V"), ("I1", 4, "V"),
                     ("YT0", 4, "A"), ("gate0", 1, "V"), ("O1", 8, "V"), ("YT1", 4, "A"), ("gate1", 1, "V"), ("rank", 1, "V"),
                     ("perm", 1, "V")]:
            ring(*args)

        def bank_of(f):
            return RING1[f % 2] if f < PHASE2 else RING2[(f - PHASE2) % 8]

        def bank(f):
            return ps[:, bank_of(f), :]

        def taken_count(f):
            return sum(t == RING[f][0] for t, _, _ in RING[:f + 1])

        def high_count(f):
            return sum(hi for _, hi, _ in RING[:f + 1])

        filled, v_taken, a_taken, high_made = sem("filled"), sem("v_taken"), sem("a_taken"), sem("high_made")
        sums_full, sums_taken = sem("sums_full"), sem("sums_taken")

        def wait_taken(eng, f):
            eng.wait_ge(v_taken if RING[f][0] == "V" else a_taken, taken_count(f))

        s_full, s_exp = sem("s_full"), sem("s_exp")
        x_in = [sem(f"x_in{q}") for q in range(B * CC)]
        w_in, aw_in, small_in, late_in, const_in, fwd_in = sem("w_in"), sem("aw_in"), sem("small_in"), sem("late_in"), sem("const_in"), sem("fwd_in")
        inv32_in, inv_in = sem("inv32_in"), sem("inv_in")
        rows_ready, mean_ready, spread_ready, affine_ready = sem("rows_ready"), sem("mean_ready"), sem("spread_ready"), sem("affine_ready")
        h32_ready, h0_low, h1_high, h1_low = sem("h32_ready"), sem("h0_low"), sem("h1_high"), sem("h1_low")
        bias_ready, p_high, p_low, u_ready = sem("bias_ready"), sem("p_high"), sem("p_low"), sem("u_ready")
        var_ready, rstd_ready, xf32_ready, xf_high, xf_ready = (sem(n) for n in ("var_ready", "rstd_ready", "xf32_ready", "xf_high", "xf_ready"))
        spec_ready, peak_ready, exp_ready, wfold_ready = (sem(n) for n in ("spec_ready", "peak_ready", "exp_ready", "wfold_ready"))
        y_ready, y_high, y_low = sem("y_ready"), sem("y_high"), sem("y_low")
        cx32_ready, cx_high, cx_low = sem("cx32_ready"), sem("cx_high"), sem("cx_low")
        yn_ready, t_bo = sem("yn_ready"), sem("t_bo")
        v_step = sem("v_step")
        root_ready = sem("root_ready")
        out_sem = sem("out_sem")
        consts_made = sem("consts_made")
        ACTV = nc.scalar.activation
        V, PL, PE = nc.vector, nc.gpsimd, nc.tensor


        xrows = nc.dram_tensor("token_rows_dram", (T, 2 * C), F16).ap()
        yrows = nc.dram_tensor("expert_rows_dram", (2 * T + TILES * P, C), F32).ap()
        late_consts = uT[:, :, :].rearrange("p a c -> p (a c)")
        small_a, small_b = (u[i][:, :, :].rearrange("p a c -> p (a c)").bitcast(F32) for i in range(2))
        const16 = late_consts[:, 0:2 * P + TT].bitcast(F16)
        ident16, before, all_ones, iota128 = (const16[:, k * P:(k + 1) * P] for k in range(4))
        token_id = const16[:, 4 * P:]
        route_f32 = late_consts[:, 2 * P + TT:2 * P + TT + 2 * TILES + TT + E * TT]
        iota_tile, spare_row = route_f32[:, 0:TILES], route_f32[:, TILES:2 * TILES]
        thresholds, scan_mask = route_f32[:, 2 * TILES:2 * TILES + TT], route_f32[:, 2 * TILES + TT:]
        wg_sb = sb("wg_sb", [P, CC, E])
        b1_sb = sb("b1_sb", [P, E, HC])
        b2_all = qk[:, :, C:2 * C]
        stage = [view(prep, 3 * i, [CC * H], F32) for i in range(2)]
        experts = view(l0, 0, [E, 4 * CC * H], F16)
        yn16 = [val[b][:, :, :].rearrange("p a c -> p (a c)").bitcast(F16).rearrange("p (a c) -> p a c", a=NT) for b in range(B)]
        ynT = view(work, 8, [CC, N], F32)
        sc, mx = (small_a[:, k * P:(k + 1) * P].rearrange("p (j e) -> p j e", e=E) for k in range(2))
        gidx = small_b[:, 0:P].bitcast(U32).rearrange("p (j e) -> p j e", e=E)
        gt = small_b[:, P:P + 4 * TT].rearrange("p (k j) -> p k j", k=4)
        cum = small_b[:, P + 4 * TT:P + 4 * TT + 4 * E].rearrange("p (k e) -> p k e", k=4)
        rt = view(work, 0, [6, TT * E], F32)
        oh = view(work, 3, [3, TT * E], F16)
        oh32 = view(work, 4, [2, TT * E], F32)
        slot = view(work, 5, [3, 2 * TT], F32)
        slot_u = view(work, 5.5, [3, 2 * TT], F32).bitcast(U32)
        onehot_p = view(tiles, 8, [2 * TT, P], F16)
        onehot_t = view(tiles, 0, [2 * TT, 2 * TILES], F16)
        pf = view(work, 6, [5, TILES], F32)
        idx = sb("idx", [P, 2, TILES], U32)
        where = sb("where_sb", [1, TILES], U32)
        wcmp = view(work, 7, [TILES * E + TILES + TILES], F16)
        gx = view(late, 0, [6, 2 * C], F16)
        hf = view(late, 6, [3, HC * P], F32)
        hh = [view(late, 10.5 + 2.25 * i, [3, HC * P], F16) for i in range(2)]
        xT = view(late, 15, [2, 4 * P], F16)
        ysb = view(late, 17, [4, C], F32)
        psx = [ps[:, 0, :], ps[:, 1, :]]
        psh = [ps[:, 2, 0:HC * P], ps[:, 3, 0:HC * P]]
        psy = [ps[:, 4, 0:C], ps[:, 5, 0:C]]
        ygot = view(l0, 0, [2, TT, C], F32)
        outT = view(l0, 32, [B * CC, N], F32)
        tt = t1[:, :, :, :].rearrange("p b j c -> p (b j) c")
        ffn_in, b1_in, b2_in = sem("ffn_in"), sem("b1_in"), sem("b2_in")
        stage_in = [sem("stage_in0"), sem("stage_in1")]
        we_high, we_low = sem("we_high"), sem("we_low")
        row_high, row_low, row_out = sem("row_high"), sem("row_low"), sem("row_out")
        gate_ready, gexp_ready, choice_ready, perm_part, idx_ready, where_ready = (
            sem(n) for n in ("gate_ready", "gexp_ready", "choice_ready", "perm_part", "idx_ready", "where_ready"))
        gathered = [sem(f"gathered{k}") for k in range(6)]
        scattered = [sem(f"scattered{k}") for k in range(4)]
        x_turned, x_taken, hid_full, gelu_done, hid_high, hid_low, y_full, y_taken = (
            sem(n) for n in ("x_turned", "x_taken", "hid_full", "gelu_done", "hid_high", "hid_low", "y_full", "y_taken"))
        y_in = [sem(f"y_in{k}") for k in range(8)]
        combined, out_turned, out_taken = sem("combined"), sem("out_turned"), sem("out_taken")

        block = ctx.enter_context(nc.Block())

        @block.sync
        def _(sp):
            sp.dma_start(const[:, :], g["const_f32"]).then_inc(const_in, 16)
            for b in range(B):
                for k in range(CC):
                    sp.dma_start(x_sb[b][:, k, :], g["x"][b].rearrange("(k p) a b -> k p (a b)", p=P)[k]).then_inc(x_in[b * CC + k], 16)
            for i, name in enumerate(["fwd_hi", "fwd_lo"]):
                sp.dma_start(fwd[i][:, :], g[name]).then_inc(fwd_in, 16)
            for i, name in enumerate(["inv_hi", "inv_lo"]):
                sp.dma_start(inv[i][:, :], g[name]).then_inc(inv_in, 16)
            sp.wait_ge(sums_full, B * NT)
            sp.dma_start(inv32, g["inv_f32"]).then_inc(inv32_in, 16)
            sp.dma_start(wg_sb[:, :, :], g["L1_ffn_Wg"].rearrange("(k p) e -> p k e", p=P)).then_inc(ffn_in, 16)
            for e in range(E):
                sp.dma_start(b1_sb[:, E - 1 - e, :], g["L1_ffn_b1"][e].rearrange("(k p) -> p k", p=P), allow_slow_non_contiguous=True).then_inc(b1_in, 16)

            def stage_load(n):
                if n == 0:
                    sp.wait_ge(filled, FIRST[f"U{B * NT - 1}"] + 1)
                if n >= 2:
                    sp.wait_ge(we_low, n - 1)
                w = g["L1_ffn_W2" if n % 2 else "L1_ffn_W1"][n // 2].rearrange("(k p) h -> p k h", p=P)
                sp.dma_start(stage[n % 2].rearrange("p (k h) -> p k h", k=HC if n % 2 else CC), w).then_inc(stage_in[n % 2], 16)

            for n in range(2):
                stage_load(n)
            sp.wait_ge(sums_full, B * NT)
            sp.wait_ge(u_ready, B * NT)
            sp.dma_start(const16, g["const_f16"]).then_inc(ffn_in, 16)
            sp.dma_start(route_f32, g["route_f32"]).then_inc(ffn_in, 16)
            for n in range(2, 8):
                stage_load(n)
            sp.wait_ge(spec_ready, B)
            for e in range(E):
                sp.dma_start(b2_all[:, E - 1 - e, :], g["L1_ffn_b2"][e].partition_broadcast(P)).then_inc(b2_in, 16)
            for n in range(8, EARLY):
                stage_load(n)
            for b in range(B):
                sp.wait_ge(row_low, b + 1)
                sp.dma_start(xrows[b * N:(b + 1) * N, :].rearrange("(j p) c -> p j c", p=P), yn16[b]).then_inc(row_out, 16)
                if b == 0:
                    for n in range(EARLY, 2 * E):
                        stage_load(n)
            for k in range(4):
                sp.wait_ge(scattered[k], 16 * len(range(k, TILES, 4)))
            for q in range(8):
                for c in range(2):
                    sp.dma_start(ygot[:, c, 2 * q:2 * q + 2, :],
                                 yrows[c * T + 2 * q * P:c * T + 2 * (q + 1) * P, :].rearrange("(j p) c -> p j c", p=P)).then_inc(y_in[q], 16)
            for b in range(B):
                for half in range(2):
                    sp.wait_ge(out_taken, 4 * b + 2 * half + 2)
                    sp.dma_start(out[b].rearrange("(k p) a b -> p k (a b)", p=P)[:, :, half * HALF:(half + 1) * HALF],
                                 outT[:, b * CC:(b + 1) * CC, half * HALF:(half + 1) * HALF]).then_inc(out_sem, 16)
            sp.wait_ge(out_sem, 16 * 2 * B)

        @block.gpsimd
        def _(pool):
            for n, name in enumerate(["L0_conv_norm_w", "L0_conv_norm_b", "L0_conv_bq", "L0_conv_bk", "L0_conv_bv"]):
                pool.dma_start(cols[:, n, :], g[name].rearrange("(k p) -> p k", p=P), allow_slow_non_contiguous=True).then_inc(small_in, 16)
            PL.memset(half_neg[:, :], -0.5).then_inc(consts_made, 1)
            pool.dma_start(bp_all[:, :], g["L0_conv_bp"].partition_broadcast(P)).then_inc(late_in, 16)
            pool.dma_start(bo_all[:, :], g["L1_attn_bo"].partition_broadcast(P)).then_inc(late_in, 16)
            pool.dma_start(bg_all[:, :], g["L1_ffn_bg"].partition_broadcast(P)).then_inc(late_in, 16)
            for n, name in enumerate(["bq", "bk", "bv"]):
                pool.dma_start(qkv_row[:, n * C:(n + 1) * C], g[f"L1_attn_{name}"].rearrange("(a n) -> a n", a=1)).then_inc(late_in, 16)
            pool.wait_ge(consts_made, 1)
            for b in range(B):
                wait_taken(pool, FIRST[f"gn{b}"] + 1)
                PL.tensor_tensor(gn[:, 3, b * CC:(b + 1) * CC], gn[:, 5, b * CC:(b + 1) * CC], half_neg[:, 0:CC], ALU.pow).then_inc(root_ready, 1)

            def rstd(n):
                pool.wait_ge(var_ready, n + 1)
                PL.tensor_tensor(trs[:, 1, :], trs[:, 0, :], half_neg[:, :], ALU.pow).then_inc(rstd_ready, 1)

            for n in range(B * NT):
                if n in (2, 3):
                    k = n - 2
                    pool.wait_ge(h1_high, k + 1)
                    PL.tensor_tensor(h[1][1][:, k, :], h32[:, k, :], h[1][0][:, k, :], ALU.subtract).then_inc(h1_low, 1)
                pool.wait_ge(p_high, n + 1)
                if n >= 2:
                    pool.wait_ge(sums_full, n - 1)
                PL.tensor_tensor(Pt[1][:, n % 2, :], prob[:, n % 2, :], Pt[0][:, n % 2, :], ALU.subtract).then_inc(p_low, 1)
                if n == 8:
                    rstd(0)
            def expert_low(n):
                pool.wait_ge(we_high, n + 1)
                o = (n % 2) * 2 * CC * H
                PL.tensor_tensor(experts[:, E - 1 - n // 2, o + CC * H:o + 2 * CC * H], stage[n % 2],
                                 experts[:, E - 1 - n // 2, o:o + CC * H], ALU.subtract).then_inc(we_low, 1)

            def rows_low(b):
                pool.wait_ge(row_high, b + 1)
                PL.tensor_tensor(yn16[b][:, :, C:2 * C], yn, yn16[b][:, :, 0:C], ALU.subtract).then_inc(row_low, 1)

            rstd(1)
            for n in range(8):
                expert_low(n)
            rstd(2)
            for n in range(8, EARLY):
                expert_low(n)
            rows_low(0)
            rstd(3)
            rows_low(1)
            for n in range(EARLY, 2 * E):
                expert_low(n)
            for b in range(B):
                pool.wait_ge(row_out, 16 * B)
            pool.wait_ge(idx_ready, 1)
            for i in range(TILES + 7):
                if i < TILES:
                    if i >= 6:
                        pool.wait_ge(x_turned, i - 5)
                    pool.indirect_dma_start(gx[:, i % 6, :], None, xrows, bass.IndirectOffsetOnAxis(idx[:, 0, i:i + 1], 0)).then_inc(gathered[i % 6], 16)
                s = i - 7
                if s >= 0:
                    pool.wait_ge(y_taken, s + 1)
                    pool.indirect_dma_start(yrows, bass.IndirectOffsetOnAxis(idx[:, 1, s:s + 1], 0), ysb[:, s % 4, :], None).then_inc(scattered[s % 4], 16)

        @block.scalar
        def _(act):
            for n, name in enumerate(["wq", "wk", "wv", "wp"]):
                act.dma_start(wraw[:, n, :].rearrange("p (k c) -> p k c", k=CC),
                              g[f"L0_conv_{name}"].rearrange("(k p) c -> p k c", p=P)).then_inc(w_in, 16)
            for n, name in enumerate(["Wq", "Wk", "Wv", "Wo"]):
                act.dma_start(wraw[:, 4 + n, :].rearrange("p (k c) -> p k c", k=CC),
                              g[f"L1_attn_{name}"].rearrange("(k p) c -> p k c", p=P)).then_inc(aw_in, 16)

            def make_high(f, dst, src, **kw):
                assert RING[f][1]
                act.wait_ge(filled, f + 1)
                ACTV(dst, src, ACT.Identity, **kw).then_inc(high_made, 1)

            def take(f, dst, src, **kw):
                act.wait_ge(filled, f + 1)
                ACTV(dst, src, ACT.Identity, **kw).then_inc(a_taken, 1)

            def weights():
                f = FIRST["A"]
                make_high(f, A[0].rearrange("p k c -> p (k c)"), bank(f), scale=ATT_SCALE)
                f = FIRST["UW"]
                make_high(f, UW[0][:, :, 0:C], bank(f).rearrange("p (k c) -> p k c", k=CC))

            def attn_weight_high(w):
                f = FIRST[f"attnW{w}"]
                dst = woW[0][:, :, :] if w == 3 else qkvW[0][:, :, w * C:(w + 1) * C]
                make_high(f, dst, bank(f).rearrange("p (k c) -> p k c", k=CC))

            def normalise(b):
                act.wait_ge(affine_ready, b + 1)
                if b:
                    act.wait_ge(h0_low, CC)
                for k in range(CC):
                    q = b * CC + k
                    ACTV(h32[:, k, :], x_sb[b][:, k, :], ACT.Identity, bias=gn[:, 7, q:q + 1],
                         scale=gn[:, 6, q:q + 1]).then_inc(h32_ready, 1)

            def z_high(b, m):
                for half in range(2):
                    f = FIRST[f"G{b}_{m}"] + half
                    make_high(f, z[b][0][:, m, half * 512:(half + 1) * 512], bank(f), bias=gq[:, m:m + 1])

            def x_high(b, m):
                for k in range(2):
                    f = FIRST[f"D{b}_{m}"] + k
                    make_high(f, xhat[0][:, m, k * 512:(k + 1) * 512], bank(f))

            def xf_hi(b):
                act.wait_ge(xf32_ready, b + 1)
                ACTV(xf[0].rearrange("p a c -> p (a c)"), xf32.rearrange("p a c -> p (a c)"), ACT.Identity).then_inc(xf_high, 1)

            def take_qkv(b):
                for k in range(2 * NT):
                    f = FIRST[f"Q{b}"] + k
                    if k == 0 and b:
                        act.wait_ge(spec_ready, b)
                    dst = qk[:, k // 2, :] if k % 2 == 0 else val[b][:, k // 2, :]
                    take(f, dst, bank(f)[:, 0:512 if k % 2 == 0 else 256])

            def delays(b):
                act.wait_ge(peak_ready, b + 1)
                ACTV(dspace[b][2][0:HEADS, :], dspace[b][0][0:HEADS, :], ACT.Exp, bias=top[:, 16:17], scale=1.0 / (N * DK)).then_inc(exp_ready, 1)

            def w_high(b):
                f = FIRST[f"T{b}"]
                make_high(f, wT[0][:, :], bank(f)[:, 0:NT * HEADS])

            def y_hi(b):
                act.wait_ge(y_ready, b + 1)
                ACTV(Y[0].rearrange("p a c -> p (a c)"), Y32.rearrange("p a c -> p (a c)"), ACT.Identity).then_inc(y_high, 1)

            def cx_hi(b):
                for m in range(CC):
                    wait_taken(act, FIRST[f"I{b}"] + 2 * m + 1)
                    ACTV(cx[0][:, m, :], cx32[:, m, :], ACT.Identity).then_inc(cx_high, 1)

            def expert_high(n):
                act.wait_ge(stage_in[n % 2], 16 * (n // 2 + 1))
                if n == 0:
                    act.wait_ge(sums_full, B * NT)
                if n == 4:
                    act.wait_ge(filled, FIRST["C1"] + 2)
                if n == 8:
                    act.wait_ge(cx_low, CC)
                o = (n % 2) * 2 * CC * H
                ACTV(experts[:, E - 1 - n // 2, o:o + CC * H], stage[n % 2], ACT.Identity).then_inc(we_high, 1)

            def rows_high(b):
                act.wait_ge(yn_ready, b + 1)
                ACTV(yn16[b][:, :, 0:C], yn, ACT.Identity).then_inc(row_high, 1)

            def turned_tokens(b):
                for k in range(4):
                    f = FIRST[f"YT{b}"] + k
                    if b and k == 0:
                        wait_taken(act, FIRST["gate0"])
                    take(f, ynT[:, :, k * 2 * P:(k + 1) * 2 * P], bank(f).rearrange("p (k t) -> p k t", k=CC))

            weights()
            normalise(0)
            z_high(0, 0)
            z_high(0, 1)
            for n in range(B * NT):
                f = FIRST[f"U{n}"]
                if n >= 2:
                    act.wait_ge(u_ready, n - 1)
                take(f, uT[:, n % 2, :], bank(f)[:, 0:C + 1])
                act.wait_ge(bias_ready, n + 1)
                if n >= 2:
                    act.wait_ge(p_low, n - 1)
                ACTV(prob[:, n % 2, :], psS, ACT.Exp, bias=sm[:, 2, n:n + 1], accum_out=sm[:, 3, n:n + 1]).then_inc(s_exp, 1)
                act.wait_ge(s_exp, n + 1)
                if n >= 2:
                    act.wait_ge(sums_full, n - 1)
                ACTV(Pt[0][:, n % 2, :], prob[:, n % 2, :], ACT.Identity).then_inc(p_high, 1)
                if n == 1:
                    normalise(1)
                if n in (2, 3):
                    act.wait_ge(h32_ready, CC + n - 1)
                    ACTV(h[1][0][:, n - 2, :], h32[:, n - 2, :], ACT.Identity).then_inc(h1_high, 1)
                if 1 <= n <= 4:
                    attn_weight_high(n - 1)
                if n in (5, 6):
                    z_high(1, n - 5)
                if n == 11:
                    xf_hi(0)
                if n in (14, 15):
                    x_high(0, n - 14)
            take_qkv(0)
            xf_hi(1)
            x_high(1, 0)
            x_high(1, 1)
            delays(0)
            take_qkv(1)
            for n in range(4):
                expert_high(n)
            w_high(0)
            y_hi(0)
            cx_hi(0)
            delays(1)
            for n in range(4, 8):
                expert_high(n)
            w_high(1)
            y_hi(1)
            for n in range(8, EARLY):
                expert_high(n)
            cx_hi(1)
            rows_high(0)
            turned_tokens(0)
            rows_high(1)
            turned_tokens(1)
            for n in range(EARLY, 2 * E):
                expert_high(n)
            act.wait_ge(gate_ready, 1)
            ACTV(gt[:, 1, :], gt[:, 0, :], ACT.Exp).then_inc(gexp_ready, 1)
            act.wait_ge(b1_in, 16 * E)
            act.wait_ge(where_ready, 1)
            for s in range(TILES):
                e = act.value_load(where[0:1, s:s + 1], min_val=0, max_val=E - 1)
                act.wait_ge(hid_full, s + 1)
                if s >= 3:
                    act.wait_ge(hid_low, s - 2)
                for m in range(HC):
                    last = ACTV(hf[:, s % 3, m * P:(m + 1) * P], psh[s % 2][:, m * P:(m + 1) * P], ACT.Gelu,
                                bias=b1_sb[:, bass.ds(e, 1), m])
                last.then_inc(gelu_done, 1)
                act.wait_ge(gelu_done, s + 1)
                if s >= 3:
                    act.wait_ge(y_full, s - 2)
                ACTV(hh[0][:, s % 3, :], hf[:, s % 3, :], ACT.Identity).then_inc(hid_high, 1)
            for q in range(8):
                act.wait_ge(out_turned, q + 1)
                ACTV(outT[:, (q // 4) * CC:(q // 4 + 1) * CC, (q % 4) * 2 * P:(q % 4 + 1) * 2 * P],
                     ps[:, 6 + q % 2, :].rearrange("p (k t) -> p k t", k=CC), ACT.Identity).then_inc(out_taken, 1)

        @block.vector
        def _(dve):
            steps = [0]

            def step(ins):
                steps[0] += 1
                ins.then_inc(v_step, 1)
                dve.wait_ge(v_step, steps[0])

            def full(f):
                dve.wait_ge(filled, f + 1)

            def low(f, dst, src, hi, scalar=1.0, op0=ALU.mult):
                full(f)
                dve.wait_ge(high_made, high_count(f))
                V.scalar_tensor_tensor(out=dst, in0=src, scalar=scalar, in1=hi, op0=op0, op1=ALU.subtract).then_inc(v_taken, 1)

            V.memset(ones[:, :], 1.0)
            step(V.memset(dc_row[:, :], 0.0))
            V.memset(dc_row[:, 0:1], float(N)).then_inc(rows_ready, 1)

            def channel_stats(b):
                for q in range(b * CC, (b + 1) * CC):
                    dve.wait_ge(x_in[q], 16)
                    for s in range(2):
                        last = V.bn_stats(bn[:, q, s, :], x_sb[b][:, q % CC, s * 512:(s + 1) * 512])
                    step(last)
                    last = V.bn_aggr(mv[:, q, :], bn[:, q, :, :].rearrange("p a b -> p (a b)"))
                last.then_inc(mean_ready, 1)

            def group_mean(b):
                q = slice(b * CC, (b + 1) * CC)
                f = FIRST[f"gn{b}"]
                full(f)
                V.tensor_copy(gn[:, 1, q], bank(f)[:, 0:CC]).then_inc(v_taken, 1)
                wait_taken(dve, f)
                step(V.tensor_tensor(gn[:, 2, q], mv[:, q, 0], gn[:, 1, q], ALU.subtract))
                step(V.tensor_tensor(gn[:, 4, q], gn[:, 2, q], gn[:, 2, q], ALU.mult))
                V.tensor_tensor(gn[:, 4, q], gn[:, 4, q], mv[:, q, 1], ALU.add).then_inc(spread_ready, 1)

            def group_affine(b):
                q = slice(b * CC, (b + 1) * CC)
                f = FIRST[f"gn{b}"] + 1
                full(f)
                V.tensor_scalar(gn[:, 5, q], bank(f)[:, 0:CC], EPS_CONV, None, ALU.add).then_inc(v_taken, 1)
                dve.wait_ge(small_in, 16 * 5)
                dve.wait_ge(root_ready, b + 1)
                step(V.tensor_tensor(gn[:, 6, q], gn[:, 3, q], cols[:, NW, :], ALU.mult))
                step(V.tensor_tensor(gn[:, 2, q], gn[:, 1, q], gn[:, 6, q], ALU.mult))
                V.tensor_tensor(gn[:, 7, q], cols[:, NB, :], gn[:, 2, q], ALU.subtract).then_inc(affine_ready, 1)

            channel_stats(0)
            group_mean(0)
            group_affine(0)
            f = FIRST["wpT"]
            full(f)
            V.tensor_copy(wpT.rearrange("p k c -> p (k c)"), bank(f)).then_inc(v_taken, 1)
            for k in range(CC):
                dve.wait_ge(h32_ready, k + 1)
                step(V.tensor_copy(h[0][0][:, k, :], h32[:, k, :]))
                V.tensor_tensor(h[0][1][:, k, :], h32[:, k, :], h[0][0][:, k, :], ALU.subtract).then_inc(h0_low, 1)
                if k == 0:
                    f = FIRST["A"]
                    low(f, A[1].rearrange("p k c -> p (k c)"), bank(f), A[0].rearrange("p k c -> p (k c)"), scalar=ATT_SCALE)
            f = FIRST["UW"]
            low(f, UW[1][:, :, 0:C], bank(f).rearrange("p (k c) -> p k c", k=CC), UW[0][:, :, 0:C])
            f = FIRST["small"]
            full(f)
            V.tensor_scalar(gq[:, :], bank(f)[:, 0:2], ATT_SCALE, None, ALU.mult)
            V.tensor_copy(ub32[:, 0:C], bank(f)[0:1, 8:8 + C])
            V.tensor_scalar(ub32[:, C:C + 1], bank(f)[0:1, 4:5], ATT_SCALE, None, ALU.mult)
            V.tensor_scalar(gn[:, 0, 0:2], bank(f)[:, 2:4], ATT_SCALE, None, ALU.mult).then_inc(v_taken, 1)
            wait_taken(dve, f)
            V.tensor_copy(ub[0][:, :], ub32[:, :])
            step(V.tensor_copy(UW[0][:, :, C], gn[:, 0, 0:2]))
            V.tensor_tensor(ub[1][:, :], ub32[:, :], ub[0][:, :], ALU.subtract)
            V.tensor_tensor(UW[1][:, :, C], gn[:, 0, 0:2], UW[0][:, :, C], ALU.subtract).then_inc(rows_ready, 1)

            def attn_weight_low(w):
                f = FIRST[f"attnW{w}"]
                dst = [woW[i][:, :, :] if w == 3 else qkvW[i][:, :, w * C:(w + 1) * C] for i in range(2)]
                low(f, dst[1], bank(f).rearrange("p (k c) -> p k c", k=CC), dst[0])

            def z_low(b, m):
                for half in range(2):
                    f = FIRST[f"G{b}_{m}"] + half
                    s = slice(half * 512, (half + 1) * 512)
                    low(f, z[b][1][:, m, s], bank(f), z[b][0][:, m, s], scalar=gq[:, m:m + 1], op0=ALU.add)

            def score_max(n):
                wait_taken(dve, FIRST[f"U{n}"])
                dve.wait_ge(s_full, n + 1)
                r = uT[:, n % 2, C:C + 1]
                step(V.reduce_max(sm[:, 0, n:n + 1], psS, AX_X))
                step(V.tensor_tensor(sm[:, 1, n:n + 1], sm[:, 0, n:n + 1], r, ALU.add))
                V.tensor_tensor(sm[:, 2, n:n + 1], r, sm[:, 1, n:n + 1], ALU.subtract).then_inc(bias_ready, 1)

            def weigh_values(n):
                dve.wait_ge(s_exp, n + 1)
                step(V.reciprocal(sm[:, 4, n:n + 1], sm[:, 3, n:n + 1]))
                if n >= 2:
                    dve.wait_ge(sums_full, n - 1)
                step(V.tensor_scalar(u[0][:, n % 2, :], uT[:, n % 2, 0:C], sm[:, 4, n:n + 1], None, ALU.mult))
                V.scalar_tensor_tensor(out=u[1][:, n % 2, :], in0=uT[:, n % 2, 0:C], scalar=sm[:, 4, n:n + 1],
                                       in1=u[0][:, n % 2, :], op0=ALU.mult, op1=ALU.subtract).then_inc(u_ready, 1)

            def take_tokens(b):
                dve.wait_ge(sums_full, NT * (b + 1))
                for j in range(0, NT, 2):
                    V.tensor_tensor(t1[:, b, j:j + 2, :], psV[:, j:j + 2, :],
                                    bp_all[:, :].unsqueeze(1).to_broadcast([P, 2, C]), ALU.add).then_inc(sums_taken, 1)
                dve.wait_ge(sums_taken, (NT // 2) * (b + 1))

            def token_stats(b, part=range(NT), end=True):
                for j in part:
                    last = V.bn_stats(tst[:, j, :], t1[:, b, j, :])
                step(last)
                if not end:
                    return
                for j in range(NT):
                    last = V.bn_aggr(tmv[:, j, :], tst[:, j, :])
                step(last)
                V.tensor_scalar(trs[:, 0, :], tmv[:, :, 1], EPS_TOK, None, ALU.add).then_inc(var_ready, 1)

            def token_norm(b, dst, n, mark=None):
                dve.wait_ge(rstd_ready, n + 1)
                for j in range(NT):
                    last = V.tensor_scalar(dst[:, j, :], t1[:, b, j, :], tmv[:, j, 0:1], trs[:, 1, j:j + 1],
                                           ALU.subtract, ALU.mult)
                if mark is None:
                    step(last)
                else:
                    last.then_inc(mark, 1)

            def fold_tokens(b):
                V.tensor_tensor(xf32[:, 0:4, :], xn[:, 0:4, :], xn[:, 4:8, :], ALU.subtract)
                step(V.tensor_tensor(fold[b], xn[:, 0:4, :], xn[:, 4:8, :], ALU.add))
                V.tensor_tensor(xf32[:, 4:6, :], fold[b][:, 0:2, :], fold[b][:, 2:4, :], ALU.subtract)
                V.tensor_tensor(xf32[:, 6:8, :], fold[b][:, 0:2, :], fold[b][:, 2:4, :], ALU.add).then_inc(xf32_ready, 1)

            def xf_low(b):
                dve.wait_ge(xf_high, b + 1)
                V.tensor_tensor(xf[1], xf32, xf[0], ALU.subtract).then_inc(xf_ready, 1)

            def residual_bias(b):
                step(V.tensor_tensor(t1[:, b, :, :], t1[:, b, :, :], bo_all[:, :].unsqueeze(1).to_broadcast([P, NT, C]), ALU.add))

            def x_low(b, m):
                for k in range(2):
                    f = FIRST[f"D{b}_{m}"] + k
                    s = slice(k * 512, (k + 1) * 512)
                    low(f, xhat[1][:, m, s], bank(f), xhat[0][:, m, s])

            def cross_spectrum(b):
                wait_taken(dve, FIRST[f"Q{b}"] + 2 * NT - 1)
                for n, (qi, ki) in enumerate([(0, 0), (1, 1), (1, 0), (0, 1)]):
                    pr = prod[b][n % 2]
                    step(V.tensor_tensor(pr, qk[:, qi::2, 0:C], qk[:, ki::2, C:2 * C], ALU.mult))
                    last = V.tensor_reduce(cs[:, n, :], pr.rearrange("p a (h d) -> p (a h) d", d=DK), AX_X, ALU.add)
                step(last)
                rr, ii, ir, ri = (cs[:, n, :] for n in range(4))
                step(V.tensor_tensor(cs[:, 4, :], pair_mask, ii, ALU.mult))
                V.tensor_tensor(spec[:, 0, :], rr, cs[:, 4, :], ALU.add)
                V.tensor_tensor(cs[:, 5, :], ii, cs[:, 4, :], ALU.subtract)
                step(V.tensor_tensor(cs[:, 6, :], ir, ri, ALU.subtract))
                step(V.tensor_tensor(cs[:, 7, :], pair_mask, cs[:, 6, :], ALU.mult))
                V.tensor_tensor(spec[:, 1, :], cs[:, 7, :], cs[:, 5, :], ALU.add).then_inc(spec_ready, 1)

            def delays(b):
                hs = slice(0, HEADS)
                corr, left, weight, wfold = (t[hs, :] for t in dspace[b])
                fe, fo = FIRST[f"C{b}"], FIRST[f"C{b}"] + 1
                ev, ep = even32[b][hs, 0:2, :], even32[b][hs, 2:4, :]
                full(fe)
                step(V.tensor_copy(ev[:, 0, :], bank(fe)[hs, QUARTER:512]))
                V.tensor_tensor(ep[:, 0, :], ev[:, 0, :], bank(fe)[hs, 0:QUARTER], ALU.add)
                V.tensor_tensor(ep[:, 1, :], ev[:, 0, :], bank(fe)[hs, 0:QUARTER], ALU.subtract).then_inc(v_taken, 1)
                wait_taken(dve, fe)
                full(fo)
                V.tensor_tensor(corr[:, 0:HALF], ep.rearrange("p a b -> p (a b)"), bank(fo)[hs, :], ALU.add)
                V.tensor_tensor(corr[:, HALF:N], ep.rearrange("p a b -> p (a b)"), bank(fo)[hs, :], ALU.subtract).then_inc(v_taken, 1)
                wait_taken(dve, fo)
                step(V.max(top[:, 0:8], corr))
                V.tensor_scalar(top[:, 16:17], top[:, 0:1], -1.0 / (N * DK), None, ALU.mult).then_inc(peak_ready, 1)
                step(V.match_replace(left, top[:, 0:8], corr, -3.0e38))
                step(V.max(top[:, 8:16], left))
                dve.wait_ge(exp_ready, b + 1)
                step(V.scalar_tensor_tensor(out=left, in0=corr, scalar=top[:, TOPK - 1:TOPK], in1=weight, op0=ALU.is_ge, op1=ALU.mult,
                                            accum_out=top[:, 17:18]))
                step(V.reciprocal(top[:, 18:19], top[:, 17:18]))
                step(V.tensor_scalar(weight, left, top[:, 18:19], None, ALU.mult))
                w, s = weight, left[:, 0:HALF]
                V.tensor_tensor(wfold[:, 0:HALF], w[:, 0:HALF], w[:, HALF:N], ALU.subtract)
                step(V.tensor_tensor(s, w[:, 0:HALF], w[:, HALF:N], ALU.add))
                V.tensor_tensor(wfold[:, HALF:HALF + QUARTER], s[:, 0:QUARTER], s[:, QUARTER:HALF], ALU.subtract)
                V.tensor_tensor(wfold[:, HALF + QUARTER:N], s[:, 0:QUARTER], s[:, QUARTER:HALF], ALU.add).then_inc(wfold_ready, 1)

            def w_low(b):
                f = FIRST[f"T{b}"]
                low(f, wT[1][:, :], bank(f)[:, 0:NT * HEADS], wT[0][:, :])

            def apply_delays(b):
                f = FIRST[f"W{b}"]
                full(f)
                V.tensor_scalar(wh_raw[:, :], bank(f)[:, 0:NT * HEADS], SPEC_SCALE, None, ALU.mult).then_inc(v_taken, 1)
                wait_taken(dve, f)
                pairs = wh_raw[:, :].rearrange("p (a i h) -> p a i h", i=2, h=HEADS)
                m = pair_mask.rearrange("p (a h) -> p a h", h=HEADS)
                w = [wh[:, n, :].rearrange("p (a h) -> p a h", h=HEADS) for n in range(4)]
                V.tensor_tensor(w[2], m, pairs[:, :, 0, :], ALU.mult)
                step(V.tensor_tensor(w[0], m, pairs[:, :, 1, :], ALU.mult))
                step(V.tensor_tensor(w[1], pairs[:, :, 1, :], w[0], ALU.subtract))
                step(V.tensor_tensor(w[3], w[2], w[1], ALU.add))

                def wide(ap):
                    return ap.unsqueeze(3).to_broadcast([P, 4, HEADS, DK])

                def heads(ap):
                    return ap.rearrange("p a (h d) -> p a h d", d=DK)

                vr, vi = heads(val[b][:, 0::2, :]), heads(val[b][:, 1::2, :])
                yr, yi = heads(Y32[:, 0::2, :]), heads(Y32[:, 1::2, :])
                pr = [heads(p) for p in prod[b]]
                V.tensor_tensor(pr[0], vr, wide(pairs[:, :, 0, :]), ALU.mult)
                step(V.tensor_tensor(pr[1], vi, wide(w[0]), ALU.mult))
                step(V.tensor_tensor(yr, pr[0], pr[1], ALU.subtract))
                V.tensor_tensor(pr[0], vr, wide(w[0]), ALU.mult)
                step(V.tensor_tensor(pr[1], vi, wide(w[3]), ALU.mult))
                V.tensor_tensor(yi, pr[0], pr[1], ALU.add).then_inc(y_ready, 1)
                dve.wait_ge(y_high, b + 1)
                V.tensor_tensor(Y[1], Y32, Y[0], ALU.subtract).then_inc(y_low, 1)

            def inverse(b):
                for m in range(CC):
                    fe = FIRST[f"I{b}"] + 2 * m
                    fo = fe + 1
                    full(fe)
                    step(V.tensor_copy(ehalf[b][:, m, 0:QUARTER], bank(fe)[:, QUARTER:512]))
                    e0 = ehalf[b][:, m, 0:QUARTER]
                    V.tensor_tensor(ehalf[b][:, m, QUARTER:HALF], e0, bank(fe)[:, 0:QUARTER], ALU.add)
                    V.tensor_tensor(ehalf[b][:, m, HALF:HALF + QUARTER], e0, bank(fe)[:, 0:QUARTER], ALU.subtract).then_inc(v_taken, 1)
                    wait_taken(dve, fe)
                    full(fo)
                    ee = ehalf[b][:, m, QUARTER:HALF + QUARTER]
                    V.tensor_tensor(cx32[:, m, 0:HALF], ee, bank(fo), ALU.add)
                    V.tensor_tensor(cx32[:, m, HALF:N], ee, bank(fo), ALU.subtract).then_inc(v_taken, 1)
                for m in range(CC):
                    dve.wait_ge(cx_high, b * CC + m + 1)
                    V.tensor_tensor(cx[1][:, m, :], cx32[:, m, :], cx[0][:, m, :], ALU.subtract).then_inc(cx_low, 1)

            def add_attention(b):
                for j in range(NT):
                    f = FIRST[f"O{b}"] + j
                    full(f)
                    V.scalar_tensor_tensor(out=t1[:, b, j, :], in0=bank(f)[:, 0:C], scalar=1.0 / (N * SPEC_SCALE),
                                           in1=t1[:, b, j, :], op0=ALU.mult, op1=ALU.add).then_inc(v_taken, 1)
                wait_taken(dve, f)

            def gate_scores(b):
                f = FIRST[f"gate{b}"]
                full(f)
                js = slice(b * NT, (b + 1) * NT)
                V.tensor_tensor(sc[:, js, :], bank(f)[:, 0:NT * E].rearrange("p (j e) -> p j e", e=E),
                                bg_all[:, :].unsqueeze(1).to_broadcast([P, NT, E]), ALU.add).then_inc(v_taken, 1)
                wait_taken(dve, f)
                for j in range(b * NT, (b + 1) * NT):
                    last = V.max(mx[:, j, :], sc[:, j, :])
                step(last)
                for j in range(b * NT, (b + 1) * NT):
                    last = V.max_index(gidx[:, j, :], mx[:, j, :], sc[:, j, :])
                step(last)

            def by_tile(ap):
                return ap.rearrange("p (j e) -> p j e", e=E)

            def by_expert(ap):
                return ap.rearrange("p (e j) -> p e j", e=E)

            def route():
                chosen, count, upto, off, prods = (rt[:, k, :] for k in range(5))
                step(V.tensor_copy(chosen, gidx[:, :, :].rearrange("p j e -> p (j e)")))
                V.tensor_tensor(gt[:, 0, :], mx[:, :, 1], mx[:, :, 0], ALU.subtract).then_inc(gate_ready, 1)
                dve.wait_ge(ffn_in, 48)
                for c in range(2):
                    last = V.tensor_tensor(by_tile(oh[:, c, :]), iota8.unsqueeze(1).to_broadcast([P, TT, E]),
                                           by_tile(chosen)[:, :, c].unsqueeze(2).to_broadcast([P, TT, E]), ALU.is_equal)
                step(last)
                V.tensor_tensor(oh[:, 2, :], oh[:, 0, :], oh[:, 1, :], ALU.add).then_inc(choice_ready, 1)
                f = FIRST["rank"]
                full(f)
                step(V.tensor_copy(by_expert(count), bank(f)[:, TT * E:2 * TT * E].rearrange("p (j e) -> p e j", e=E)))
                step(V.tensor_tensor_scan(upto, scan_mask, count, 0.0, ALU.mult, ALU.add))
                V.tensor_tensor(off, upto, count, ALU.subtract)
                step(V.tensor_tensor(by_expert(prods), by_expert(upto)[:, :, TT - 1].unsqueeze(2).to_broadcast([P, E, TT]),
                                     thresholds.unsqueeze(1).to_broadcast([P, E, TT]), ALU.is_gt))
                step(V.tensor_reduce(cum[:, 0, :], by_expert(prods), AX_X, ALU.add))
                step(V.tensor_tensor_scan(cum[:, 1, :], scan_mask[:, 1:1 + E], cum[:, 0, :], 0.0, ALU.mult, ALU.add))
                step(V.tensor_tensor(cum[:, 2, :], cum[:, 1, :], cum[:, 0, :], ALU.subtract))
                step(V.scalar_tensor_tensor(out=by_expert(off), in0=cum[:, 2, :].unsqueeze(2).to_broadcast([P, E, TT]), scalar=float(P),
                                            in1=by_expert(off), op0=ALU.mult, op1=ALU.add))
                step(V.tensor_tensor(by_tile(upto), off.rearrange("p (e j) -> p j e", e=E), by_tile(bank(f)[:, 0:TT * E]), ALU.add))
                for c in range(2):
                    last = V.tensor_tensor(oh32[:, c, :], oh[:, c, :], upto, ALU.mult)
                last.then_inc(v_taken, 1)
                wait_taken(dve, f)
                step(V.tensor_reduce(slot[:, 0, :], oh32.rearrange("p c (j e) -> p (c j) e", e=E), AX_X, ALU.add))
                step(V.tensor_copy(slot_u[:, 0, :], slot[:, 0, :]))
                V.tensor_scalar(slot_u[:, 1, :], slot_u[:, 0, :], P - 1, None, ALU.bitwise_and)
                step(V.tensor_scalar(slot_u[:, 2, :], slot_u[:, 0, :], 7, None, ALU.logical_shift_right))
                step(V.tensor_copy(slot[:, 1:3, :], slot_u[:, 1:3, :]))
                t_hot = onehot_t[:, :, 0:TILES]
                step(V.tensor_tensor(onehot_t[:, :, TILES:], iota_tile.unsqueeze(1).to_broadcast([P, 2 * TT, TILES]),
                                     slot[:, 2, :].unsqueeze(2).to_broadcast([P, 2 * TT, TILES]), ALU.is_equal))
                step(V.tensor_tensor(t_hot, onehot_t[:, :, TILES:], token_id.unsqueeze(2).to_broadcast([P, 2 * TT, TILES]), ALU.mult))
                step(V.tensor_scalar(onehot_t[:, TT:, TILES:], onehot_t[:, TT:, TILES:], 2.0, None, ALU.mult))
                for q in range(2 * TT):
                    last = V.tensor_scalar(onehot_p[:, q, :], iota128, slot[:, 1, q:q + 1], None, ALU.is_equal)
                    if q % 8 == 7:
                        last.then_inc(perm_part, 1)
                after = wcmp[0:1, 0:TILES * E].rearrange("p (s e) -> p s e", e=E)
                step(V.tensor_tensor(after, iota_tile[0:1, :].unsqueeze(2).to_broadcast([1, TILES, E]),
                                     cum[0:1, 1, :].unsqueeze(1).to_broadcast([1, TILES, E]), ALU.is_ge))
                step(V.tensor_reduce(pf[0:1, 0, :], after, AX_X, ALU.add))
                step(V.tensor_scalar(pf[0:1, 1, :], pf[0:1, 0, :], -1.0, float(E - 1), ALU.mult, ALU.add))
                step(V.tensor_scalar(pf[0:1, 2, :], pf[0:1, 1, :], 0.0, None, ALU.max))
                V.tensor_copy(where[:, :], pf[0:1, 2, :]).then_inc(where_ready, 1)
                f = FIRST["perm"]
                full(f)
                V.tensor_copy(pf[:, 0, :], bank(f)[:, 0:TILES])
                step(V.tensor_copy(pf[:, 1, :], bank(f)[:, TILES:2 * TILES]))
                V.tensor_copy(idx[:, 0, :], pf[:, 0, :])
                V.tensor_scalar(pf[:, 2, :], pf[:, 1, :], 0.0, None, ALU.is_equal)
                step(V.scalar_tensor_tensor(out=pf[:, 3, :], in0=pf[:, 1, :], scalar=float(T), in1=pf[:, 0, :], op0=ALU.mult, op1=ALU.add))
                step(V.tensor_tensor(pf[:, 4, :], pf[:, 2, :], spare_row, ALU.mult))
                step(V.scalar_tensor_tensor(out=pf[:, 2, :], in0=pf[:, 3, :], scalar=float(T), in1=pf[:, 4, :], op0=ALU.subtract, op1=ALU.add))
                V.tensor_copy(idx[:, 1, :], pf[:, 2, :]).then_inc(idx_ready, 1)
                dve.wait_ge(gexp_ready, 1)
                step(V.tensor_scalar(gt[:, 3, :], gt[:, 1, :], 1.0, None, ALU.add))
                step(V.reciprocal(gt[:, 2, :], gt[:, 3, :]))
                step(V.tensor_tensor(gt[:, 3, :], gt[:, 1, :], gt[:, 2, :], ALU.mult))

            def take_gathered(s):
                dve.wait_ge(x_turned, s + 1)
                if s >= 2:
                    dve.wait_ge(hid_full, s - 1)
                V.tensor_copy(xT[:, s % 2, :], psx[s % 2]).then_inc(x_taken, 1)

            def hidden_low(s):
                dve.wait_ge(hid_high, s + 1)
                if s >= 3:
                    dve.wait_ge(y_full, s - 2)
                V.tensor_tensor(hh[1][:, s % 3, :], hf[:, s % 3, :], hh[0][:, s % 3, :], ALU.subtract).then_inc(hid_low, 1)

            def take_result(s):
                e = dve.value_load(where[0:1, s:s + 1], min_val=0, max_val=E - 1)
                dve.wait_ge(y_full, s + 1)
                if s >= 4:
                    dve.wait_ge(scattered[s % 4], 16 * (s // 4))
                V.tensor_tensor(ysb[:, s % 4, :], psy[s % 2], b2_all[:, bass.ds(e, 1), :].rearrange("p a c -> p (a c)"), ALU.add).then_inc(y_taken, 1)

            def combine():
                for q in range(8):
                    dve.wait_ge(y_in[q], 32)
                    for c in range(2):
                        for j in (2 * q, 2 * q + 1):
                            last = V.scalar_tensor_tensor(out=tt[:, j, :], in0=ygot[:, c, j, :], scalar=gt[:, 2 + c, j:j + 1],
                                                          in1=tt[:, j, :], op0=ALU.mult, op1=ALU.add)
                        if c == 0:
                            step(last)
                    last.then_inc(combined, 1)

            z_low(0, 0)
            z_low(0, 1)
            for n in range(B * NT + 1):
                if n >= 1:
                    weigh_values(n - 1)
                if n < B * NT:
                    score_max(n)
                if n == 0:
                    channel_stats(1)
                    group_mean(1)
                    group_affine(1)
                if 1 <= n <= 4:
                    attn_weight_low(n - 1)
                if n in (5, 6):
                    z_low(1, n - 5)
                if n == NT:
                    dve.wait_ge(late_in, 16 * 6)
                    take_tokens(0)
                if n == 9:
                    token_stats(0)
                if n == 10:
                    token_norm(0, xn, 0)
                if n == 11:
                    fold_tokens(0)
                if n == 12:
                    xf_low(0)
                if n == 13:
                    residual_bias(0)
                if n in (14, 15):
                    x_low(0, n - 14)
            take_tokens(1)
            token_stats(1)
            token_norm(1, xn, 1)
            dve.wait_ge(filled, FIRST["Q0"] + 2 * NT)
            fold_tokens(1)
            xf_low(1)
            residual_bias(1)
            cross_spectrum(0)
            x_low(1, 0)
            x_low(1, 1)
            delays(0)
            w_low(0)
            apply_delays(0)
            cross_spectrum(1)
            inverse(0)
            delays(1)
            add_attention(0)
            w_low(1)
            apply_delays(1)
            token_stats(0)
            token_norm(0, yn, 2, yn_ready)
            inverse(1)
            gate_scores(0)
            add_attention(1)
            token_stats(1)
            wait_taken(dve, FIRST["YT0"] + 3)
            dve.wait_ge(row_low, 1)
            token_norm(1, yn, 3, yn_ready)
            gate_scores(1)
            route()
            dve.wait_ge(b2_in, 16 * E)
            for i in range(TILES + 3):
                if i < TILES:
                    take_gathered(i)
                if 0 <= i - 2 < TILES:
                    hidden_low(i - 2)
                if 0 <= i - 3 < TILES:
                    take_result(i - 3)
            combine()

        @block.tensor
        def _(pe):
            at = [0]

            def fill(name):
                f = at[0]
                at[0] += 1
                assert RING[f][2] == name
                if f < PHASE2:
                    if f >= 2:
                        wait_taken(pe, f - 2)
                elif f < PHASE2 + 2:
                    wait_taken(pe, f - 2)
                elif f < PHASE2 + 4:
                    pe.wait_ge(s_exp, B * NT)
                elif f < PHASE2 + 8:
                    pe.wait_ge(sums_taken, (NT // 2) * B)
                else:
                    wait_taken(pe, f - 8)
                return bank(f)

            def product(dst, parts, more=()):
                seq = []
                for (lh, ll), (rh, rl) in parts:
                    seq += [(lh, rh), (lh, rl), (ll, rh)]
                seq += list(more)
                for n, (lhs, rhs) in enumerate(seq):
                    last = PE.matmul(dst, lhs, rhs, start=(n == 0), stop=(n == len(seq) - 1))
                return last

            def hl(pair, *ix):
                return tuple(t[ix] for t in pair)

            S = slice(None)

            def groups(b):
                q = slice(b * CC, (b + 1) * CC)
                pe.wait_ge(mean_ready, b + 1)
                PE.matmul(fill(f"gn{b}")[:, 0:CC], blockdiag, mv[:, q, 0], start=True, stop=True).then_inc(filled, 1)
                pe.wait_ge(spread_ready, b + 1)
                PE.matmul(fill(f"gn{b}")[:, 0:CC], blockdiag, gn[:, 4, q], start=True, stop=True).then_inc(filled, 1)

            def attn_weight(w):
                if w == 0:
                    pe.wait_ge(aw_in, 64)
                dst = fill(f"attnW{w}")
                for m in range(CC):
                    for o in range(CC):
                        last = PE.transpose(dst[:, m * C + o * P:m * C + (o + 1) * P], raw(4 + w, o)[:, m * P:(m + 1) * P], ident)
                last.then_inc(filled, 1)

            pe.wait_ge(const_in, 16)
            groups(0)
            pe.wait_ge(w_in, 64)
            dst = fill("wpT")
            for m in range(CC):
                for o in range(CC):
                    last = PE.transpose(dst[:, m * C + o * P:m * C + (o + 1) * P], raw(WP, o)[:, m * P:(m + 1) * P], ident)
            last.then_inc(filled, 1)
            dst = fill("A")
            for m in range(CC):
                for o in range(CC):
                    last = PE.matmul(dst[:, m * C:(m + 1) * C], raw(WQ, o)[:, m * P:(m + 1) * P], raw(WK, o), start=(o == 0), stop=(o == CC - 1))
            last.then_inc(filled, 1)
            wait_taken(pe, FIRST["wpT"])
            dst = fill("UW")
            for m in range(CC):
                for o in range(CC):
                    last = PE.matmul(dst[:, m * C:(m + 1) * C], raw(WV, o)[:, m * P:(m + 1) * P], wpT[:, o, :], start=(o == 0), stop=(o == CC - 1))
            last.then_inc(filled, 1)
            pe.wait_ge(small_in, 16 * 5)
            dst = fill("small")
            for col, w, c in ((0, WK, BQ), (2, WQ, BK)):
                for m in range(CC):
                    for o in range(CC):
                        PE.matmul(dst[:, col + m:col + m + 1], raw(w, o)[:, m * P:(m + 1) * P], cols[:, c, o:o + 1], start=(o == 0), stop=(o == CC - 1))
            for o in range(CC):
                PE.matmul(dst[0:1, 4:5], cols[:, BQ, o:o + 1], cols[:, BK, o:o + 1], start=(o == 0), stop=(o == CC - 1))
            for o in range(CC):
                last = PE.matmul(dst[0:1, 8:8 + C], cols[:, BV, o:o + 1], wpT[:, o, :], start=(o == 0), stop=(o == CC - 1))
            last.then_inc(filled, 1)

            def project_queries(b, m):
                pe.wait_ge(h1_low if b else h0_low, CC)
                if b == 0:
                    wait_taken(pe, FIRST["small"])
                for half in range(2):
                    s = slice(half * 512, (half + 1) * 512)
                    product(fill(f"G{b}_{m}"), [(hl(A, S, k, slice(m * P, (m + 1) * P)), hl(h[b], S, k, s)) for k in range(CC)]).then_inc(filled, 1)

            def project_values(n):
                b, i = n // NT, n % NT
                pe.wait_ge(rows_ready, 2)
                product(fill(f"U{n}")[:, 0:C + 1], [(hl(h[b], S, k, slice(i * P, (i + 1) * P)), hl(UW, S, k, S)) for k in range(CC)],
                        [(ones[:, :], t[:, :]) for t in ub]).then_inc(filled, 1)

            def scores(n):
                b, i = n // NT, n % NT
                if n >= 1:
                    pe.wait_ge(s_exp, n)
                if i == 0:
                    wait_taken(pe, FIRST[f"G{b}_1"] + 1)
                for half in range(2):
                    last = product(psS[:, half * 512:(half + 1) * 512],
                                   [(hl(z[b], S, k, slice(i * P, (i + 1) * P)), hl(h[b], S, k, slice(half * 512, (half + 1) * 512))) for k in range(CC)])
                last.then_inc(s_full, 1)

            def sum_values(n):
                b, i = n // NT, n % NT
                if i == 0:
                    if b:
                        pe.wait_ge(sums_taken, (NT // 2) * b)
                    for j in range(NT):
                        for k in range(CC):
                            PE.matmul(psV[:, j, k * P:(k + 1) * P], x_sb[b][:, k, j * P:(j + 1) * P], ident, is_transpose=True,
                                      start=(j % 2 == 0 and k == 0), stop=False, skip_group_check=True)
                pe.wait_ge(p_low, n + 1)
                pe.wait_ge(u_ready, n + 1)
                for j in range(NT):
                    for l, r in ((0, 0), (0, 1), (1, 0)):
                        last = PE.matmul(psV[:, j, :], Pt[l][:, n % 2, j * P:(j + 1) * P], u[r][:, n % 2, :],
                                         start=False, stop=(i == NT - 1), skip_group_check=True)
                last.then_inc(sums_full, 1)

            def spectra(b, m):
                pe.wait_ge(fwd_in, 32)
                pe.wait_ge(xf_ready, b + 1)
                cs_ = slice(m * P, (m + 1) * P)
                product(fill(f"D{b}_{m}"), [(hl(xf, S, k, cs_), tuple(odd(t, k) for t in fwd)) for k in range(4)]).then_inc(filled, 1)
                dst = fill(f"D{b}_{m}")
                for which in range(2):
                    last = product(dst[:, which * QUARTER:(which + 1) * QUARTER],
                                   [(hl(xf, S, 4 + 2 * which + k, cs_), tuple(even(t, which, k) for t in fwd)) for k in range(2)])
                last.then_inc(filled, 1)

            def project(b):
                pe.wait_ge(late_in, 16 * 6)
                wait_taken(pe, FIRST[f"D{b}_1"] + 1)
                for j in range(NT):
                    for lo, n in ((0, 512), (512, 256)):
                        more = [(dc_row[:, :], qkv_row[:, lo:lo + n])] if j == 6 else []
                        product(fill(f"Q{b}")[:, 0:n], [(hl(xhat, S, k, slice(j * P, (j + 1) * P)), hl(qkvW, S, k, slice(lo, lo + n))) for k in range(CC)],
                                more).then_inc(filled, 1)

            def correlate(b):
                pe.wait_ge(inv32_in, 16)
                pe.wait_ge(spec_ready, b + 1)

                def sp_(chunk):
                    return spec[:, chunk % 2, (chunk // 2) * HEADS:(chunk // 2 + 1) * HEADS]

                dst = fill(f"C{b}")
                for which in range(2):
                    for k in range(2):
                        last = PE.matmul(dst[0:HEADS, which * QUARTER:(which + 1) * QUARTER], sp_(4 + 2 * which + k),
                                         even(inv32, which, k), start=(k == 0), stop=(k == 1))
                last.then_inc(filled, 1)
                dst = fill(f"C{b}")
                for k in range(4):
                    last = PE.matmul(dst[0:HEADS, :], sp_(k), odd(inv32, k), start=(k == 0), stop=(k == 3))
                last.then_inc(filled, 1)

            def weight_spectrum(b):
                pe.wait_ge(wfold_ready, b + 1)
                dst = fill(f"T{b}")
                for j in range(NT):
                    last = PE.transpose(dst[:, j * HEADS:(j + 1) * HEADS], dspace[b][3][0:HEADS, j * P:(j + 1) * P], ident[0:HEADS, 0:HEADS])
                last.then_inc(filled, 1)
                wait_taken(pe, FIRST[f"T{b}"])
                dst = fill(f"W{b}")
                for j in range(NT):
                    if j < 4:
                        ks = [(k, tuple(odd(t, k)[:, j * P:(j + 1) * P] for t in fwd)) for k in range(4)]
                    else:
                        which = (j - 4) // 2
                        ks = [(4 + 2 * which + k, tuple(even(t, which, k)[:, (j % 2) * P:(j % 2 + 1) * P] for t in fwd)) for k in range(2)]
                    last = product(dst[:, j * HEADS:(j + 1) * HEADS],
                                   [(tab, hl(wT, S, slice(k * HEADS, (k + 1) * HEADS))) for k, tab in ks])
                last.then_inc(filled, 1)

            def inverse(b):
                pe.wait_ge(inv_in, 32)
                pe.wait_ge(y_low, b + 1)
                for m in range(CC):
                    cs_ = slice(m * P, (m + 1) * P)
                    dst = fill(f"I{b}")
                    for which in range(2):
                        last = product(dst[:, which * QUARTER:(which + 1) * QUARTER],
                                       [(hl(Y, S, 4 + 2 * which + k, cs_), tuple(even(t, which, k) for t in inv)) for k in range(2)])
                    last.then_inc(filled, 1)
                    product(fill(f"I{b}"), [(hl(Y, S, k, cs_), tuple(odd(t, k) for t in inv)) for k in range(4)]).then_inc(filled, 1)

            def out_project(b):
                pe.wait_ge(cx_low, CC * (b + 1))
                for j in range(NT):
                    product(fill(f"O{b}")[:, 0:C], [(hl(cx, S, k, slice(j * P, (j + 1) * P)), hl(woW, S, k, S)) for k in range(CC)]).then_inc(filled, 1)

            def turn_tokens(b):
                pe.wait_ge(yn_ready, b + 1)
                for k in range(4):
                    dst = fill(f"YT{b}")
                    for m in range(CC):
                        for a in range(2):
                            last = PE.transpose(dst[:, m * 2 * P + a * P:m * 2 * P + (a + 1) * P], yn[:, 2 * k + a, m * P:(m + 1) * P], ident)
                    last.then_inc(filled, 1)

            def gate(b):
                pe.wait_ge(ffn_in, 48)
                wait_taken(pe, FIRST[f"YT{b}"] + 3)
                dst = fill(f"gate{b}")
                for j in range(NT):
                    for k in range(CC):
                        last = PE.matmul(dst[:, j * E:(j + 1) * E], ynT[:, k, j * P:(j + 1) * P], wg_sb[:, k, :], start=(k == 0), stop=(k == CC - 1))
                last.then_inc(filled, 1)

            def turn_gathered(s):
                pe.wait_ge(gathered[s % 6], 16 * (s // 6 + 1))
                if s >= 2:
                    pe.wait_ge(x_taken, s - 1)
                for k in range(4):
                    last = PE.matmul(psx[s % 2][:, k * P:(k + 1) * P], gx[:, s % 6, k * P:(k + 1) * P], ident16, start=True, stop=True)
                last.then_inc(x_turned, 1)

            def hidden(s):
                e = pe.value_load(where[0:1, s:s + 1], min_val=0, max_val=E - 1)
                at_expert[s % 4] = e
                if s in (0, 10, 20, 30):
                    pe.wait_ge(we_low, 2 * E)
                pe.wait_ge(x_taken, s + 1)
                if s >= 2:
                    pe.wait_ge(gelu_done, s - 1)
                for m in range(HC):
                    for n, (l, r, k) in enumerate([(l, r, k) for k in range(CC) for l, r in ((0, 0), (0, 1), (1, 0))]):
                        o = l * CC * H + k * H + m * P
                        last = PE.matmul(psh[s % 2][:, m * P:(m + 1) * P], experts[:, bass.ds(e, 1), o:o + P].rearrange("p a c -> p (a c)"),
                                         xT[:, s % 2, (r * CC + k) * P:(r * CC + k + 1) * P], start=(n == 0), stop=(n == 3 * CC - 1))
                last.then_inc(hid_full, 1)

            def results(s):
                e = at_expert[s % 4]
                pe.wait_ge(hid_low, s + 1)
                if s >= 2:
                    pe.wait_ge(y_taken, s - 1)
                for n, (l, r, m) in enumerate([(l, r, m) for m in range(HC) for l, r in ((0, 0), (0, 1), (1, 0))]):
                    o = (2 + r) * CC * H + m * C
                    last = PE.matmul(psy[s % 2], hh[l][:, s % 3, m * P:(m + 1) * P], experts[:, bass.ds(e, 1), o:o + C].rearrange("p a c -> p (a c)"),
                                     start=(n == 0), stop=(n == 3 * HC - 1))
                last.then_inc(y_full, 1)

            at_expert = [None] * 4
            project_queries(0, 0)
            project_queries(0, 1)
            for n in range(B * NT):
                project_values(n)
                scores(n)
                if n == 0:
                    groups(1)
                if 1 <= n <= 4:
                    attn_weight(n - 1)
                if n in (5, 6):
                    project_queries(1, n - 5)
                if n in (14, 15):
                    spectra(0, n - 14)
                if n >= 1:
                    sum_values(n - 1)
            sum_values(B * NT - 1)
            project(0)
            spectra(1, 0)
            spectra(1, 1)
            correlate(0)
            project(1)
            weight_spectrum(0)
            inverse(0)
            correlate(1)
            out_project(0)
            weight_spectrum(1)
            inverse(1)
            turn_tokens(0)
            gate(0)
            out_project(1)
            turn_tokens(1)
            gate(1)
            pe.wait_ge(choice_ready, 1)
            dst = fill("rank")
            PE.matmul(dst[:, 0:TT * E], before, oh[:, 2, :], start=True, stop=True)
            PE.matmul(dst[:, TT * E:2 * TT * E], all_ones, oh[:, 2, :], start=True, stop=True).then_inc(filled, 1)
            dst = fill("perm")
            for q in range(2 * TT):
                if q % 8 == 0:
                    pe.wait_ge(perm_part, q // 8 + 1)
                last = PE.matmul(dst[:, 0:2 * TILES], onehot_p[:, q, :], onehot_t[:, q, :], start=(q == 0), stop=(q == 2 * TT - 1))
            last.then_inc(filled, 1)
            wait_taken(pe, FIRST["gate1"])
            pe.wait_ge(idx_ready, 1)
            pe.wait_ge(where_ready, 1)
            for i in range(TILES + 3):
                if i < TILES:
                    turn_gathered(i)
                if 0 <= i - 1 < TILES:
                    hidden(i - 1)
                if 0 <= i - 3 < TILES:
                    results(i - 3)
            for q in range(8):
                pe.wait_ge(combined, q + 1)
                if q >= 2:
                    pe.wait_ge(out_taken, q - 1)
                for a in range(2):
                    for m in range(CC):
                        last = PE.transpose(ps[:, 6 + q % 2, m * 2 * P + a * P:m * 2 * P + (a + 1) * P], tt[:, 2 * q + a, m * P:(m + 1) * P], ident)
                last.then_inc(out_turned, 1)


_INS = ['x', 'L0_conv_norm_w', 'L0_conv_norm_b', 'L0_conv_wq', 'L0_conv_bq', 'L0_conv_wk', 'L0_conv_bk',
        'L0_conv_wv', 'L0_conv_bv', 'L0_conv_wp', 'L0_conv_bp', 'L1_attn_Wq', 'L1_attn_bq', 'L1_attn_Wk',
        'L1_attn_bk', 'L1_attn_Wv', 'L1_attn_bv', 'L1_attn_Wo', 'L1_attn_bo', 'L1_ffn_Wg', 'L1_ffn_bg',
        'L1_ffn_W1', 'L1_ffn_b1', 'L1_ffn_W2', 'L1_ffn_b2']


def kernel(**inputs):
    import numpy as _np
    import concourse.bacc as _bacc
    from concourse import mybir as _mybir
    from concourse.bass_utils import run_bass_kernel_spmd as _run

    nc = _bacc.Bacc("TRN2", target_bir_lowering=False, num_devices=1)
    arrays, tensors = {}, {}
    given = {name: _np.ascontiguousarray(inputs[name]) for name in _INS}
    for name, a in {**given, **dft_constants()}.items():
        arrays[f"in_{name}_dram"] = a
        tensors[name] = nc.dram_tensor(f"in_{name}_dram", a.shape, _mybir.dt.from_np(a.dtype), kind="ExternalInput").ap()
    out = nc.dram_tensor("out_0_dram", (B, C, 32, 32), _mybir.dt.float32, kind="ExternalOutput").ap()
    conv_attn_moe_kernel(nc, tensors, out)
    r = _run(nc, [arrays], core_ids=[0])
    return r.results[0]["out_0_dram"]
```

```python
from contextlib import ExitStack

import numpy as np

import concourse.bass as bass
from concourse import mybir

ALU = mybir.AluOpType
ACT = mybir.ActivationFunctionType
AX_X = mybir.AxisListType.X
F32 = mybir.dt.float32
F16 = mybir.dt.float16
U32 = mybir.dt.uint32

P = 128
B = 2
C = 256
CC = C // P
N = 1024
NT = N // P
HALF = N // 2
QUARTER = N // 4
HEADS = 8
DK = C // HEADS
TOPK = int(2 * np.log(N))
GROUP = C // 32
E = 8
H = 384
HC = H // P
T = B * N
TT = T // P
TILES = 2 * TT + E - 1
EPS_CONV = 1e-6
EPS_TOK = 1e-5
ATT_SCALE = C ** -0.5
SPEC_SCALE = 1.0 / 32
ODD, EVEN = 4 * HALF, 2 * QUARTER
TAB = ODD + 2 * EVEN


def split16(a):
    hi = a.astype(np.float16)
    return hi, (a - hi.astype(np.float64)).astype(np.float16)


def dft_constants():
    k = np.arange(P)

    def rows(freq, length, last):
        t = np.arange(length)
        ang = 2 * np.pi * np.outer(freq, t) / N
        re, im = np.cos(ang), -np.sin(ang)
        weight = np.full(len(freq), 2.0)
        wim = weight.copy()
        if last:
            im[0] = np.cos(np.pi * t)
            weight[0] = wim[0] = 1.0
        return [re, im], [re * weight[:, None], im * wim[:, None]]

    o0, io0 = rows(1 + 2 * k, HALF, False)
    o1, io1 = rows(1 + 2 * (k + P), HALF, False)
    e, ie = rows(2 + 4 * k, QUARTER, False)
    z, iz = rows(4 * k, QUARTER, True)

    def forward(parts, length):
        m = np.concatenate(parts, 0).T
        return m.reshape(length // P, P, -1).transpose(1, 0, 2).reshape(P, -1)

    def inverse(parts):
        return np.stack(parts, 1).reshape(P, -1)

    fwd = np.concatenate([forward(o0 + o1, HALF), forward(e, QUARTER), forward(z, QUARTER)], 1)
    inv = np.concatenate([inverse(io0 + io1), inverse(ie), inverse(iz)], 1)
    pair_mask = np.ones((P, 4 * HEADS), np.float32)
    pair_mask[0, 3 * HEADS:] = 0.0
    p = np.arange(P)
    consts = np.concatenate([
        np.eye(P), (p[:, None] // GROUP == p[None, :] // GROUP) / float(GROUP),
        pair_mask, np.tile(np.arange(E), (P, 1)),
    ], 1).astype(np.float32)
    tile = np.arange(TILES)
    route = np.zeros((P, 2 * TILES + TT + E * TT), np.float32)
    route[:, 0:TILES] = tile
    route[:, TILES:2 * TILES] = 3 * T + P * tile[None, :] + p[:, None]
    route[:, 2 * TILES:2 * TILES + TT] = P * np.arange(TT)
    route[:, 2 * TILES + TT:] = np.tile(np.arange(TT) > 0, E)
    token = P * np.arange(TT)[None, :] + p[:, None]
    const16 = np.concatenate([np.eye(P), p[:, None] < p[None, :], np.ones((P, P)), np.tile(p, (P, 1)), token, token], 1)
    return {
        "const_f16": const16.astype(np.float16), "route_f32": route,
        "const_f32": consts, "inv_f32": inv.astype(np.float32),
        "fwd_hi": split16(fwd)[0], "fwd_lo": split16(fwd)[1],
        "inv_hi": split16(inv)[0], "inv_lo": split16(inv)[1],
    }


def conv_attn_moe_kernel(nc, g, out):
    with ExitStack() as ctx:
        def sb(name, shape, dt=F32):
            return ctx.enter_context(nc.sbuf_tensor(name, shape, dt))

        def sem(name):
            return ctx.enter_context(nc.semaphore(name))

        def view(region, at_kb, dims, dt):
            size = int(np.prod(dims)) * (2 if dt == F32 else 1)
            flat = region[:, int(at_kb * 512):int(at_kb * 512) + size]
            if dt == F32:
                flat = flat.bitcast(F32)
            names = "abc"[:len(dims)]
            return flat.rearrange(f"p ({' '.join(names)}) -> p {' '.join(names)}", **dict(zip(names[1:], dims[1:]))) \
                if len(dims) > 1 else flat

        ps = ctx.enter_context(nc.psum_tensor("ps", [P, 8, 512], F32))
        psS = ps[:, 0:2, :].rearrange("p a n -> p (a n)")
        psV = ps[:, 2:6, :].rearrange("p a n -> p (a n)").rearrange("p (j c) -> p j c", c=C)
        RING0 = [0, 1, 2, 3, 4, 5, 6, 7, 6, 7]
        RING1, RING2 = [6, 7], [6, 7, 0, 1, 2, 3, 4, 5]

        const = sb("const", [P, 2 * P + 4 * HEADS + E])
        where = sb("where_sb", [1, TILES + 1], U32)
        ident, blockdiag = const[:, 0:P], const[:, P:2 * P]
        pair_mask = const[:, 2 * P:2 * P + 4 * HEADS]
        iota8 = const[:, 2 * P + 4 * HEADS:]
        fwd = [sb("fwd_hi_sb", [P, TAB], F16), sb("fwd_lo_sb", [P, TAB], F16)]
        ones = sb("ones", [1, P], F16)
        dc_row = sb("dc_row", [1, P])
        half_neg = sb("half_neg", [P, NT])

        def odd(tab, k):
            return tab[:, 512 * k:512 * (k + 1)]

        def even(tab, which, k):
            o = ODD + which * EVEN + QUARTER * k
            return tab[:, o:o + QUARTER]

        late = sb("late", [P, 12 * 1024], F16)
        wraw = view(late, 0, [8, CC * C], F32)

        def raw(which, chunk):
            return wraw[:, which, chunk * C:(chunk + 1) * C]

        WQ, WK, WV, WP = range(4)
        prep = sb("prep", [P, 3 * 1024 + 256], F16)
        wpT = view(prep, 0, [CC, C], F32)
        A = [view(prep, 2 + i, [CC, C], F16) for i in range(2)]
        UW = [view(prep, 4 + 1.25 * i, [CC, C + 1], F16) for i in range(2)]
        gq = sb("gq", [P, CC])
        ub = [sb(f"ub_{i}", [1, C + 1], F16) for i in "hl"]
        qkvW = [sb(f"qkvW_{i}", [P, CC, 3 * C], F16) for i in "hl"]
        woW = [sb(f"woW_{i}", [P, CC, C], F16) for i in "hl"]
        cols = sb("cols", [P, 5, CC])
        NW, NB, BQ, BK, BV = range(5)
        bp_all = sb("bp_all", [P, C])
        bo_all = sb("bo_all", [P, C])
        qkv_row = sb("qkv_row", [1, 3 * C])
        bg_all = sb("bg_all", [P, E])

        l0 = sb("l0", [P, 24 * 1024], F16)
        x_sb = [view(l0, 24 * b, [CC, N], F32) for b in range(B)]
        h = [[view(l0, 24 * b + 8 + 4 * i, [CC, N], F16) for i in range(2)] for b in range(B)]
        z = [[view(l0, 24 * b + 16 + 4 * i, [CC, N], F16) for i in range(2)] for b in range(B)]
        bn = sb("bn", [P, B * CC, 2, 6])
        mv = sb("mv", [P, B * CC, 2])
        gn = sb("gn", [P, 8, B * CC])
        inv32 = view(l0, 24, [TAB], F32)
        inv = [sb("inv_hi_sb", [P, TAB], F16), sb("inv_lo_sb", [P, TAB], F16)]
        tiles = sb("tiles", [P, 8 * 1024], F16)
        prob = view(tiles, 0, [2, N], F32)
        Pt = [view(tiles, 8 + 4 * i, [2, N], F16) for i in range(2)]
        uT = sb("uT", [P, 2, C + 1])
        u = [sb(f"u_{i}", [P, 2, C], F16) for i in "hl"]
        sm = sb("sm", [P, 5, B * NT])
        t1 = sb("t1", [P, B, NT, C])
        tst = sb("tst", [P, NT, 6])
        tmv = sb("tmv", [P, NT, 2])
        trs = sb("trs", [P, 3, NT])
        work = sb("work", [P, 8 * 1024], F16)
        h32 = view(work, 0, [2, N], F32)
        xn = view(work, 0, [NT, C], F32)
        xf32 = [view(work, 8, [NT, C], F32), view(tiles, 4, [NT, C], F32)]
        ub32 = view(work, 8, [C + 1], F32)[0:1, :]
        xf = [view(work, 4 * i, [NT, C], F16) for i in range(2)]
        xhat = [view(work, 8 + 4 * i, [CC, N], F16) for i in range(2)]
        fold = [view(l0, 16, [4, C], F32), view(tiles, 0, [4, C], F32)]
        prod = [[view(l0, 16 + 4 * i, [4, C], F32) for i in range(2)], [view(work, 4 * i, [4, C], F32) for i in range(2)]]
        prod_pool = [[view(l0, 4 * i, [4, C], F32) for i in range(2)], [view(work, 8 + 4 * i, [4, C], F32) for i in range(2)]]
        cross_pool = [prod_pool[0], [view(tiles, 4 * i, [4, C], F32) for i in range(2)]]
        qk = sb("qk", [P, NT, 2 * C])
        val = [sb(f"val{b}", [P, NT, C]) for b in range(B)]
        cs = sb("cs", [P, 8, 4 * HEADS])
        spec = sb("spec", [P, 2, 4 * HEADS])
        dspace = [[view(l0, 4 * i, [N], F32) for i in range(4)], [view(tiles, 4 * i, [N], F32) for i in range(4)]]
        even32 = [view(l0, 16, [4, QUARTER], F32), view(work, 0, [4, QUARTER], F32)]
        top = sb("top", [HEADS, 24])
        wT = [sb(f"wT_{i}", [P, NT * HEADS], F16) for i in "hl"]
        by_sum = sb("by_sum", [HEADS, HEADS])
        w32 = cs[:, :, :].rearrange("p a b -> p (a b)")
        wh = sb("wh", [P, 5, 4 * HEADS])
        wh_raw = sb("wh_raw", [P, NT * HEADS])
        Y32 = view(late, 0, [NT, C], F32)
        Y = [view(late, 8 + 4 * i, [NT, C], F16) for i in range(2)]
        cx32 = view(late, 0, [CC, N], F32)
        cx = [view(late, 16 + 4 * i, [CC, N], F16) for i in range(2)]
        yn = qk[:, :, 0:C]
        ehalf = [view(l0, 16, [CC, 3 * QUARTER], F32), view(work, 0, [CC, 3 * QUARTER], F32)]
        RING, FIRST = [], {}
        SPLIT = 3

        def ring(name, n, taker, high=0):
            FIRST.setdefault(name, len(RING))
            RING.extend([(taker, high, name)] * n)

        def step_fills(n):
            ring(f"U{n}", 1, "A")
            if n in (1, 2):
                ring("gn1", 1, "V")
            if 1 <= n <= 4:
                ring(f"attnW{n - 1}", 1, "V", 1)
            if n in (6, 7):
                ring(f"G1_{n - 6}", 2, "V", 1)
            if n in (14, 15):
                ring(f"D0_{n - 14}", 2, "V", 1)

        for args in [("gn0", 1, "V"), ("wpT", 1, "V"), ("gn0", 1, "V"), ("A", 1, "V", 1), ("small", 1, "V"),
                     ("UW", 1, "V", 1), ("G0_0", 2, "V", 1), ("G0_1", 2, "V", 1)]:
            ring(*args)
        for n in range(B * NT):
            step_fills(n)
        PHASE2 = len(RING)
        for args in [("Q0", 2 * NT, "A"), ("D1_0", 2, "V", 1), ("D1_1", 2, "V", 1), ("C0", 2, "V"), ("Q1", 2 * SPLIT, "A"),
                     ("wgm", 1, "V"), ("T0", 1, "V"), ("W0", 1, "V"), ("Q1", 2 * (NT - SPLIT), "A"), ("I0", 4, "V"), ("C1", 2, "V"),
                     ("O0", 8, "V"), ("T1", 1, "V"), ("W1", 1, "V"), ("YT0", 4, "A"), ("gate0", 2, "V"), ("I1", 4, "V"), ("O1", 4, "V"),
                     ("YT1", 1, "A"), ("O1", 4, "V"), ("YT1", 3, "A"), ("gate1", 2, "V"), ("rank", 1, "V"), ("perm", 1, "V")]:
            ring(*args)

        def bank_of(f):
            if f < len(RING0):
                return RING0[f]
            return RING1[f % 2] if f < PHASE2 else RING2[(f - PHASE2) % 8]

        def bank(f):
            return ps[:, bank_of(f), :]

        def taken_count(f):
            return sum(t == RING[f][0] for t, _, _ in RING[:f + 1])

        def high_count(f):
            return sum(hi for _, hi, _ in RING[:f + 1])

        filled, v_taken, a_taken, high_made = sem("filled"), sem("v_taken"), sem("a_taken"), sem("high_made")
        sums_full, sums_taken = sem("sums_full"), sem("sums_taken")

        def fills(name):
            return [f for f, (_, _, n) in enumerate(RING) if n == name]

        def wait_taken(eng, f):
            eng.wait_ge(v_taken if RING[f][0] == "V" else a_taken, taken_count(f))

        s_full, s_exp = sem("s_full"), sem("s_exp")
        x_in = [sem(f"x_in{q}") for q in range(B * CC)]
        w_in, aw_in, small_in, late_in, const_in, fwd_in = sem("w_in"), sem("aw_in"), sem("small_in"), sem("late_in"), sem("const_in"), sem("fwd_in")
        inv32_in, inv_in = sem("inv32_in"), sem("inv_in")
        rows_ready, mean_ready, spread_ready, affine_ready = sem("rows_ready"), sem("mean_ready"), sem("spread_ready"), sem("affine_ready")
        h32_ready, h0_high, h0_low, h1_high, h1_low = sem("h32_ready"), sem("h0_high"), sem("h0_low"), sem("h1_high"), sem("h1_low")
        bias_ready, p_high, p_low, u_ready = sem("bias_ready"), sem("p_high"), sem("p_low"), sem("u_ready")
        var_ready, rstd_ready, xf32_ready, xf_high, xf_ready = (sem(n) for n in ("var_ready", "rstd_ready", "xf32_ready", "xf_high", "xf_ready"))
        spec_ready, peak_ready, exp_ready, weight_ready = (sem(n) for n in ("spec_ready", "peak_ready", "exp_ready", "weight_ready"))
        y_ready, y_high, y_low = sem("y_ready"), sem("y_high"), sem("y_low")
        cx_half, cx_high, cx_low0, cx_low1 = sem("cx_half"), sem("cx_high"), sem("cx_low0"), sem("cx_low1")
        shift_ready = sem("shift_ready")
        yn_ready, t_bo = sem("yn_ready"), sem("t_bo")
        crossed, wh_ready, vi_weighed = sem("crossed"), sem("wh_ready"), sem("vi_weighed")
        v_step = sem("v_step")
        root_ready = sem("root_ready")
        out_sem = sem("out_sem")
        consts_made = sem("consts_made")
        ACTV = nc.scalar.activation
        V, PL, PE = nc.vector, nc.gpsimd, nc.tensor

        xrows = nc.dram_tensor("token_rows_dram", (T, 2 * C), F16).ap()
        yrows = nc.dram_tensor("expert_rows_dram", (2 * T + TILES * P, C), F32).ap()
        late_consts = uT[:, :, :].rearrange("p a c -> p (a c)")
        small_a, small_b = (u[i][:, :, :].rearrange("p a c -> p (a c)").bitcast(F32) for i in range(2))
        const16 = late_consts[:, 0:2 * P + TT].bitcast(F16)
        ident16, before, all_ones, iota128 = (const16[:, k * P:(k + 1) * P] for k in range(4))
        token_id = const16[:, 4 * P:]
        route_f32 = late_consts[:, 2 * P + TT:2 * P + TT + 2 * TILES + TT + E * TT]
        iota_tile, spare_row = route_f32[:, 0:TILES], route_f32[:, TILES:2 * TILES]
        thresholds, scan_mask = route_f32[:, 2 * TILES:2 * TILES + TT], route_f32[:, 2 * TILES + TT:]
        wg_sb = sb("wg_sb", [P, CC, E])
        mean_of_all = sb("mean_of_all", [P, P])
        b1_sb = sb("b1_sb", [P, E, HC])
        b2_all = qk[:, :, C:2 * C]
        stage = [view(prep, 3 * i, [CC * H], F32) for i in range(2)]
        experts = view(l0, 0, [E, 4 * CC * H], F16)
        yn16 = [val[b][:, :, :].rearrange("p a c -> p (a c)").bitcast(F16).rearrange("p (a c) -> p a c", a=NT) for b in range(B)]
        tT = [view(l0, 0, [CC, N], F32), view(work, 8, [CC, N], F32)]
        sc, mx = (small_a[:, k * P:(k + 1) * P].rearrange("p (j e) -> p j e", e=E) for k in range(2))
        gidx = small_b[:, 0:P].bitcast(U32).rearrange("p (j e) -> p j e", e=E)
        gt = small_b[:, P:P + 4 * TT].rearrange("p (k j) -> p k j", k=4)
        cum = small_b[:, P + 4 * TT:P + 4 * TT + 4 * E].rearrange("p (k e) -> p k e", k=4)
        rt = view(work, 0, [5, TT * E], F32)
        oh = view(work, 3, [3, TT * E], F16)
        oh32 = view(work, 4, [2, TT * E], F32)
        slot = view(work, 5, [3, 2 * TT], F32)
        slot_u = view(work, 5.5, [3, 2 * TT], F32).bitcast(U32)
        onehot_p = view(tiles, 8, [2 * TT, P], F16)
        hot = view(tiles, 5, [2 * TT, TILES], F16)
        onehot_t = view(tiles, 0, [2 * TT, 2 * TILES], F16)
        pf, at_row = view(work, 6, [5, TILES], F32), view(work, 7.75, [3, TILES], F32)
        idx = sb("idx", [P, 2, TILES], U32)
        ended = view(work, 7, [TILES * E], F16)
        gx = view(late, 0, [6, 2 * C], F16)
        hf = view(late, 6, [3, HC * P], F32)
        hh = [view(late, 10.5 + 2.25 * i, [3, HC * P], F16) for i in range(2)]
        xT = view(late, 15, [2, 4 * P], F16)
        ysb = view(late, 17, [4, C], F32)
        psx = [ps[:, 0, :], ps[:, 1, :]]
        psh = [ps[:, 2, 0:HC * P], ps[:, 3, 0:HC * P]]
        psy = [ps[:, 4, 0:C], ps[:, 5, 0:C]]
        ygot = view(l0, 0, [2, TT, C], F32)
        outT = view(l0, 32, [B * CC, N], F32)
        tt = t1[:, :, :, :].rearrange("p b j c -> p (b j) c")
        ffn_in, b1_in, b2_in = sem("ffn_in"), sem("b1_in"), sem("b2_in")
        stage_in = [sem("stage_in0"), sem("stage_in1")]
        we_high, we_low = sem("we_high"), sem("we_low")
        row_high, row_low, row_low_v, row_out = sem("row_high"), sem("row_low"), sem("row_low_v"), sem("row_out")
        gate_ready, gexp_ready, choice_ready, perm_part, idx_ready, where_ready = (
            sem(n) for n in ("gate_ready", "gexp_ready", "choice_ready", "perm_part", "idx_ready", "where_ready"))
        gates_ready, weighed, pool_added, pool_combined = sem("gates_ready"), sem("weighed"), sem("pool_added"), sem("pool_combined")
        POOL_PAIRS, TURN_ORDER = (1, 5), (0, 2, 1, 3, 4, 6, 5, 7)
        OUT_PAIRS = ((0, 1), (2, 3), (6,), (4, 5), (7,))
        hot_ready, hot_weighed, hot_chosen = sem("hot_ready"), sem("hot_weighed"), sem("hot_chosen")
        gathered = [sem(f"gathered{k}") for k in range(6)]
        scattered = [sem(f"scattered{k}") for k in range(4)]
        x_turned, x_taken, hid_full, gelu_done, hid_high, hid_low, y_full, y_taken = (
            sem(n) for n in ("x_turned", "x_taken", "hid_full", "gelu_done", "hid_high", "hid_low", "y_full", "y_taken"))
        y_in = [[sem(f"y{c + 1}_in{q}") for q in range(8)] for c in range(2)]
        combined, out_turned, out_taken, last_taken = sem("combined"), sem("out_turned"), sem("out_taken"), sem("last_taken")

        def out_part(q):
            return outT[:, (q // 4) * CC:(q // 4 + 1) * CC, (q % 4) * 2 * P:(q % 4 + 1) * 2 * P]

        def out_bank(n):
            return ps[:, n, :].rearrange("p (k t) -> p k t", k=CC)

        block = ctx.enter_context(nc.Block())

        @block.sync
        def _(sp):
            for b in range(B):
                for k in range(CC):
                    sp.dma_start(x_sb[b][:, k, :], g["x"][b].rearrange("(k p) a b -> k p (a b)", p=P)[k]).then_inc(x_in[b * CC + k], 16)
                if b == 0:
                    sp.dma_start(const[:, :], g["const_f32"]).then_inc(const_in, 16)
                    for n, name in enumerate(["L0_conv_norm_w", "L0_conv_norm_b", "L0_conv_bq", "L0_conv_bk", "L0_conv_bv"]):
                        sp.dma_start(cols[:, n, :], g[name].rearrange("(k p) -> p k", p=P), allow_slow_non_contiguous=True).then_inc(small_in, 16)
            for i, name in enumerate(["fwd_hi", "fwd_lo"]):
                sp.dma_start(fwd[i][:, :], g[name]).then_inc(fwd_in, 16)
            for i, name in enumerate(["inv_hi", "inv_lo"]):
                sp.dma_start(inv[i][:, :], g[name]).then_inc(inv_in, 16)
            sp.wait_ge(sums_full, B * NT)
            sp.dma_start(inv32, g["inv_f32"]).then_inc(inv32_in, 16)
            sp.dma_start(wg_sb[:, :, :], g["L1_ffn_Wg"].rearrange("(k p) e -> p k e", p=P)).then_inc(ffn_in, 16)
            for e in range(E):
                sp.dma_start(b1_sb[:, E - 1 - e, :], g["L1_ffn_b1"][e].rearrange("(k p) -> p k", p=P), allow_slow_non_contiguous=True).then_inc(b1_in, 16)

            def stage_load(n):
                if n == 0:
                    sp.wait_ge(filled, FIRST[f"U{B * NT - 1}"] + 1)
                if n >= 2:
                    sp.wait_ge(we_low, n - 1)
                w = g["L1_ffn_W2" if n % 2 else "L1_ffn_W1"][n // 2].rearrange("(k p) h -> p k h", p=P)
                sp.dma_start(stage[n % 2].rearrange("p (k h) -> p k h", k=HC if n % 2 else CC), w).then_inc(stage_in[n % 2], 16)

            for n in range(2):
                stage_load(n)
            sp.wait_ge(sums_full, B * NT)
            sp.wait_ge(u_ready, B * NT)
            sp.dma_start(const16, g["const_f16"]).then_inc(ffn_in, 16)
            sp.dma_start(route_f32, g["route_f32"]).then_inc(ffn_in, 16)
            for n in range(2, 8):
                stage_load(n)
            sp.wait_ge(spec_ready, B)
            for e in range(E):
                sp.dma_start(b2_all[:, E - 1 - e, :], g["L1_ffn_b2"][e].partition_broadcast(P)).then_inc(b2_in, 16)
            for b in range(B):
                for n in range(8, 14) if b == 0 else range(14, 16):
                    stage_load(n)
                sp.wait_ge(row_low, b + 1)
                if b == 0:
                    sp.wait_ge(row_low_v, 1)
                sp.dma_start(xrows[b * N:(b + 1) * N, :].rearrange("(j p) c -> p j c", p=P), yn16[b]).then_inc(row_out, 16)
            for k in range(4):
                sp.wait_ge(scattered[k], 16 * len(range(k, TILES, 4)))
            for q in range(8):
                for c in range(2):
                    sp.dma_start(ygot[:, c, 2 * q:2 * q + 2, :],
                                 yrows[c * T + 2 * q * P:c * T + 2 * (q + 1) * P, :].rearrange("(j p) c -> p j c", p=P)).then_inc(y_in[c][q], 16)
            for pairs in OUT_PAIRS:
                b, of = pairs[0] // 4, slice(pairs[0] % 4 * 2 * P, (pairs[-1] % 4 + 1) * 2 * P)
                sp.wait_ge(out_taken, 1 + max(TURN_ORDER.index(q) for q in pairs))
                if TURN_ORDER[-1] in pairs:
                    sp.wait_ge(last_taken, 1)
                sp.dma_start(out[b].rearrange("(k p) a b -> p k (a b)", p=P)[:, :, of], outT[:, b * CC:(b + 1) * CC, of]).then_inc(out_sem, 16)
            sp.wait_ge(out_sem, 16 * len(OUT_PAIRS))

        @block.gpsimd
        def _(pool):
            PL.memset(half_neg[:, :], -0.5).then_inc(consts_made, 1)
            PL.memset(mean_of_all[:, :], 1.0 / C).then_inc(consts_made, 1)
            pool.dma_start(bp_all[:, :], g["L0_conv_bp"].partition_broadcast(P)).then_inc(late_in, 16)
            pool.dma_start(bo_all[:, :], g["L1_attn_bo"].partition_broadcast(P)).then_inc(late_in, 16)
            pool.dma_start(bg_all[:, :], g["L1_ffn_bg"].partition_broadcast(P)).then_inc(late_in, 16)
            for n, name in enumerate(["bq", "bk", "bv"]):
                pool.dma_start(qkv_row[:, n * C:(n + 1) * C], g[f"L1_attn_{name}"].rearrange("(a n) -> a n", a=1)).then_inc(late_in, 16)
            pool.wait_ge(consts_made, 2)

            def group_root(b):
                wait_taken(pool, fills(f"gn{b}")[1])
                PL.tensor_tensor(gn[:, 3, b * CC:(b + 1) * CC], gn[:, 5, b * CC:(b + 1) * CC], half_neg[:, 0:CC], ALU.pow).then_inc(root_ready, 1)

            group_root(0)
            pool.wait_ge(h0_high, 1)
            PL.tensor_tensor(h[0][1][:, 0, :], h32[:, 0, :], h[0][0][:, 0, :], ALU.subtract).then_inc(h0_low, 1)

            def rstd(n):
                pool.wait_ge(var_ready, n + 1)
                PL.tensor_tensor(trs[:, 1, :], trs[:, 0, :], half_neg[:, :], ALU.pow).then_inc(rstd_ready, 1)

            for n in range(B * NT):
                if n in (4, 5):
                    k = n - 4
                    pool.wait_ge(h1_high, k + 1)
                    PL.tensor_tensor(h[1][1][:, k, :], h32[:, k, :], h[1][0][:, k, :], ALU.subtract).then_inc(h1_low, 1)
                pool.wait_ge(p_high, n + 1)
                if n >= 2:
                    pool.wait_ge(sums_full, n - 1)
                PL.tensor_tensor(Pt[1][:, n % 2, :], prob[:, n % 2, :], Pt[0][:, n % 2, :], ALU.subtract).then_inc(p_low, 1)
                if n == 1:
                    group_root(1)
                if n == 9:
                    rstd(0)
            def expert_low(n):
                pool.wait_ge(we_high, n + 1)
                o = (n % 2) * 2 * CC * H
                PL.tensor_tensor(experts[:, E - 1 - n // 2, o + CC * H:o + 2 * CC * H], stage[n % 2],
                                 experts[:, E - 1 - n // 2, o:o + CC * H], ALU.subtract).then_inc(we_low, 1)

            def rows_low(b):
                pool.wait_ge(row_high, b + 1)
                js = slice(0, NT if b else NT // 2)
                PL.tensor_tensor(yn16[b][:, js, C:2 * C], yn[:, js, :], yn16[b][:, js, 0:C], ALU.subtract).then_inc(row_low, 1)

            def cross_products(b):
                for half in range(2):
                    wait_taken(pool, fills(f"Q{b}")[NT * (half + 1) - 1])
                    a = slice(2 * half, 2 * half + 2)
                    for n, (qi, ki) in enumerate([(1, 0), (0, 1)]):
                        PL.tensor_tensor(cross_pool[b][n][:, a, :], qk[:, qi::2, 0:C][:, a, :], qk[:, ki::2, C:2 * C][:, a, :], ALU.mult).then_inc(crossed, 1)

            def weigh_imaginary(b):
                pool.wait_ge(wh_ready, b + 1)
                vi = val[b][:, 1::2, :].rearrange("p a (h d) -> p a h d", d=DK)
                for n, row in enumerate((4, 3)):
                    w = wh[:, row, :].rearrange("p (a h) -> p a h", h=HEADS).unsqueeze(3).to_broadcast([P, 4, HEADS, DK])
                    PL.tensor_tensor(prod_pool[b][n].rearrange("p a (h d) -> p a h d", d=DK), vi, w, ALU.mult).then_inc(vi_weighed, 1)

            def context_low(b):
                pool.wait_ge(cx_high, 3 * b + 1)
                PL.tensor_tensor(cx[1][:, 0, :], cx32[:, 0, :], cx[0][:, 0, :], ALU.subtract).then_inc(cx_low0, 1)

            def residual_bias(b):
                pool.wait_ge(xf32_ready, 2 * b + 2)
                PL.tensor_tensor(t1[:, b, :, :], t1[:, b, :, :], bo_all[:, :].unsqueeze(1).to_broadcast([P, NT, C]), ALU.add).then_inc(t_bo, 1)

            rstd(1)
            cross_products(0)
            residual_bias(0)
            residual_bias(1)
            weigh_imaginary(0)
            cross_products(1)
            for n in range(2):
                expert_low(n)
            context_low(0)
            for n in range(2, 4):
                expert_low(n)
            for n in range(4, 8):
                expert_low(n)
            weigh_imaginary(1)
            for n in range(8, 10):
                expert_low(n)
            rstd(2)
            context_low(1)
            rows_low(0)
            for n in range(10, 12):
                expert_low(n)
            rstd(3)
            for n in range(12, 14):
                expert_low(n)
            rows_low(1)
            pool.wait_ge(hot_ready, 1)
            PL.tensor_tensor(onehot_t[:, :, 0:TILES], hot, token_id.unsqueeze(2).to_broadcast([P, 2 * TT, TILES]), ALU.mult).then_inc(hot_weighed, 1)
            for n in range(14, 2 * E):
                expert_low(n)
            pool.wait_ge(row_out, 16 * B)
            pool.wait_ge(idx_ready, 1)
            for i in range(TILES + 7):
                if i == 7:
                    pool.wait_ge(idx_ready, 2)
                if i < TILES:
                    if i >= 6:
                        pool.wait_ge(x_turned, i - 5)
                    pool.indirect_dma_start(gx[:, i % 6, :], None, xrows, bass.IndirectOffsetOnAxis(idx[:, 0, i:i + 1], 0)).then_inc(gathered[i % 6], 16)
                s = i - 7
                if s >= 0:
                    pool.wait_ge(y_taken, s + 1)
                    pool.indirect_dma_start(yrows, bass.IndirectOffsetOnAxis(idx[:, 1, s:s + 1], 0), ysb[:, s % 4, :], None).then_inc(scattered[s % 4], 16)

            for n, q in enumerate(POOL_PAIRS):
                pool.wait_ge(weighed, n + 1)
                js = slice(2 * q, 2 * q + 2)
                PL.tensor_tensor(ygot[:, 0, js, :], ygot[:, 0, js, :], ygot[:, 1, js, :], ALU.add).then_inc(pool_added, 1)
                pool.wait_ge(pool_added, n + 1)
                PL.tensor_tensor(tt[:, js, :], tt[:, js, :], ygot[:, 0, js, :], ALU.add).then_inc(pool_combined, 1)

        @block.scalar
        def _(act):
            for n, name in enumerate(["wq", "wk", "wv", "wp"]):
                act.dma_start(wraw[:, n, :].rearrange("p (k c) -> p k c", k=CC),
                              g[f"L0_conv_{name}"].rearrange("(k p) c -> p k c", p=P)).then_inc(w_in, 16)
            for n, name in enumerate(["Wq", "Wk", "Wv", "Wo"]):
                act.dma_start(wraw[:, 4 + n, :].rearrange("p (k c) -> p k c", k=CC),
                              g[f"L1_attn_{name}"].rearrange("(k p) c -> p k c", p=P)).then_inc(aw_in, 16)

            def make_high(f, dst, src, **kw):
                act.wait_ge(filled, f + 1)
                ACTV(dst, src, ACT.Identity, **kw).then_inc(high_made, 1)

            def take(f, dst, src, **kw):
                act.wait_ge(filled, f + 1)
                ACTV(dst, src, ACT.Identity, **kw).then_inc(a_taken, 1)

            def attn_weight_high(w):
                f = FIRST[f"attnW{w}"]
                dst = woW[0][:, :, :] if w == 3 else qkvW[0][:, :, w * C:(w + 1) * C]
                make_high(f, dst, bank(f).rearrange("p (k c) -> p k c", k=CC))

            def normalise(b):
                act.wait_ge(affine_ready, b + 1)
                if b:
                    act.wait_ge(h0_low, CC)
                for k in range(CC):
                    q = b * CC + k
                    ACTV(h32[:, k, :], x_sb[b][:, k, :], ACT.Identity, bias=gn[:, 7, q:q + 1],
                         scale=gn[:, 6, q:q + 1]).then_inc(h32_ready, 1)

            def z_high(b, m):
                wait_taken(act, FIRST["small"])
                for half in range(2):
                    f = FIRST[f"G{b}_{m}"] + half
                    make_high(f, z[b][0][:, m, half * 512:(half + 1) * 512], bank(f), bias=gq[:, m:m + 1])

            def x_high(b, m):
                for k in range(2):
                    f = FIRST[f"D{b}_{m}"] + k
                    make_high(f, xhat[0][:, m, k * 512:(k + 1) * 512], bank(f))

            def xf_hi(b):
                for i, part in enumerate((slice(0, 4), slice(4, 8))):
                    act.wait_ge(xf32_ready, 2 * b + i + 1)
                    ACTV(xf[0][:, part, :], xf32[b][:, part, :], ACT.Identity).then_inc(xf_high, 1)

            def take_qkv(b, chunks=range(NT)):
                for k in range(2 * chunks[0], 2 * chunks[-1] + 2):
                    f = fills(f"Q{b}")[k]
                    if k == 0 and b:
                        act.wait_ge(spec_ready, b)
                    dst = qk[:, k // 2, :] if k % 2 == 0 else val[b][:, k // 2, :]
                    take(f, dst, bank(f)[:, 0:512 if k % 2 == 0 else 256])

            def delays(b):
                act.wait_ge(peak_ready, b + 1)
                ACTV(dspace[b][2][0:HEADS, :], dspace[b][0][0:HEADS, :], ACT.Exp, bias=top[:, 16:17], scale=1.0 / (N * DK)).then_inc(exp_ready, 1)

            def y_hi(b):
                for i in range(2):
                    act.wait_ge(y_ready, 2 * b + i + 1)
                    ACTV(Y[0][:, i::2, :], Y32[:, i::2, :], ACT.Identity).then_inc(y_high, 1)

            def cx_hi(b):
                wait_taken(act, FIRST[f"I{b}"] + 1)
                ACTV(cx[0][:, 0, :], cx32[:, 0, :], ACT.Identity).then_inc(cx_high, 1)
                for i, half in enumerate((slice(0, HALF), slice(HALF, N))):
                    if i == 0:
                        act.wait_ge(cx_half, b + 1)
                    else:
                        wait_taken(act, FIRST[f"I{b}"] + 3)
                    ACTV(cx[0][:, 1, half], cx32[:, 1, half], ACT.Identity).then_inc(cx_high, 1)

            def expert_high(n):
                act.wait_ge(stage_in[n % 2], 16 * (n // 2 + 1))
                if n == 0:
                    act.wait_ge(sums_full, B * NT)
                if n == 4:
                    act.wait_ge(filled, FIRST["C1"] + 2)
                if n == 8:
                    act.wait_ge(cx_low1, 2)
                if n == 12:
                    wait_taken(act, fills("gate0")[1])
                o = (n % 2) * 2 * CC * H
                ACTV(experts[:, E - 1 - n // 2, o:o + CC * H], stage[n % 2], ACT.Identity).then_inc(we_high, 1)

            def normal_rows(b):
                act.wait_ge(shift_ready, b + 1)
                if b:
                    act.wait_ge(row_low, 1)
                    act.wait_ge(row_low_v, 1)
                for j in range(NT):
                    last = ACTV(yn[:, j, :], t1[:, b, j, :], ACT.Identity, bias=trs[:, 2, j:j + 1], scale=trs[:, 1, j:j + 1])
                last.then_inc(yn_ready, 1)

            def rows_high(b):
                act.wait_ge(yn_ready, b + 1)
                ACTV(yn16[b][:, :, 0:C], yn, ACT.Identity).then_inc(row_high, 1)

            def turned_tokens(b, parts=range(4)):
                for k in parts:
                    f = fills(f"YT{b}")[k]
                    take(f, tT[b][:, :, k * 2 * P:(k + 1) * 2 * P], bank(f).rearrange("p (k t) -> p k t", k=CC))

            normalise(0)
            f = FIRST["A"]
            make_high(f, A[0].rearrange("p k c -> p (k c)"), bank(f), scale=ATT_SCALE)
            f = FIRST["UW"]
            make_high(f, UW[0][:, :, 0:C], bank(f).rearrange("p (k c) -> p k c", k=CC))
            z_high(0, 0)
            z_high(0, 1)
            for n in range(B * NT):
                f = FIRST[f"U{n}"]
                if n >= 2:
                    act.wait_ge(u_ready, n - 1)
                take(f, uT[:, n % 2, :], bank(f)[:, 0:C + 1])
                act.wait_ge(bias_ready, n + 1)
                if n >= 2:
                    act.wait_ge(p_low, n - 1)
                ACTV(prob[:, n % 2, :], psS, ACT.Exp, bias=sm[:, 2, n:n + 1], accum_out=sm[:, 3, n:n + 1]).then_inc(s_exp, 1)
                act.wait_ge(s_exp, n + 1)
                if n >= 2:
                    act.wait_ge(sums_full, n - 1)
                ACTV(Pt[0][:, n % 2, :], prob[:, n % 2, :], ACT.Identity).then_inc(p_high, 1)
                if n == 2:
                    normalise(1)
                if n in (3, 4):
                    act.wait_ge(h32_ready, CC + n - 2)
                    ACTV(h[1][0][:, n - 3, :], h32[:, n - 3, :], ACT.Identity).then_inc(h1_high, 1)
                if 1 <= n <= 4:
                    attn_weight_high(n - 1)
                if n in (6, 7):
                    z_high(1, n - 6)
                if n == 11:
                    xf_hi(0)
                if n in (14, 15):
                    x_high(0, n - 14)
            take_qkv(0, range(6))
            xf_hi(1)
            take_qkv(0, range(6, NT))
            x_high(1, 0)
            x_high(1, 1)
            delays(0)
            take_qkv(1, range(5))
            y_hi(0)
            take_qkv(1, range(5, NT))
            for n in range(2):
                expert_high(n)
            cx_hi(0)
            for n in range(2, 4):
                expert_high(n)
            delays(1)
            for n in range(4, 8):
                expert_high(n)
            turned_tokens(0)
            y_hi(1)
            for n in range(8, 10):
                expert_high(n)
            normal_rows(0)
            cx_hi(1)
            rows_high(0)
            for n in range(10, 12):
                expert_high(n)
            turned_tokens(1)
            for n in range(12, 14):
                expert_high(n)
            normal_rows(1)
            rows_high(1)
            for n in range(14, 2 * E):
                expert_high(n)
            act.wait_ge(gate_ready, 1)
            ACTV(gt[:, 1, :], gt[:, 0, :], ACT.Exp).then_inc(gexp_ready, 1)
            act.wait_ge(hot_ready, 1)
            for c in range(2):
                last = ACTV(onehot_t[:, c * TT:(c + 1) * TT, TILES:], hot[:, c * TT:(c + 1) * TT, :], ACT.Identity, scale=float(c + 1))
            last.then_inc(hot_chosen, 1)
            act.wait_ge(b1_in, 16 * E)
            act.wait_ge(where_ready, 1)
            for s in range(TILES):
                e = act.value_load(where[0:1, s:s + 1], min_val=0, max_val=E - 1)
                act.wait_ge(hid_full, s + 1)
                if s >= 3:
                    act.wait_ge(hid_low, s - 2)
                for m in range(HC):
                    last = ACTV(hf[:, s % 3, m * P:(m + 1) * P], psh[s % 2][:, m * P:(m + 1) * P], ACT.Gelu,
                                bias=b1_sb[:, bass.ds(e, 1), m])
                last.then_inc(gelu_done, 1)
                act.wait_ge(gelu_done, s + 1)
                if s >= 3:
                    act.wait_ge(y_full, s - 2)
                ACTV(hh[0][:, s % 3, :], hf[:, s % 3, :], ACT.Identity).then_inc(hid_high, 1)
            def weigh(q):
                for c in range(2):
                    act.wait_ge(y_in[c][q], 16)
                    for j in (2 * q, 2 * q + 1):
                        last = ACTV(ygot[:, c, j, :], ygot[:, c, j, :], ACT.Identity, scale=gt[:, 2 + c, j:j + 1])
                last.then_inc(weighed, 1)

            act.wait_ge(gates_ready, 1)
            weigh(POOL_PAIRS[0])
            for n, q in enumerate(TURN_ORDER):
                if n == 3:
                    weigh(POOL_PAIRS[1])
                act.wait_ge(out_turned, n + 1)
                ks = slice(0, 1 if n == 7 else CC)
                ACTV(out_part(q)[:, ks, :], out_bank(n)[:, ks, :], ACT.Identity).then_inc(out_taken, 1)

        @block.vector
        def _(dve):
            steps = [0]

            def step(ins):
                steps[0] += 1
                ins.then_inc(v_step, 1)
                dve.wait_ge(v_step, steps[0])

            def full(f):
                dve.wait_ge(filled, f + 1)

            def low(f, dst, src, hi, scalar=1.0, op0=ALU.mult):
                full(f)
                dve.wait_ge(high_made, high_count(f))
                V.scalar_tensor_tensor(out=dst, in0=src, scalar=scalar, in1=hi, op0=op0, op1=ALU.subtract).then_inc(v_taken, 1)

            V.memset(ones[:, :], 1.0)
            step(V.memset(dc_row[:, :], 0.0))
            V.memset(dc_row[:, 0:1], float(N)).then_inc(rows_ready, 1)

            def channel_stats(b):
                for q in range(b * CC, (b + 1) * CC):
                    dve.wait_ge(x_in[q], 16)
                    for s in range(2):
                        last = V.bn_stats(bn[:, q, s, :], x_sb[b][:, q % CC, s * 512:(s + 1) * 512])
                    step(last)
                    last = V.bn_aggr(mv[:, q, :], bn[:, q, :, :].rearrange("p a b -> p (a b)"))
                last.then_inc(mean_ready, 1)

            def group_mean(b):
                q = slice(b * CC, (b + 1) * CC)
                f = fills(f"gn{b}")[0]
                full(f)
                V.tensor_copy(gn[:, 1, q], bank(f)[:, 0:CC]).then_inc(v_taken, 1)
                wait_taken(dve, f)
                step(V.tensor_tensor(gn[:, 2, q], mv[:, q, 0], gn[:, 1, q], ALU.subtract))
                step(V.tensor_tensor(gn[:, 4, q], gn[:, 2, q], gn[:, 2, q], ALU.mult))
                V.tensor_tensor(gn[:, 4, q], gn[:, 4, q], mv[:, q, 1], ALU.add).then_inc(spread_ready, 1)

            def group_affine(b):
                q = slice(b * CC, (b + 1) * CC)
                f = fills(f"gn{b}")[1]
                full(f)
                V.tensor_scalar(gn[:, 5, q], bank(f)[:, 0:CC], EPS_CONV, None, ALU.add).then_inc(v_taken, 1)
                dve.wait_ge(small_in, 16 * 5)
                dve.wait_ge(root_ready, b + 1)
                step(V.tensor_tensor(gn[:, 6, q], gn[:, 3, q], cols[:, NW, :], ALU.mult))
                step(V.tensor_tensor(gn[:, 2, q], gn[:, 1, q], gn[:, 6, q], ALU.mult))
                V.tensor_tensor(gn[:, 7, q], cols[:, NB, :], gn[:, 2, q], ALU.subtract).then_inc(affine_ready, 1)

            channel_stats(0)
            group_mean(0)
            f = FIRST["wpT"]
            full(f)
            V.tensor_copy(wpT.rearrange("p k c -> p (k c)"), bank(f)).then_inc(v_taken, 1)
            group_affine(0)
            for k in range(CC):
                dve.wait_ge(h32_ready, k + 1)
                high = V.tensor_copy(h[0][0][:, k, :], h32[:, k, :])
                if k == 0:
                    high.then_inc(h0_high, 1)
                else:
                    step(high)
                    V.tensor_tensor(h[0][1][:, k, :], h32[:, k, :], h[0][0][:, k, :], ALU.subtract).then_inc(h0_low, 1)
            f = FIRST["A"]
            low(f, A[1].rearrange("p k c -> p (k c)"), bank(f), A[0].rearrange("p k c -> p (k c)"), scalar=ATT_SCALE)
            f = FIRST["small"]
            full(f)
            V.tensor_scalar(gq[:, :], bank(f)[:, 0:2], ATT_SCALE, None, ALU.mult)
            V.tensor_copy(ub32[:, 0:C], bank(f)[0:1, 8:8 + C])
            V.tensor_scalar(ub32[:, C:C + 1], bank(f)[0:1, 4:5], ATT_SCALE, None, ALU.mult)
            V.tensor_scalar(gn[:, 0, 0:2], bank(f)[:, 2:4], ATT_SCALE, None, ALU.mult).then_inc(v_taken, 1)
            wait_taken(dve, f)
            V.tensor_copy(ub[0][:, :], ub32[:, :])
            step(V.tensor_copy(UW[0][:, :, C], gn[:, 0, 0:2]))
            V.tensor_tensor(ub[1][:, :], ub32[:, :], ub[0][:, :], ALU.subtract)
            V.tensor_tensor(UW[1][:, :, C], gn[:, 0, 0:2], UW[0][:, :, C], ALU.subtract).then_inc(rows_ready, 1)

            def attn_weight_low(w):
                f = FIRST[f"attnW{w}"]
                dst = [woW[i][:, :, :] if w == 3 else qkvW[i][:, :, w * C:(w + 1) * C] for i in range(2)]
                low(f, dst[1], bank(f).rearrange("p (k c) -> p k c", k=CC), dst[0])

            def z_low(b, m):
                for half in range(2):
                    f = FIRST[f"G{b}_{m}"] + half
                    s = slice(half * 512, (half + 1) * 512)
                    low(f, z[b][1][:, m, s], bank(f), z[b][0][:, m, s], scalar=gq[:, m:m + 1], op0=ALU.add)

            def score_max(n):
                wait_taken(dve, FIRST[f"U{n}"])
                dve.wait_ge(s_full, n + 1)
                r = uT[:, n % 2, C:C + 1]
                step(V.reduce_max(sm[:, 0, n:n + 1], psS, AX_X))
                step(V.tensor_tensor(sm[:, 1, n:n + 1], sm[:, 0, n:n + 1], r, ALU.add))
                V.tensor_tensor(sm[:, 2, n:n + 1], r, sm[:, 1, n:n + 1], ALU.subtract).then_inc(bias_ready, 1)

            def weigh_values(n):
                dve.wait_ge(s_exp, n + 1)
                step(V.reciprocal(sm[:, 4, n:n + 1], sm[:, 3, n:n + 1]))
                if n >= 2:
                    dve.wait_ge(sums_full, n - 1)
                step(V.tensor_scalar(u[0][:, n % 2, :], uT[:, n % 2, 0:C], sm[:, 4, n:n + 1], None, ALU.mult))
                V.scalar_tensor_tensor(out=u[1][:, n % 2, :], in0=uT[:, n % 2, 0:C], scalar=sm[:, 4, n:n + 1],
                                       in1=u[0][:, n % 2, :], op0=ALU.mult, op1=ALU.subtract).then_inc(u_ready, 1)

            def take_tokens(b):
                dve.wait_ge(sums_full, NT * (b + 1))
                for j in range(0, NT, 2):
                    V.tensor_tensor(t1[:, b, j:j + 2, :], psV[:, j:j + 2, :],
                                    bp_all[:, :].unsqueeze(1).to_broadcast([P, 2, C]), ALU.add).then_inc(sums_taken, 1)
                dve.wait_ge(sums_taken, (NT // 2) * (b + 1))

            def token_stats(b, done=0):
                for j in range(done, NT):
                    last = V.bn_stats(tst[:, j, :], t1[:, b, j, :])
                step(last)
                for j in range(NT):
                    last = V.bn_aggr(tmv[:, j, :], tst[:, j, :])
                step(last)
                V.tensor_scalar(trs[:, 0, :], tmv[:, :, 1], EPS_TOK, None, ALU.add).then_inc(var_ready, 1)

            def token_norm(b):
                dve.wait_ge(rstd_ready, b + 1)
                for j in range(NT):
                    last = V.tensor_scalar(xn[:, j, :], t1[:, b, j, :], tmv[:, j, 0:1], trs[:, 1, j:j + 1],
                                           ALU.subtract, ALU.mult)
                step(last)

            def token_shift(b):
                dve.wait_ge(rstd_ready, B + b + 1)
                V.scalar_tensor_tensor(out=trs[:, 2, :], in0=tmv[:, :, 0], scalar=-1.0, in1=trs[:, 1, :],
                                       op0=ALU.mult, op1=ALU.mult).then_inc(shift_ready, 1)

            def fold_tokens(b):
                x32 = xf32[b]
                V.tensor_tensor(x32[:, 0:4, :], xn[:, 0:4, :], xn[:, 4:8, :], ALU.subtract)
                V.tensor_tensor(fold[b], xn[:, 0:4, :], xn[:, 4:8, :], ALU.add).then_inc(xf32_ready, 1)
                dve.wait_ge(xf32_ready, 2 * b + 1)
                V.tensor_tensor(x32[:, 4:6, :], fold[b][:, 0:2, :], fold[b][:, 2:4, :], ALU.subtract)
                V.tensor_tensor(x32[:, 6:8, :], fold[b][:, 0:2, :], fold[b][:, 2:4, :], ALU.add).then_inc(xf32_ready, 1)

            def xf_low(b):
                for i, part in enumerate((slice(0, 4), slice(4, 8))):
                    dve.wait_ge(xf_high, 2 * b + i + 1)
                    V.tensor_tensor(xf[1][:, part, :], xf32[b][:, part, :], xf[0][:, part, :], ALU.subtract).then_inc(xf_ready, 1)

            def x_low(b, m):
                for k in range(2):
                    f = FIRST[f"D{b}_{m}"] + k
                    s = slice(k * 512, (k + 1) * 512)
                    low(f, xhat[1][:, m, s], bank(f), xhat[0][:, m, s])

            def cross_spectrum(b, halves=range(2)):
                for half in halves:
                    wait_taken(dve, fills(f"Q{b}")[NT * (half + 1) - 1])
                    a, ah = slice(2 * half, 2 * half + 2), slice(2 * half * HEADS, (2 * half + 2) * HEADS)
                    for n, (qi, ki) in enumerate([(0, 0), (1, 1)]):
                        pr = prod[b][n][:, a, :]
                        step(V.tensor_tensor(pr, qk[:, qi::2, 0:C][:, a, :], qk[:, ki::2, C:2 * C][:, a, :], ALU.mult))
                        V.tensor_reduce(cs[:, n, ah], pr.rearrange("p a (h d) -> p (a h) d", d=DK), AX_X, ALU.add)
                    for n in range(2):
                        dve.wait_ge(crossed, 4 * b + 2 * half + n + 1)
                        last = V.tensor_reduce(cs[:, 2 + n, ah], cross_pool[b][n][:, a, :].rearrange("p a (h d) -> p (a h) d", d=DK), AX_X, ALU.add)
                if 1 not in halves:
                    return
                step(last)
                rr, ii, ir, ri = (cs[:, n, :] for n in range(4))
                step(V.tensor_tensor(cs[:, 4, :], pair_mask, ii, ALU.mult))
                V.tensor_tensor(spec[:, 0, :], rr, cs[:, 4, :], ALU.add)
                V.tensor_tensor(cs[:, 5, :], ii, cs[:, 4, :], ALU.subtract)
                step(V.tensor_tensor(cs[:, 6, :], ir, ri, ALU.subtract))
                step(V.tensor_tensor(cs[:, 7, :], pair_mask, cs[:, 6, :], ALU.mult))
                V.tensor_tensor(spec[:, 1, :], cs[:, 7, :], cs[:, 5, :], ALU.add).then_inc(spec_ready, 1)

            def delays(b):
                hs = slice(0, HEADS)
                corr, left, weight = (t[hs, :] for t in dspace[b][0:3])
                fe, fo = FIRST[f"C{b}"], FIRST[f"C{b}"] + 1
                ev, ep = even32[b][hs, 0:2, :], even32[b][hs, 2:4, :]
                full(fe)
                step(V.tensor_copy(ev[:, 0, :], bank(fe)[hs, QUARTER:512]))
                V.tensor_tensor(ep[:, 0, :], ev[:, 0, :], bank(fe)[hs, 0:QUARTER], ALU.add)
                V.tensor_tensor(ep[:, 1, :], ev[:, 0, :], bank(fe)[hs, 0:QUARTER], ALU.subtract).then_inc(v_taken, 1)
                wait_taken(dve, fe)
                full(fo)
                V.tensor_tensor(corr[:, 0:HALF], ep.rearrange("p a b -> p (a b)"), bank(fo)[hs, :], ALU.add)
                V.tensor_tensor(corr[:, HALF:N], ep.rearrange("p a b -> p (a b)"), bank(fo)[hs, :], ALU.subtract).then_inc(v_taken, 1)
                wait_taken(dve, fo)
                step(V.max(top[:, 0:8], corr))
                V.tensor_scalar(top[:, 16:17], top[:, 0:1], -1.0 / (N * DK), None, ALU.mult).then_inc(peak_ready, 1)
                step(V.match_replace(left, top[:, 0:8], corr, -3.0e38))
                step(V.max(top[:, 8:16], left))
                dve.wait_ge(exp_ready, b + 1)
                step(V.scalar_tensor_tensor(out=left, in0=corr, scalar=top[:, TOPK - 1:TOPK], in1=weight, op0=ALU.is_ge, op1=ALU.mult,
                                            accum_out=top[:, 17:18]))
                step(V.reciprocal(top[:, 18:19], top[:, 17:18]))
                V.tensor_scalar(by_sum[:, :], ident[hs, hs], top[:, 18:19], None, ALU.mult).then_inc(weight_ready, 1)

            def w_fold(b):
                f = FIRST[f"T{b}"]
                full(f)
                w = w32[:, 0:NT * HEADS]
                step(V.tensor_copy(w, bank(f)[:, 0:NT * HEADS]))
                q = NT * HEADS // 4
                fd, sums = w32[:, 4 * q:8 * q], w32[:, 8 * q:10 * q]
                V.tensor_tensor(fd[:, 0:2 * q], w[:, 0:2 * q], w[:, 2 * q:4 * q], ALU.subtract)
                step(V.tensor_tensor(sums, w[:, 0:2 * q], w[:, 2 * q:4 * q], ALU.add))
                V.tensor_tensor(fd[:, 2 * q:3 * q], sums[:, 0:q], sums[:, q:2 * q], ALU.subtract)
                step(V.tensor_tensor(fd[:, 3 * q:4 * q], sums[:, 0:q], sums[:, q:2 * q], ALU.add))
                step(V.tensor_copy(wT[0][:, :], fd))
                V.tensor_tensor(wT[1][:, :], fd, wT[0][:, :], ALU.subtract).then_inc(v_taken, 1)

            def apply_delays(b):
                f = FIRST[f"W{b}"]
                full(f)
                V.tensor_scalar(wh_raw[:, :], bank(f)[:, 0:NT * HEADS], SPEC_SCALE, None, ALU.mult).then_inc(v_taken, 1)
                wait_taken(dve, f)
                pairs = wh_raw[:, :].rearrange("p (a i h) -> p a i h", i=2, h=HEADS)
                m = pair_mask.rearrange("p (a h) -> p a h", h=HEADS)
                w = [wh[:, n, :].rearrange("p (a h) -> p a h", h=HEADS) for n in range(4)]
                V.tensor_tensor(w[2], m, pairs[:, :, 0, :], ALU.mult)
                step(V.tensor_tensor(w[0], m, pairs[:, :, 1, :], ALU.mult))
                step(V.tensor_tensor(w[1], pairs[:, :, 1, :], w[0], ALU.subtract))
                step(V.tensor_tensor(w[3], w[2], w[1], ALU.add))

                def wide(ap):
                    return ap.unsqueeze(3).to_broadcast([P, 4, HEADS, DK])

                def heads(ap):
                    return ap.rearrange("p a (h d) -> p a h d", d=DK)

                vr = heads(val[b][:, 0::2, :])
                yr, yi = heads(Y32[:, 0::2, :]), heads(Y32[:, 1::2, :])
                pr = [heads(p) for p in prod[b]]
                V.tensor_copy(wh[:, 4, :].rearrange("p (a h) -> p a h", h=HEADS), w[0]).then_inc(wh_ready, 1)
                V.tensor_tensor(pr[0], vr, wide(pairs[:, :, 0, :]), ALU.mult)
                dve.wait_ge(vi_weighed, 2 * b + 1)
                step(V.tensor_tensor(pr[1], vr, wide(w[0]), ALU.mult))
                V.tensor_tensor(yr, pr[0], heads(prod_pool[b][0]), ALU.subtract).then_inc(y_ready, 1)
                dve.wait_ge(vi_weighed, 2 * b + 2)
                V.tensor_tensor(yi, pr[1], heads(prod_pool[b][1]), ALU.add).then_inc(y_ready, 1)
                for i in range(2):
                    dve.wait_ge(y_high, 2 * b + i + 1)
                    V.tensor_tensor(Y[1][:, i::2, :], Y32[:, i::2, :], Y[0][:, i::2, :], ALU.subtract).then_inc(y_low, 1)

            def inverse(b, ms=range(CC)):
                for m in ms:
                    fe = FIRST[f"I{b}"] + 2 * m
                    fo = fe + 1
                    full(fe)
                    step(V.tensor_copy(ehalf[b][:, m, 0:QUARTER], bank(fe)[:, QUARTER:512]))
                    e0 = ehalf[b][:, m, 0:QUARTER]
                    V.tensor_tensor(ehalf[b][:, m, QUARTER:HALF], e0, bank(fe)[:, 0:QUARTER], ALU.add)
                    V.tensor_tensor(ehalf[b][:, m, HALF:HALF + QUARTER], e0, bank(fe)[:, 0:QUARTER], ALU.subtract).then_inc(v_taken, 1)
                    wait_taken(dve, fe)
                    full(fo)
                    ee = ehalf[b][:, m, QUARTER:HALF + QUARTER]
                    first = V.tensor_tensor(cx32[:, m, 0:HALF], ee, bank(fo), ALU.add)
                    if m == 1:
                        first.then_inc(cx_half, 1)
                    V.tensor_tensor(cx32[:, m, HALF:N], ee, bank(fo), ALU.subtract).then_inc(v_taken, 1)
                if 1 not in ms:
                    return
                for i, half in enumerate((slice(0, HALF), slice(HALF, N))):
                    dve.wait_ge(cx_high, 3 * b + 2 + i)
                    V.tensor_tensor(cx[1][:, 1, half], cx32[:, 1, half], cx[0][:, 1, half], ALU.subtract).then_inc(cx_low1, 1)

            def add_attention(b, stats=False):
                dve.wait_ge(t_bo, b + 1)
                for j in range(NT):
                    f = fills(f"O{b}")[j]
                    full(f)
                    V.scalar_tensor_tensor(out=t1[:, b, j, :], in0=bank(f)[:, 0:C], scalar=1.0 / (N * SPEC_SCALE),
                                           in1=t1[:, b, j, :], op0=ALU.mult, op1=ALU.add).then_inc(v_taken, 1)
                    if stats and j:
                        wait_taken(dve, fills(f"O{b}")[j - 1])
                        V.bn_stats(tst[:, j - 1, :], t1[:, b, j - 1, :])
                wait_taken(dve, f)

            def gate_take(b):
                for half, f in enumerate(fills(f"gate{b}")):
                    full(f)
                    js = slice(b * NT + half * NT // 2, b * NT + (half + 1) * NT // 2)
                    V.tensor_copy(sc[:, js, :], bank(f)[:, 0:NT // 2 * E].rearrange("p (j e) -> p j e", e=E)).then_inc(v_taken, 1)
                    wait_taken(dve, f)

            def gate_order(b):
                js = slice(b * NT, (b + 1) * NT)
                step(V.tensor_tensor(sc[:, js, :], sc[:, js, :], trs[:, 1, :].unsqueeze(2).to_broadcast([P, NT, E]), ALU.mult))
                step(V.tensor_tensor(sc[:, js, :], sc[:, js, :], bg_all[:, :].unsqueeze(1).to_broadcast([P, NT, E]), ALU.add))
                for j in range(b * NT, (b + 1) * NT):
                    last = V.max(mx[:, j, :], sc[:, j, :])
                step(last)
                for j in range(b * NT, (b + 1) * NT):
                    last = V.max_index(gidx[:, j, :], mx[:, j, :], sc[:, j, :])
                step(last)

            def by_tile(ap):
                return ap.rearrange("p (j e) -> p j e", e=E)

            def by_expert(ap):
                return ap.rearrange("p (e j) -> p e j", e=E)

            def route():
                chosen, count, upto, off, prods = (rt[:, k, :] for k in range(5))
                step(V.tensor_copy(chosen, gidx[:, :, :].rearrange("p j e -> p (j e)")))
                V.tensor_tensor(gt[:, 0, :], mx[:, :, 1], mx[:, :, 0], ALU.subtract).then_inc(gate_ready, 1)
                dve.wait_ge(ffn_in, 48)
                for c in range(2):
                    last = V.tensor_tensor(by_tile(oh[:, c, :]), iota8.unsqueeze(1).to_broadcast([P, TT, E]),
                                           by_tile(chosen)[:, :, c].unsqueeze(2).to_broadcast([P, TT, E]), ALU.is_equal)
                step(last)
                V.tensor_tensor(oh[:, 2, :], oh[:, 0, :], oh[:, 1, :], ALU.add).then_inc(choice_ready, 1)
                f = FIRST["rank"]
                full(f)
                step(V.tensor_copy(by_expert(count), bank(f)[:, TT * E:2 * TT * E].rearrange("p (j e) -> p e j", e=E)))
                step(V.tensor_tensor_scan(upto, scan_mask, count, 0.0, ALU.mult, ALU.add))
                V.tensor_tensor(off, upto, count, ALU.subtract)
                step(V.tensor_tensor(by_expert(prods), by_expert(upto)[:, :, TT - 1].unsqueeze(2).to_broadcast([P, E, TT]),
                                     thresholds.unsqueeze(1).to_broadcast([P, E, TT]), ALU.is_gt))
                step(V.tensor_reduce(cum[:, 0, :], by_expert(prods), AX_X, ALU.add))
                step(V.tensor_tensor_scan(cum[:, 1, :], scan_mask[:, 1:1 + E], cum[:, 0, :], 0.0, ALU.mult, ALU.add))
                step(V.tensor_tensor(cum[:, 2, :], cum[:, 1, :], cum[:, 0, :], ALU.subtract))
                step(V.scalar_tensor_tensor(out=by_expert(off), in0=cum[:, 2, :].unsqueeze(2).to_broadcast([P, E, TT]), scalar=float(P),
                                            in1=by_expert(off), op0=ALU.mult, op1=ALU.add))
                step(V.tensor_tensor(by_tile(upto), off.rearrange("p (e j) -> p j e", e=E), by_tile(bank(f)[:, 0:TT * E]), ALU.add))
                for c in range(2):
                    last = V.tensor_tensor(oh32[:, c, :], oh[:, c, :], upto, ALU.mult)
                last.then_inc(v_taken, 1)
                wait_taken(dve, f)
                step(V.tensor_reduce(slot[:, 0, :], oh32.rearrange("p c (j e) -> p (c j) e", e=E), AX_X, ALU.add))
                step(V.tensor_copy(slot_u[:, 0, :], slot[:, 0, :]))
                V.tensor_scalar(slot_u[:, 1, :], slot_u[:, 0, :], P - 1, None, ALU.bitwise_and)
                step(V.tensor_scalar(slot_u[:, 2, :], slot_u[:, 0, :], 7, None, ALU.logical_shift_right))
                step(V.tensor_copy(slot[:, 1:3, :], slot_u[:, 1:3, :]))
                V.tensor_tensor(hot, iota_tile.unsqueeze(1).to_broadcast([P, 2 * TT, TILES]),
                                     slot[:, 2, :].unsqueeze(2).to_broadcast([P, 2 * TT, TILES]), ALU.is_equal).then_inc(hot_ready, 1)
                for q in range(0, 2 * TT, 8):
                    V.tensor_tensor(onehot_p[:, q:q + 8, :], iota128.unsqueeze(1).to_broadcast([P, 8, P]),
                                    slot[:, 1, q:q + 8].unsqueeze(2).to_broadcast([P, 8, P]), ALU.is_equal).then_inc(perm_part, 1)
                f = FIRST["perm"]
                full(f)
                V.tensor_copy(pf[:, 0, :], bank(f)[:, 0:TILES])
                step(V.tensor_copy(pf[:, 1, :], bank(f)[:, TILES:2 * TILES]))
                V.tensor_copy(idx[:, 0, :], pf[:, 0, :]).then_inc(idx_ready, 1)
                after = ended[0:1, :].rearrange("p (s e) -> p s e", e=E)
                step(V.tensor_tensor(after, iota_tile[0:1, :].unsqueeze(2).to_broadcast([1, TILES, E]),
                                     cum[0:1, 1, :].unsqueeze(1).to_broadcast([1, TILES, E]), ALU.is_ge))
                step(V.tensor_reduce(at_row[0:1, 0, :], after, AX_X, ALU.add))
                step(V.tensor_scalar(at_row[0:1, 1, :], at_row[0:1, 0, :], -1.0, float(E - 1), ALU.mult, ALU.add))
                step(V.tensor_scalar(at_row[0:1, 2, :], at_row[0:1, 1, :], 0.0, None, ALU.max))
                V.tensor_copy(where[:, 0:TILES], at_row[0:1, 2, :]).then_inc(where_ready, 1)
                V.tensor_scalar(pf[:, 2, :], pf[:, 1, :], 0.0, None, ALU.is_equal)
                step(V.scalar_tensor_tensor(out=pf[:, 3, :], in0=pf[:, 1, :], scalar=float(T), in1=pf[:, 0, :], op0=ALU.mult, op1=ALU.add))
                step(V.tensor_tensor(pf[:, 4, :], pf[:, 2, :], spare_row, ALU.mult))
                step(V.scalar_tensor_tensor(out=pf[:, 2, :], in0=pf[:, 3, :], scalar=float(T), in1=pf[:, 4, :], op0=ALU.subtract, op1=ALU.add))
                V.tensor_copy(idx[:, 1, :], pf[:, 2, :]).then_inc(idx_ready, 1)
                dve.wait_ge(gexp_ready, 1)
                step(V.tensor_scalar(gt[:, 3, :], gt[:, 1, :], 1.0, None, ALU.add))
                step(V.reciprocal(gt[:, 2, :], gt[:, 3, :]))
                V.tensor_tensor(gt[:, 3, :], gt[:, 1, :], gt[:, 2, :], ALU.mult).then_inc(gates_ready, 1)
                dve.wait_ge(gates_ready, 1)

            def take_gathered(s):
                dve.wait_ge(x_turned, s + 1)
                if s >= 2:
                    dve.wait_ge(hid_full, s - 1)
                V.tensor_copy(xT[:, s % 2, :], psx[s % 2]).then_inc(x_taken, 1)

            def hidden_low(s):
                dve.wait_ge(hid_high, s + 1)
                if s >= 3:
                    dve.wait_ge(y_full, s - 2)
                V.tensor_tensor(hh[1][:, s % 3, :], hf[:, s % 3, :], hh[0][:, s % 3, :], ALU.subtract).then_inc(hid_low, 1)

            def take_result(s):
                e = dve.value_load(where[0:1, s:s + 1], min_val=0, max_val=E - 1)
                dve.wait_ge(y_full, s + 1)
                if s >= 4:
                    dve.wait_ge(scattered[s % 4], 16 * (s // 4))
                V.tensor_tensor(ysb[:, s % 4, :], psy[s % 2], b2_all[:, bass.ds(e, 1), :].rearrange("p a c -> p (a c)"), ALU.add).then_inc(y_taken, 1)

            def combine():
                for q in range(8):
                    if q in POOL_PAIRS:
                        continue
                    for c in range(2):
                        dve.wait_ge(y_in[c][q], 16)
                        for j in (2 * q, 2 * q + 1):
                            last = V.scalar_tensor_tensor(out=tt[:, j, :], in0=ygot[:, c, j, :], scalar=gt[:, 2 + c, j:j + 1],
                                                          in1=tt[:, j, :], op0=ALU.mult, op1=ALU.add)
                        if c == 0:
                            step(last)
                    last.then_inc(combined, 1)
                dve.wait_ge(out_turned, 9)
                V.tensor_copy(out_part(TURN_ORDER[-1])[:, 1, :], out_bank(0)[:, 1, :]).then_inc(last_taken, 1)

            f = FIRST["UW"]
            low(f, UW[1][:, :, 0:C], bank(f).rearrange("p (k c) -> p k c", k=CC), UW[0][:, :, 0:C])
            z_low(0, 0)
            z_low(0, 1)
            for n in range(B * NT + 1):
                if n >= 1:
                    weigh_values(n - 1)
                if n < B * NT:
                    score_max(n)
                if n == 0:
                    channel_stats(1)
                if n == 1:
                    group_mean(1)
                if n == 2:
                    group_affine(1)
                if 1 <= n <= 4:
                    attn_weight_low(n - 1)
                if n in (6, 7):
                    z_low(1, n - 6)
                if n == NT:
                    dve.wait_ge(late_in, 16 * 6)
                    take_tokens(0)
                if n == 9:
                    token_stats(0)
                if n == 10:
                    token_norm(0)
                if n == 11:
                    fold_tokens(0)
                if n == 12:
                    xf_low(0)
                if n in (14, 15):
                    x_low(0, n - 14)
            take_tokens(1)
            token_stats(1)
            token_norm(1)
            fold_tokens(1)
            xf_low(1)
            cross_spectrum(0)
            x_low(1, 0)
            x_low(1, 1)
            delays(0)
            f = FIRST["wgm"]
            full(f)
            V.tensor_tensor(wg_sb[:, :, :], wg_sb[:, :, :], bank(f)[:, 0:E].unsqueeze(1).to_broadcast([P, CC, E]), ALU.subtract).then_inc(v_taken, 1)
            w_fold(0)
            apply_delays(0)
            cross_spectrum(1)
            inverse(0)
            delays(1)
            add_attention(0)
            w_fold(1)
            for j in range(0, 6):
                V.bn_stats(tst[:, j, :], t1[:, 0, j, :])
            apply_delays(1)
            gate_take(0)
            token_stats(0, 6)
            token_shift(0)
            inverse(1)
            gate_order(0)
            add_attention(1, stats=True)
            dve.wait_ge(yn_ready, 1)
            token_stats(1, NT - 1)
            dve.wait_ge(row_high, 1)
            V.tensor_tensor(yn16[0][:, NT // 2:, C:2 * C], yn[:, NT // 2:, :], yn16[0][:, NT // 2:, 0:C], ALU.subtract).then_inc(row_low_v, 1)
            token_shift(1)
            gate_take(1)
            gate_order(1)
            route()
            dve.wait_ge(b2_in, 16 * E)
            for i in range(TILES + 3):
                if i < TILES:
                    take_gathered(i)
                if 0 <= i - 2 < TILES:
                    hidden_low(i - 2)
                if 0 <= i - 3 < TILES:
                    take_result(i - 3)
            combine()

        @block.tensor
        def _(pe):
            at = [0]

            def fill(name):
                f = at[0]
                at[0] += 1
                assert RING[f][2] == name
                if f < len(RING0):
                    if RING0[f] in RING0[:f]:
                        wait_taken(pe, f - 2)
                elif f < PHASE2 + 2:
                    wait_taken(pe, f - 2)
                elif f < PHASE2 + 4:
                    pe.wait_ge(s_exp, B * NT)
                elif f < PHASE2 + 8:
                    pe.wait_ge(sums_taken, (NT // 2) * B)
                else:
                    wait_taken(pe, f - 8)
                return bank(f)

            def product(dst, parts, more=()):
                seq = []
                for (lh, ll), (rh, rl) in parts:
                    seq += [(lh, rh), (lh, rl), (ll, rh)]
                seq += list(more)
                for n, (lhs, rhs) in enumerate(seq):
                    last = PE.matmul(dst, lhs, rhs, start=(n == 0), stop=(n == len(seq) - 1))
                return last

            def hl(pair, *ix):
                return tuple(t[ix] for t in pair)

            S = slice(None)

            def group_means(b):
                pe.wait_ge(mean_ready, b + 1)
                PE.matmul(fill(f"gn{b}")[:, 0:CC], blockdiag, mv[:, b * CC:(b + 1) * CC, 0], start=True, stop=True).then_inc(filled, 1)

            def group_spreads(b):
                pe.wait_ge(spread_ready, b + 1)
                PE.matmul(fill(f"gn{b}")[:, 0:CC], blockdiag, gn[:, 4, b * CC:(b + 1) * CC], start=True, stop=True).then_inc(filled, 1)

            def attn_weight(w):
                if w == 0:
                    pe.wait_ge(aw_in, 64)
                dst = fill(f"attnW{w}")
                for m in range(CC):
                    for o in range(CC):
                        last = PE.transpose(dst[:, m * C + o * P:m * C + (o + 1) * P], raw(4 + w, o)[:, m * P:(m + 1) * P], ident)
                last.then_inc(filled, 1)

            pe.wait_ge(const_in, 16)
            group_means(0)
            pe.wait_ge(w_in, 64)
            dst = fill("wpT")
            for m in range(CC):
                for o in range(CC):
                    last = PE.transpose(dst[:, m * C + o * P:m * C + (o + 1) * P], raw(WP, o)[:, m * P:(m + 1) * P], ident)
            last.then_inc(filled, 1)
            group_spreads(0)
            dst = fill("A")
            for m in range(CC):
                for o in range(CC):
                    last = PE.matmul(dst[:, m * C:(m + 1) * C], raw(WQ, o)[:, m * P:(m + 1) * P], raw(WK, o), start=(o == 0), stop=(o == CC - 1))
            last.then_inc(filled, 1)
            pe.wait_ge(small_in, 16 * 5)
            wait_taken(pe, FIRST["wpT"])
            dst = fill("small")
            for col, w, c in ((0, WK, BQ), (2, WQ, BK)):
                for m in range(CC):
                    for o in range(CC):
                        PE.matmul(dst[:, col + m:col + m + 1], raw(w, o)[:, m * P:(m + 1) * P], cols[:, c, o:o + 1], start=(o == 0), stop=(o == CC - 1))
            for o in range(CC):
                PE.matmul(dst[0:1, 4:5], cols[:, BQ, o:o + 1], cols[:, BK, o:o + 1], start=(o == 0), stop=(o == CC - 1))
            for o in range(CC):
                last = PE.matmul(dst[0:1, 8:8 + C], cols[:, BV, o:o + 1], wpT[:, o, :], start=(o == 0), stop=(o == CC - 1))
            last.then_inc(filled, 1)

            def project_queries(b, m):
                pe.wait_ge(h1_low if b else h0_low, CC)
                if b == 0:
                    wait_taken(pe, FIRST["A"])
                for half in range(2):
                    s = slice(half * 512, (half + 1) * 512)
                    product(fill(f"G{b}_{m}"), [(hl(A, S, k, slice(m * P, (m + 1) * P)), hl(h[b], S, k, s)) for k in range(CC)]).then_inc(filled, 1)

            def project_values(n):
                b, i = n // NT, n % NT
                pe.wait_ge(rows_ready, 2)
                if n == 0:
                    wait_taken(pe, FIRST["UW"])
                product(fill(f"U{n}")[:, 0:C + 1], [(hl(h[b], S, k, slice(i * P, (i + 1) * P)), hl(UW, S, k, S)) for k in range(CC)],
                        [(ones[:, :], t[:, :]) for t in ub]).then_inc(filled, 1)

            def scores(n):
                b, i = n // NT, n % NT
                if n >= 1:
                    pe.wait_ge(s_exp, n)
                if i == 0:
                    wait_taken(pe, FIRST[f"G{b}_1"] + 1)
                for half in range(2):
                    last = product(psS[:, half * 512:(half + 1) * 512],
                                   [(hl(z[b], S, k, slice(i * P, (i + 1) * P)), hl(h[b], S, k, slice(half * 512, (half + 1) * 512))) for k in range(CC)])
                last.then_inc(s_full, 1)

            def residual(b):
                if b:
                    pe.wait_ge(sums_taken, (NT // 2) * b)
                else:
                    wait_taken(pe, FIRST["UW"])
                for j in range(NT):
                    for k in range(CC):
                        PE.matmul(psV[:, j, k * P:(k + 1) * P], x_sb[b][:, k, j * P:(j + 1) * P], ident, is_transpose=True,
                                  start=(j % 2 == 0 and k == 0), stop=False, skip_group_check=True)

            def sum_values(n):
                b, i = n // NT, n % NT
                pe.wait_ge(p_low, n + 1)
                pe.wait_ge(u_ready, n + 1)
                for j in range(NT):
                    for l, r in ((0, 0), (0, 1), (1, 0)):
                        last = PE.matmul(psV[:, j, :], Pt[l][:, n % 2, j * P:(j + 1) * P], u[r][:, n % 2, :],
                                         start=False, stop=(i == NT - 1), skip_group_check=True)
                last.then_inc(sums_full, 1)

            def spectra(b, m):
                pe.wait_ge(fwd_in, 32)
                pe.wait_ge(xf_ready, 2 * b + 1)
                cs_ = slice(m * P, (m + 1) * P)
                product(fill(f"D{b}_{m}"), [(hl(xf, S, k, cs_), tuple(odd(t, k) for t in fwd)) for k in range(4)]).then_inc(filled, 1)
                pe.wait_ge(xf_ready, 2 * b + 2)
                dst = fill(f"D{b}_{m}")
                for which in range(2):
                    last = product(dst[:, which * QUARTER:(which + 1) * QUARTER],
                                   [(hl(xf, S, 4 + 2 * which + k, cs_), tuple(even(t, which, k) for t in fwd)) for k in range(2)])
                last.then_inc(filled, 1)

            def project(b, chunks=range(NT)):
                pe.wait_ge(late_in, 16 * 6)
                wait_taken(pe, FIRST[f"D{b}_1"] + 1)
                for j in chunks:
                    for lo, n in ((0, 512), (512, 256)):
                        more = [(dc_row[:, :], qkv_row[:, lo:lo + n])] if j == 6 else []
                        product(fill(f"Q{b}")[:, 0:n], [(hl(xhat, S, k, slice(j * P, (j + 1) * P)), hl(qkvW, S, k, slice(lo, lo + n))) for k in range(CC)],
                                more).then_inc(filled, 1)

            def correlate(b):
                pe.wait_ge(inv32_in, 16)
                pe.wait_ge(spec_ready, b + 1)

                def sp_(chunk):
                    return spec[:, chunk % 2, (chunk // 2) * HEADS:(chunk // 2 + 1) * HEADS]

                dst = fill(f"C{b}")
                for which in range(2):
                    for k in range(2):
                        last = PE.matmul(dst[0:HEADS, which * QUARTER:(which + 1) * QUARTER], sp_(4 + 2 * which + k),
                                         even(inv32, which, k), start=(k == 0), stop=(k == 1))
                last.then_inc(filled, 1)
                dst = fill(f"C{b}")
                for k in range(4):
                    last = PE.matmul(dst[0:HEADS, :], sp_(k), odd(inv32, k), start=(k == 0), stop=(k == 3))
                last.then_inc(filled, 1)

            def weight_spectrum(b):
                pe.wait_ge(weight_ready, b + 1)
                dst = fill(f"T{b}")
                for j in range(NT):
                    last = PE.matmul(dst[:, j * HEADS:(j + 1) * HEADS], dspace[b][1][0:HEADS, j * P:(j + 1) * P], by_sum[:, :], start=True, stop=True)
                last.then_inc(filled, 1)
                wait_taken(pe, FIRST[f"T{b}"])
                dst = fill(f"W{b}")
                for j in range(NT):
                    if j < 4:
                        ks = [(k, tuple(odd(t, k)[:, j * P:(j + 1) * P] for t in fwd)) for k in range(4)]
                    else:
                        which = (j - 4) // 2
                        ks = [(4 + 2 * which + k, tuple(even(t, which, k)[:, (j % 2) * P:(j % 2 + 1) * P] for t in fwd)) for k in range(2)]
                    last = product(dst[:, j * HEADS:(j + 1) * HEADS],
                                   [(tab, hl(wT, S, slice(k * HEADS, (k + 1) * HEADS))) for k, tab in ks])
                last.then_inc(filled, 1)

            def inverse(b):
                pe.wait_ge(inv_in, 32)
                pe.wait_ge(y_low, 2 * b + 2)
                for m in range(CC):
                    cs_ = slice(m * P, (m + 1) * P)
                    dst = fill(f"I{b}")
                    for which in range(2):
                        last = product(dst[:, which * QUARTER:(which + 1) * QUARTER],
                                       [(hl(Y, S, 4 + 2 * which + k, cs_), tuple(even(t, which, k) for t in inv)) for k in range(2)])
                    last.then_inc(filled, 1)
                    product(fill(f"I{b}"), [(hl(Y, S, k, cs_), tuple(odd(t, k) for t in inv)) for k in range(4)]).then_inc(filled, 1)

            def out_project(b, chunks=range(NT)):
                pe.wait_ge(cx_low0, b + 1)
                for j in chunks:
                    if j in (0, NT // 2):
                        pe.wait_ge(cx_low1, 2 * b + 1 + 2 * j // NT)
                    product(fill(f"O{b}")[:, 0:C], [(hl(cx, S, k, slice(j * P, (j + 1) * P)), hl(woW, S, k, S)) for k in range(CC)]).then_inc(filled, 1)

            def turn_tokens(b, k):
                wait_taken(pe, fills(f"O{b}")[2 * k + 1])
                dst = fill(f"YT{b}")
                for m in range(CC):
                    for a in range(2):
                        last = PE.transpose(dst[:, m * 2 * P + a * P:m * 2 * P + (a + 1) * P], t1[:, b, 2 * k + a, m * P:(m + 1) * P], ident)
                last.then_inc(filled, 1)

            def gate(b, half):
                wait_taken(pe, FIRST["wgm"])
                wait_taken(pe, fills(f"YT{b}")[2 * half + 1])
                dst = fill(f"gate{b}")
                for j in range(NT // 2):
                    at_token = (half * NT // 2 + j) * P
                    for k in range(CC):
                        last = PE.matmul(dst[:, j * E:(j + 1) * E], tT[b][:, k, at_token:at_token + P], wg_sb[:, k, :],
                                         start=(k == 0), stop=(k == CC - 1))
                last.then_inc(filled, 1)

            def turn_gathered(s):
                pe.wait_ge(gathered[s % 6], 16 * (s // 6 + 1))
                if s >= 2:
                    pe.wait_ge(x_taken, s - 1)
                for k in range(4):
                    last = PE.matmul(psx[s % 2][:, k * P:(k + 1) * P], gx[:, s % 6, k * P:(k + 1) * P], ident16, start=True, stop=True)
                last.then_inc(x_turned, 1)

            def hidden(s):
                pe.wait_ge(x_taken, s + 1)
                if s >= 2:
                    pe.wait_ge(gelu_done, s - 1)
                e = at_expert[s % 16]
                for m in range(HC):
                    for n, (l, r, k) in enumerate([(l, r, k) for k in range(CC) for l, r in ((0, 0), (0, 1), (1, 0))]):
                        o = l * CC * H + k * H + m * P
                        last = PE.matmul(psh[s % 2][:, m * P:(m + 1) * P], experts[:, bass.ds(e, 1), o:o + P].rearrange("p a c -> p (a c)"),
                                         xT[:, s % 2, (r * CC + k) * P:(r * CC + k + 1) * P], start=(n == 0), stop=(n == 3 * CC - 1))
                        if (m, n) == (HC - 1, 3 * CC - 1):
                            last.then_inc(hid_full, 1)
                        yield

            def results(s):
                e = at_expert[s % 16]
                pe.wait_ge(hid_low, s + 1)
                if s >= 2:
                    pe.wait_ge(y_taken, s - 1)
                for n, (l, r, m) in enumerate([(l, r, m) for m in range(HC) for l, r in ((0, 0), (0, 1), (1, 0))]):
                    o = (2 + r) * CC * H + m * C
                    last = PE.matmul(psy[s % 2], hh[l][:, s % 3, m * P:(m + 1) * P], experts[:, bass.ds(e, 1), o:o + C].rearrange("p a c -> p (a c)"),
                                     start=(n == 0), stop=(n == 3 * HC - 1))
                    if n == 3 * HC - 1:
                        last.then_inc(y_full, 1)
                    yield

            at_expert = [None] * 16

            def read_where(i):
                n = min(8, TILES - i)
                _, at_expert[i % 16:i % 16 + n] = nc.values_load_multi_w_load_instructions(
                    where[0:1, i:i + n], engines=(mybir.EngineType.PE,), min_val=0, max_val=E - 1,
                    skip_runtime_bounds_check_because="VectorE holds them between 0 and E - 1")

            dst = fill("UW")
            for m in range(CC):
                for o in range(CC):
                    last = PE.matmul(dst[:, m * C:(m + 1) * C], raw(WV, o)[:, m * P:(m + 1) * P], wpT[:, o, :], start=(o == 0), stop=(o == CC - 1))
            last.then_inc(filled, 1)
            project_queries(0, 0)
            project_queries(0, 1)
            for n in range(B * NT):
                project_values(n)
                if n == 1:
                    residual(0)
                scores(n)
                if n == 1:
                    group_means(1)
                if n == 2:
                    group_spreads(1)
                if 1 <= n <= 4:
                    attn_weight(n - 1)
                if n in (6, 7):
                    project_queries(1, n - 6)
                if n in (14, 15):
                    spectra(0, n - 14)
                if n == NT + 1:
                    residual(1)
                if n >= 1:
                    sum_values(n - 1)
            sum_values(B * NT - 1)
            project(0)
            spectra(1, 0)
            spectra(1, 1)
            correlate(0)
            project(1, range(SPLIT))
            pe.wait_ge(consts_made, 2)
            pe.wait_ge(ffn_in, 48)
            dst = fill("wgm")
            for k in range(CC):
                last = PE.matmul(dst[:, 0:E], mean_of_all[:, :], wg_sb[:, k, :], start=(k == 0), stop=(k == CC - 1))
            last.then_inc(filled, 1)
            weight_spectrum(0)
            project(1, range(SPLIT, NT))
            inverse(0)
            correlate(1)
            out_project(0)
            weight_spectrum(1)
            for k in range(4):
                turn_tokens(0, k)
            gate(0, 0)
            gate(0, 1)
            inverse(1)
            out_project(1, range(4))
            turn_tokens(1, 0)
            out_project(1, range(4, NT))
            for k in range(1, 4):
                turn_tokens(1, k)
            gate(1, 0)
            gate(1, 1)
            pe.wait_ge(choice_ready, 1)
            dst = fill("rank")
            PE.matmul(dst[:, 0:TT * E], before, oh[:, 2, :], start=True, stop=True)
            PE.matmul(dst[:, TT * E:2 * TT * E], all_ones, oh[:, 2, :], start=True, stop=True).then_inc(filled, 1)
            dst = fill("perm")
            for q in range(2 * TT):
                if q == 0:
                    pe.wait_ge(hot_weighed, 1)
                    pe.wait_ge(hot_chosen, 1)
                if q % 8 == 0:
                    pe.wait_ge(perm_part, q // 8 + 1)
                last = PE.matmul(dst[:, 0:2 * TILES], onehot_p[:, q, :], onehot_t[:, q, :], start=(q == 0), stop=(q == 2 * TT - 1))
            last.then_inc(filled, 1)
            pe.wait_ge(idx_ready, 1)
            pe.wait_ge(where_ready, 1)
            pe.wait_ge(we_low, 2 * E)
            read_where(0)
            for i in range(TILES + 3):
                if i < TILES:
                    turn_gathered(i)
                first = hidden(i - 1) if 0 <= i - 1 < TILES else iter(())
                second = results(i - 3) if 0 <= i - 3 < TILES else iter(())
                for n in range(3 * HC):
                    next(first, None)
                    next(second, None)
                    next(first, None)
                    if n == 4 and 0 < i < TILES and i % 8 == 0:
                        read_where(i)
                for _ in first:
                    pass
                for _ in second:
                    pass
            for n, q in enumerate(TURN_ORDER):
                if q in POOL_PAIRS:
                    pe.wait_ge(pool_combined, POOL_PAIRS.index(q) + 1)
                else:
                    pe.wait_ge(combined, q + 1 - sum(p < q for p in POOL_PAIRS))
                for m in range(CC):
                    apart = m == 1 and n == 7
                    if apart:
                        last.then_inc(out_turned, 1)
                        pe.wait_ge(out_taken, 1)
                    for a in range(2):
                        last = PE.transpose(ps[:, 0 if apart else n, m * 2 * P + a * P:m * 2 * P + (a + 1) * P], tt[:, 2 * q + a, m * P:(m + 1) * P], ident)
                last.then_inc(out_turned, 1)


_INS = ['x', 'L0_conv_norm_w', 'L0_conv_norm_b', 'L0_conv_wq', 'L0_conv_bq', 'L0_conv_wk', 'L0_conv_bk',
        'L0_conv_wv', 'L0_conv_bv', 'L0_conv_wp', 'L0_conv_bp', 'L1_attn_Wq', 'L1_attn_bq', 'L1_attn_Wk',
        'L1_attn_bk', 'L1_attn_Wv', 'L1_attn_bv', 'L1_attn_Wo', 'L1_attn_bo', 'L1_ffn_Wg', 'L1_ffn_bg',
        'L1_ffn_W1', 'L1_ffn_b1', 'L1_ffn_W2', 'L1_ffn_b2']


def kernel(**inputs):
    import numpy as _np
    import concourse.bacc as _bacc
    from concourse import mybir as _mybir
    from concourse.bass_utils import run_bass_kernel_spmd as _run

    nc = _bacc.Bacc("TRN2", target_bir_lowering=False, num_devices=1)
    arrays, tensors = {}, {}
    given = {name: _np.ascontiguousarray(inputs[name]) for name in _INS}
    for name, a in {**given, **dft_constants()}.items():
        arrays[f"in_{name}_dram"] = a
        tensors[name] = nc.dram_tensor(f"in_{name}_dram", a.shape, _mybir.dt.from_np(a.dtype), kind="ExternalInput").ap()
    out = nc.dram_tensor("out_0_dram", (B, C, 32, 32), _mybir.dt.float32, kind="ExternalOutput").ap()
    conv_attn_moe_kernel(nc, tensors, out)
    r = _run(nc, [arrays], core_ids=[0])
    return r.results[0]["out_0_dram"]
```
